# Optimizing a Trainium2 kernel written in Bass

```python
import numpy as np
import jax
import jax.numpy as jnp

def _softmax(x, axis=-1):
    return jax.nn.softmax(x, axis=axis)

def _gelu(x):
    return jax.nn.gelu(x, approximate=True)

def _silu(x):
    return jax.nn.silu(x)

def _sigmoid(x):
    return jax.nn.sigmoid(x)

def _layernorm(x, axis=-1, eps=1e-05):
    m = jnp.mean(x, axis=axis, keepdims=True)
    v = jnp.var(x, axis=axis, keepdims=True)
    return (x - m) / jnp.sqrt(v + eps)

def _scatter_add(tgt, idx, src, axis=0):
    return tgt.at[idx].add(src)

def _segment_sum(src, seg, n):
    return jax.ops.segment_sum(src, seg, n)
kernel_name = 'mk_conv_preact_d4_conv_nhwc128_r2_569a6b'

def setup_inputs(seed: int=0):
    np.random.seed(seed)
    _w = jnp.asarray

    def _rec_inputs():
        import jax
        import jax.numpy as jnp
        _gk = jax.random.key(seed)
        x = -0.000125 + 0.9999 * jax.random.normal(jax.random.fold_in(_gk, 1), (1, 256, 256, 64), jnp.float32)
        return x
    x = _rec_inputs()

    def _L0_conv_setup():
        import jax, jax.numpy as jnp
        import numpy as np
        B, S, D, H = (1, 256, 64, 64)
        EPS = 1e-05

        def layernorm(x, g, b):
            mu = jnp.mean(x, axis=-1, keepdims=True)
            var = jnp.mean(jnp.square(x - mu), axis=-1, keepdims=True)
            return (x - mu) * jax.lax.rsqrt(var + EPS) * g + b
        key = jax.random.key(seed)
        ks = jax.random.split(key, 10)
        scale_d = 1.0 / np.sqrt(D)
        scale_h = 1.0 / np.sqrt(H)
        return {'x': jax.random.normal(ks[0], (B, S, S, D), dtype=jnp.float32), 'mask': jax.random.uniform(ks[1], (B, S, S), dtype=jnp.float32), 'norm_g': jnp.ones((D,), jnp.float32), 'norm_b': jnp.zeros((D,), jnp.float32), 'Wl': jax.random.normal(ks[2], (H, D), jnp.float32) * scale_d, 'Wr': jax.random.normal(ks[3], (H, D), jnp.float32) * scale_d, 'Wlg': jax.random.normal(ks[4], (H, D), jnp.float32) * scale_d, 'Wrg': jax.random.normal(ks[5], (H, D), jnp.float32) * scale_d, 'Wog': jax.random.normal(ks[6], (H, D), jnp.float32) * scale_d, 'out_norm_g': jnp.ones((H,), jnp.float32), 'out_norm_b': jnp.zeros((H,), jnp.float32), 'Wout': jax.random.normal(ks[7], (D, H), jnp.float32) * scale_h}
    _L0_conv_all = _L0_conv_setup()
    _L0_conv_in = {k: v for k, v in _L0_conv_all.items() if k in ('mask', 'norm_g', 'norm_b', 'Wl', 'Wr', 'Wlg', 'Wrg', 'Wog', 'out_norm_g', 'out_norm_b', 'Wout')}
    del _L0_conv_all

    def _L1_conv_setup():
        import jax, jax.numpy as jnp
        import numpy as np
        B, L, DIM, HID = (1, 256, 64, 64)
        EPS = 1e-05

        def layernorm(x, w, b):
            mu = jnp.mean(x, axis=-1, keepdims=True)
            var = jnp.var(x, axis=-1, keepdims=True)
            return (x - mu) * jax.lax.rsqrt(var + EPS) * w + b
        key = jax.random.key(seed)
        ks = jax.random.split(key, 12)
        s = 1.0 / np.sqrt(DIM)
        sh = 1.0 / np.sqrt(HID)
        x = jax.random.normal(ks[0], (B, L, L, DIM), dtype=jnp.float32)
        mask = (jax.random.uniform(ks[1], (B, L, L)) > 0.1).astype(jnp.float32)
        return {'x': x, 'mask': mask, 'norm_w': jnp.ones((DIM,), jnp.float32), 'norm_b': jnp.zeros((DIM,), jnp.float32), 'w_left': jax.random.uniform(ks[2], (HID, DIM), jnp.float32, -s, s), 'w_right': jax.random.uniform(ks[3], (HID, DIM), jnp.float32, -s, s), 'w_lgate': jax.random.uniform(ks[4], (HID, DIM), jnp.float32, -s, s), 'w_rgate': jax.random.uniform(ks[5], (HID, DIM), jnp.float32, -s, s), 'w_ogate': jax.random.uniform(ks[6], (HID, DIM), jnp.float32, -s, s), 'onorm_w': jnp.ones((HID,), jnp.float32), 'onorm_b': jnp.zeros((HID,), jnp.float32), 'w_out': jax.random.uniform(ks[7], (DIM, HID), jnp.float32, -sh, sh)}
    _L1_conv_all = _L1_conv_setup()
    _L1_conv_in = {k: v for k, v in _L1_conv_all.items() if k in ('mask', 'norm_w', 'norm_b', 'w_left', 'w_right', 'w_lgate', 'w_rgate', 'w_ogate', 'onorm_w', 'onorm_b', 'w_out')}
    del _L1_conv_all

    def _L2_conv_setup():
        import jax, jax.numpy as jnp
        import numpy as np
        EPS = 1e-05

        def _ln(x, g, b):
            m = jnp.mean(x, axis=-1, keepdims=True)
            v = jnp.var(x, axis=-1, keepdims=True)
            return (x - m) / jnp.sqrt(v + EPS) * g + b
        key = jax.random.key(seed)
        ks = jax.random.split(key, 16)
        B, N, CZ, C = (1, 256, 64, 16)
        s_cz = 1.0 / np.sqrt(CZ)
        s_c = 1.0 / np.sqrt(C)

        def lin(k, fan_in, shape):
            return jax.random.uniform(k, shape, jnp.float32, -1.0, 1.0) / np.sqrt(fan_in)
        return {'x': jax.random.normal(ks[0], (B, N, N, CZ), jnp.float32), 'Wa1': lin(ks[1], CZ, (CZ, C)), 'ba1': lin(ks[2], CZ, (C,)), 'Wa2': lin(ks[3], CZ, (CZ, C)), 'ba2': lin(ks[4], CZ, (C,)), 'Wb1': lin(ks[5], CZ, (CZ, C)), 'bb1': lin(ks[6], CZ, (C,)), 'Wb2': lin(ks[7], CZ, (CZ, C)), 'bb2': lin(ks[8], CZ, (C,)), 'ln2_g': jnp.ones((C,), jnp.float32), 'ln2_b': jnp.zeros((C,), jnp.float32), 'Wg': lin(ks[9], CZ, (CZ, CZ)), 'bg': lin(ks[10], CZ, (CZ,)), 'Wz': lin(ks[11], C, (C, CZ)), 'bz': lin(ks[12], C, (CZ,))}
    _L2_conv_all = _L2_conv_setup()
    _L2_conv_in = {k: v for k, v in _L2_conv_all.items() if k in ('Wa1', 'ba1', 'Wa2', 'ba2', 'Wb1', 'bb1', 'Wb2', 'bb2', 'ln2_g', 'ln2_b', 'Wg', 'bg', 'Wz', 'bz')}
    del _L2_conv_all

    def _L3_conv_setup():
        import jax, jax.numpy as jnp
        import numpy as np
        B, L, D, C = (1, 256, 64, 64)

        def _layernorm(x, w, b, eps=1e-05):
            mu = jnp.mean(x, axis=-1, keepdims=True)
            var = jnp.var(x, axis=-1, keepdims=True)
            return (x - mu) * jax.lax.rsqrt(var + eps) * w + b
        key = jax.random.key(seed)
        ks = jax.random.split(key, 12)
        s = 0.05
        f32 = jnp.float32
        return {'z': jax.random.normal(ks[0], (B, L, L, D), f32), 'ln_in_w': jnp.ones((D,), f32), 'ln_in_b': jnp.zeros((D,), f32), 'Wga': jax.random.normal(ks[1], (D, C), f32) * s, 'bga': jnp.zeros((C,), f32), 'Wla': jax.random.normal(ks[2], (D, C), f32) * s, 'bla': jnp.zeros((C,), f32), 'Wgb': jax.random.normal(ks[3], (D, C), f32) * s, 'bgb': jnp.zeros((C,), f32), 'Wlb': jax.random.normal(ks[4], (D, C), f32) * s, 'blb': jnp.zeros((C,), f32), 'ln_o_w': jnp.ones((C,), f32), 'ln_o_b': jnp.zeros((C,), f32), 'Wgo': jax.random.normal(ks[5], (D, D), f32) * s, 'bgo': jnp.zeros((D,), f32), 'Wlo': jax.random.normal(ks[6], (C, D), f32) * s, 'blo': jnp.zeros((D,), f32)}
    _L3_conv_all = _L3_conv_setup()
    _L3_conv_in = {k: v for k, v in _L3_conv_all.items() if k in ('ln_in_w', 'ln_in_b', 'Wga', 'bga', 'Wla', 'bla', 'Wgb', 'bgb', 'Wlb', 'blb', 'ln_o_w', 'ln_o_b', 'Wgo', 'bgo', 'Wlo', 'blo')}
    del _L3_conv_all
    return {'x': x, 'L0_conv_mask': _L0_conv_in['mask'], 'L0_conv_norm_g': _L0_conv_in['norm_g'], 'L0_conv_norm_b': _L0_conv_in['norm_b'], 'L0_conv_Wl': _L0_conv_in['Wl'], 'L0_conv_Wr': _L0_conv_in['Wr'], 'L0_conv_Wlg': _L0_conv_in['Wlg'], 'L0_conv_Wrg': _L0_conv_in['Wrg'], 'L0_conv_Wog': _L0_conv_in['Wog'], 'L0_conv_out_norm_g': _L0_conv_in['out_norm_g'], 'L0_conv_out_norm_b': _L0_conv_in['out_norm_b'], 'L0_conv_Wout': _L0_conv_in['Wout'], 'L1_conv_mask': _L1_conv_in['mask'], 'L1_conv_norm_w': _L1_conv_in['norm_w'], 'L1_conv_norm_b': _L1_conv_in['norm_b'], 'L1_conv_w_left': _L1_conv_in['w_left'], 'L1_conv_w_right': _L1_conv_in['w_right'], 'L1_conv_w_lgate': _L1_conv_in['w_lgate'], 'L1_conv_w_rgate': _L1_conv_in['w_rgate'], 'L1_conv_w_ogate': _L1_conv_in['w_ogate'], 'L1_conv_onorm_w': _L1_conv_in['onorm_w'], 'L1_conv_onorm_b': _L1_conv_in['onorm_b'], 'L1_conv_w_out': _L1_conv_in['w_out'], 'L2_conv_Wa1': _L2_conv_in['Wa1'], 'L2_conv_ba1': _L2_conv_in['ba1'], 'L2_conv_Wa2': _L2_conv_in['Wa2'], 'L2_conv_ba2': _L2_conv_in['ba2'], 'L2_conv_Wb1': _L2_conv_in['Wb1'], 'L2_conv_bb1': _L2_conv_in['bb1'], 'L2_conv_Wb2': _L2_conv_in['Wb2'], 'L2_conv_bb2': _L2_conv_in['bb2'], 'L2_conv_ln2_g': _L2_conv_in['ln2_g'], 'L2_conv_ln2_b': _L2_conv_in['ln2_b'], 'L2_conv_Wg': _L2_conv_in['Wg'], 'L2_conv_bg': _L2_conv_in['bg'], 'L2_conv_Wz': _L2_conv_in['Wz'], 'L2_conv_bz': _L2_conv_in['bz'], 'L3_conv_ln_in_w': _L3_conv_in['ln_in_w'], 'L3_conv_ln_in_b': _L3_conv_in['ln_in_b'], 'L3_conv_Wga': _L3_conv_in['Wga'], 'L3_conv_bga': _L3_conv_in['bga'], 'L3_conv_Wla': _L3_conv_in['Wla'], 'L3_conv_bla': _L3_conv_in['bla'], 'L3_conv_Wgb': _L3_conv_in['Wgb'], 'L3_conv_bgb': _L3_conv_in['bgb'], 'L3_conv_Wlb': _L3_conv_in['Wlb'], 'L3_conv_blb': _L3_conv_in['blb'], 'L3_conv_ln_o_w': _L3_conv_in['ln_o_w'], 'L3_conv_ln_o_b': _L3_conv_in['ln_o_b'], 'L3_conv_Wgo': _L3_conv_in['Wgo'], 'L3_conv_bgo': _L3_conv_in['bgo'], 'L3_conv_Wlo': _L3_conv_in['Wlo'], 'L3_conv_blo': _L3_conv_in['blo']}

def reference(x, L0_conv_mask, L0_conv_norm_g, L0_conv_norm_b, L0_conv_Wl, L0_conv_Wr, L0_conv_Wlg, L0_conv_Wrg, L0_conv_Wog, L0_conv_out_norm_g, L0_conv_out_norm_b, L0_conv_Wout, L1_conv_mask, L1_conv_norm_w, L1_conv_norm_b, L1_conv_w_left, L1_conv_w_right, L1_conv_w_lgate, L1_conv_w_rgate, L1_conv_w_ogate, L1_conv_onorm_w, L1_conv_onorm_b, L1_conv_w_out, L2_conv_Wa1, L2_conv_ba1, L2_conv_Wa2, L2_conv_ba2, L2_conv_Wb1, L2_conv_bb1, L2_conv_Wb2, L2_conv_bb2, L2_conv_ln2_g, L2_conv_ln2_b, L2_conv_Wg, L2_conv_bg, L2_conv_Wz, L2_conv_bz, L3_conv_ln_in_w, L3_conv_ln_in_b, L3_conv_Wga, L3_conv_bga, L3_conv_Wla, L3_conv_bla, L3_conv_Wgb, L3_conv_bgb, L3_conv_Wlb, L3_conv_blb, L3_conv_ln_o_w, L3_conv_ln_o_b, L3_conv_Wgo, L3_conv_bgo, L3_conv_Wlo, L3_conv_blo):
    import jax
    import jax.numpy as jnp

    def _L0_conv_ref(x, mask, norm_g, norm_b, Wl, Wr, Wlg, Wrg, Wog, out_norm_g, out_norm_b, Wout):
        import jax, jax.numpy as jnp
        import numpy as np
        B, S, D, H = (1, 256, 64, 64)
        EPS = 1e-05

        def layernorm(x, g, b):
            mu = jnp.mean(x, axis=-1, keepdims=True)
            var = jnp.mean(jnp.square(x - mu), axis=-1, keepdims=True)
            return (x - mu) * jax.lax.rsqrt(var + EPS) * g + b
        xn = layernorm(x, norm_g, norm_b)
        m = mask[..., None]
        left = xn @ Wl.T * m * jax.nn.sigmoid(xn @ Wlg.T)
        right = xn @ Wr.T * m * jax.nn.sigmoid(xn @ Wrg.T)
        out_gate = jax.nn.sigmoid(xn @ Wog.T)
        out = jnp.einsum('bikd,bjkd->bijd', left, right)
        out = layernorm(out, out_norm_g, out_norm_b) * out_gate
        return out @ Wout.T

    def _L1_conv_ref(x, mask, norm_w, norm_b, w_left, w_right, w_lgate, w_rgate, w_ogate, onorm_w, onorm_b, w_out):
        import jax, jax.numpy as jnp
        import numpy as np
        B, L, DIM, HID = (1, 256, 64, 64)
        EPS = 1e-05

        def layernorm(x, w, b):
            mu = jnp.mean(x, axis=-1, keepdims=True)
            var = jnp.var(x, axis=-1, keepdims=True)
            return (x - mu) * jax.lax.rsqrt(var + EPS) * w + b
        xn = layernorm(x, norm_w, norm_b)
        m = mask[..., None]
        left = jnp.einsum('bijd,hd->bijh', xn, w_left) * m
        right = jnp.einsum('bijd,hd->bijh', xn, w_right) * m
        lg = jax.nn.sigmoid(jnp.einsum('bijd,hd->bijh', xn, w_lgate))
        rg = jax.nn.sigmoid(jnp.einsum('bijd,hd->bijh', xn, w_rgate))
        og = jax.nn.sigmoid(jnp.einsum('bijd,hd->bijh', xn, w_ogate))
        left = (left * lg).astype(jnp.bfloat16)
        right = (right * rg).astype(jnp.bfloat16)
        out = jnp.einsum('bikh,bjkh->bijh', left, right).astype(jnp.float32)
        out = layernorm(out, onorm_w, onorm_b) * og
        return jnp.einsum('bijh,dh->bijd', out, w_out)

    def _L2_conv_ref(x, Wa1, ba1, Wa2, ba2, Wb1, bb1, Wb2, bb2, ln2_g, ln2_b, Wg, bg, Wz, bz):
        import jax, jax.numpy as jnp
        import numpy as np
        EPS = 1e-05

        def _ln(x, g, b):
            m = jnp.mean(x, axis=-1, keepdims=True)
            v = jnp.var(x, axis=-1, keepdims=True)
            return (x - m) / jnp.sqrt(v + EPS) * g + b
        direction = 'outgoing'
        a = jax.nn.sigmoid((x @ Wa1 + ba1) * (x @ Wa2 + ba2))
        b = jax.nn.sigmoid((x @ Wb1 + bb1) * (x @ Wb2 + bb2))
        if direction == 'incoming':
            a = jnp.swapaxes(a, 1, 2)
            b = jnp.swapaxes(b, 1, 2)
        g = jax.nn.sigmoid(x @ Wg + bg)
        z = jnp.einsum('bikc,bkjc->bijc', a, b)
        return g * (_ln(z, ln2_g, ln2_b) @ Wz + bz)

    def _L3_conv_ref(z, ln_in_w, ln_in_b, Wga, bga, Wla, bla, Wgb, bgb, Wlb, blb, ln_o_w, ln_o_b, Wgo, bgo, Wlo, blo):
        import jax, jax.numpy as jnp
        import numpy as np
        B, L, D, C = (1, 256, 64, 64)

        def _layernorm(x, w, b, eps=1e-05):
            mu = jnp.mean(x, axis=-1, keepdims=True)
            var = jnp.var(x, axis=-1, keepdims=True)
            return (x - mu) * jax.lax.rsqrt(var + eps) * w + b
        zn = _layernorm(z, ln_in_w, ln_in_b)
        a = jax.nn.sigmoid(zn @ Wga + bga) * (zn @ Wla + bla)
        b = jax.nn.sigmoid(zn @ Wgb + bgb) * (zn @ Wlb + blb)
        k = jnp.einsum('bimc,bmjc->bijc', a, b)
        out = jax.nn.sigmoid(zn @ Wgo + bgo) * (_layernorm(k, ln_o_w, ln_o_b) @ Wlo + blo)
        return out

    def _gn(v, G=32, eps=1e-05):
        B_, H_, W_, C_ = v.shape
        g = v.reshape(B_, H_, W_, G, C_ // G)
        m = jnp.mean(g, axis=(1, 2, 4), keepdims=True)
        s = jnp.var(g, axis=(1, 2, 4), keepdims=True)
        return ((g - m) / jnp.sqrt(s + eps)).reshape(v.shape)

    def _ln_c(v, eps=1e-06):
        m = jnp.mean(v, axis=-1, keepdims=True)
        s = jnp.var(v, axis=-1, keepdims=True)
        return (v - m) / jnp.sqrt(s + eps)

    def _ln_t(v, eps=1e-05):
        m = jnp.mean(v, axis=-1, keepdims=True)
        s = jnp.var(v, axis=-1, keepdims=True)
        return (v - m) / jnp.sqrt(s + eps)

    def _to_tokens(v):
        B_, H_, W_, C_ = v.shape
        return v.reshape(B_, H_ * W_, C_)

    def _from_tokens(t, like):
        return t.reshape(like.shape)
    x = x + _L0_conv_ref(_gn(x), L0_conv_mask, L0_conv_norm_g, L0_conv_norm_b, L0_conv_Wl, L0_conv_Wr, L0_conv_Wlg, L0_conv_Wrg, L0_conv_Wog, L0_conv_out_norm_g, L0_conv_out_norm_b, L0_conv_Wout)
    x = x + _L1_conv_ref(_gn(x), L1_conv_mask, L1_conv_norm_w, L1_conv_norm_b, L1_conv_w_left, L1_conv_w_right, L1_conv_w_lgate, L1_conv_w_rgate, L1_conv_w_ogate, L1_conv_onorm_w, L1_conv_onorm_b, L1_conv_w_out)
    x = x + _L2_conv_ref(_gn(x), L2_conv_Wa1, L2_conv_ba1, L2_conv_Wa2, L2_conv_ba2, L2_conv_Wb1, L2_conv_bb1, L2_conv_Wb2, L2_conv_bb2, L2_conv_ln2_g, L2_conv_ln2_b, L2_conv_Wg, L2_conv_bg, L2_conv_Wz, L2_conv_bz)
    x = x + _L3_conv_ref(_gn(x), L3_conv_ln_in_w, L3_conv_ln_in_b, L3_conv_Wga, L3_conv_bga, L3_conv_Wla, L3_conv_bla, L3_conv_Wgb, L3_conv_bgb, L3_conv_Wlb, L3_conv_blb, L3_conv_ln_o_w, L3_conv_ln_o_b, L3_conv_Wgo, L3_conv_bgo, L3_conv_Wlo, L3_conv_blo)
    return x

_drawn_inputs = setup_inputs


def setup_inputs(seed=0):
    import zlib

    import numpy as np

    out = dict(_drawn_inputs(seed))
    spreads = {'L0_conv_norm_g': (1.0, 0.2),
     'L0_conv_norm_b': (0.0, 0.1),
     'L0_conv_out_norm_g': (1.0, 0.2),
     'L0_conv_out_norm_b': (0.0, 0.1),
     'L1_conv_norm_w': (1.0, 0.2),
     'L1_conv_norm_b': (0.0, 0.1),
     'L1_conv_onorm_w': (1.0, 0.2),
     'L1_conv_onorm_b': (0.0, 0.38),
     'L2_conv_ln2_g': (1.0, 0.2),
     'L2_conv_ln2_b': (0.0, 0.366),
     'L3_conv_ln_in_w': (1.0, 0.2),
     'L3_conv_ln_in_b': (0.0, 0.1),
     'L3_conv_bga': (0.0, 0.8),
     'L3_conv_bla': (0.0, 0.1),
     'L3_conv_bgb': (0.0, 0.8),
     'L3_conv_blb': (0.0, 0.1),
     'L3_conv_ln_o_w': (1.0, 0.6),
     'L3_conv_ln_o_b': (0.0, 0.573),
     'L3_conv_bgo': (0.0, 0.8),
     'L3_conv_blo': (0.0, 0.1)}
    factors = {'L2_conv_bg': 6.103, 'L3_conv_Wga': 3.004, 'L3_conv_Wgb': 2.874}
    for name, (base, spread) in spreads.items():
        noise = np.random.default_rng([zlib.crc32(name.encode()), seed]).standard_normal(out[name].shape)
        drawn = base * np.exp(spread * noise) if base else spread * noise
        out[name] = jnp.asarray(drawn.astype(out[name].dtype))
    for name, factor in factors.items():
        out[name] = (out[name] * factor).astype(out[name].dtype)
    return out
```

```python
from contextlib import ExitStack

import numpy as np

import concourse.bass as bass
from concourse import mybir

F32 = mybir.dt.float32
BF16 = mybir.dt.bfloat16
ALU = mybir.AluOpType
ACT = mybir.ActivationFunctionType

P = 128
S = 256
C = 64
HALF = S // 2
CH = 512
NCH = HALF * S // CH
ROWS = CH // S
SEG = 16
SCH = SEG // ROWS
MINI = 4
BODY = 2 * SCH
EPS = 1e-5
FIRST = 16
LN_SET = "natural_log_exp_and_others"

V_LN_G, V_LN_B, V_ON_G, V_ON_B, V_GATE_B, V_OUT_B, NVEC = range(7)


class Counter:

    def __init__(self, handle, base):
        self.sem, self.base = handle, base

    def __call__(self, n):
        return n + self.base

    def advance(self, n):
        self.base += n


def build(nc, a, out):
    with ExitStack() as ctx:
        def sb(name, shape, dt=F32):
            return ctx.enter_context(nc.sbuf_tensor(name, shape, dt))

        def counter(name, base=FIRST):
            return Counter(ctx.enter_context(nc.semaphore(name)), base)

        k = {
            "basis": sb("basis", [P, P]), "var_w": sb("var_w", [P, P]), "ident": sb("ident", [P, P]),
            "pool_w": sb("pool_w", [P, P]), "last_row": sb("last_row", [2, P]), "unit": sb("unit", [P, 3]),
            "gn": sb("gn", [P, 12]), "gn_stats": sb("gn_stats", [P, NCH, 6]),
            "vec": sb("vec", [P, NVEC]), "center": sb("center", [P, P]), "shift": sb("shift", [P, 1]),
            "w_proj": sb("w_proj", [P, 640]), "w_out": sb("w_out", [P, P]),
            "out_bias": sb("out_bias", [P, 1]), "one": sb("one", [1, P]),
            "mask": sb("mask", [P, 2, S]),
        }
        ps = [ctx.enter_context(nc.psum_tensor(f"ps{n}", [P, 2, 512], F32)) for n in range(4)]
        c = {n: counter(n) for n in (
            "fold_vec", "fold_mm", "fold_act", "stat_done", "z_done", "sq_done", "var_done", "log_done", "r_done", "xn_done",
            "proj_done", "gate_mm_done", "sig_done", "gate_done", "masked", "lr_done",
            "tr_done", "tr_copied", "tri_done", "o_copied",
            "ln_stat", "ln_small", "ln_var", "ln_root", "ln_scale", "centered", "scaled", "wt_done", "wt_copied", "gated",
            "out_mm_done", "out_gated", "x_new", "counted")}
        for n, ring in (("const_in", 1), ("x_in", 8), ("lr_out", 2), ("gate_out", 4), ("lr_in", 2),
                        ("xc_in", 4), ("gc_in", 4), ("x_out", 4)):
            for i in range(ring):
                c[f"{n}{i}"] = counter(f"{n}{i}", 16)
        start_counters(nc, c, k, a)
        first_statistics(nc, a["x"], c, k)
        x = a["x"]
        for n, kind in enumerate(("masked", "masked_bf16", "plain", "normed")):
            x_new = out if n == 3 else a[f"x_dram{n % 2}"]
            layer(nc, n, kind, a, x, x_new, c, k, ps)
            x = x_new


def start_counters(nc, c, k, a):
    with nc.Block() as block:
        @block.sync
        def _(sp):
            for name, counter in c.items():
                sp.sem_inc(counter.sem, counter.base)


def first_statistics(nc, x, c, k):
    wide = 4 * CH
    turns = HALF * S // wide
    with ExitStack() as ctx:
        xin = ctx.enter_context(nc.sbuf_tensor("xin", [P, 4, wide], F32))
        block = ctx.enter_context(nc.Block())

        @block.sync
        def _(sp):
            with sp.Fori(0, turns // 4) as t:
                for s in range(4):
                    sp.wait_ge(c["stat_done"].sem, c["stat_done"](t * 4 + s - 3))
                    sp.dma_start(xin[:, s, :], x[:, bass.ds((t * 4 + s) * wide, wide)]).then_inc(c[f"xc_in{s}"].sem, 16)

        @block.vector
        def _(dve):
            with dve.Fori(0, turns // 4) as t:
                for s in range(4):
                    load = c[f"xc_in{s}"]
                    dve.wait_ge(load.sem, load(t * 16 + 16))
                    for q in range(4):
                        last = dve.bn_stats(k["gn_stats"][:, bass.ds(t * 16 + s * 4 + q, 1), :].rearrange("p a b -> p (a b)"),
                                            xin[:, s, q * CH:(q + 1) * CH])
                    last.then_inc(c["stat_done"].sem, 1)
    for s in range(4):
        c[f"xc_in{s}"].advance(16 * turns // 4)
    c["stat_done"].advance(turns)


def layer(nc, n, kind, a, x, x_new, c, k, ps):
    normed_in = kind != "plain"
    masked = kind in ("masked", "masked_bf16")
    low = BF16 if kind == "masked_bf16" else F32
    H = 16 if kind == "plain" else C
    HG = 16 if low == BF16 else 8
    left_right = a[f"left_right{n}"]
    fold(nc, n, kind, a, c, k, ps)
    if normed_in:
        project(nc, n, masked, low, HG, x, a["gate"], left_right, c, k, ps)
    else:
        project_plain(nc, n, HG, x, a["gate"], left_right, c, k, ps)
    with ExitStack() as ctx:
        O = ctx.enter_context(nc.sbuf_tensor(f"O{n}", [P, 2, HALF, 2, H], low))
        triangle(nc, n, not masked, low, H, HG, left_right, O, c, k, ps)
        output(nc, n, masked, H, O, x, a["gate"], x_new, c, k, ps)


def fold(nc, n, kind, a, c, k, ps):
    normed_in = kind != "plain"
    masked = kind in ("masked", "masked_bf16")
    fold_ctx = ExitStack()
    local = {name: fold_ctx.enter_context(nc.sbuf_tensor(f"{name}_{n}", shape, F32)) for name, shape in (
        ("w_raw", [P, 640]), ("w_scaled", [P, 640]), ("b_rows", [2, 640]), ("ln_sel", [P, P]), ("mask_in", [P, 2, S]))}
    k = {**k, **local}
    loads = [(k["vec"][:], a[f"vec{n}"]), (k["w_raw"][:], a[f"w_proj{n}"]), (k["w_out"][:], a[f"w_out{n}"]),
             (k["b_rows"][:], a[f"b_rows{n}"])]
    if n == 0:
        loads += [(k[x][:], a[x]) for x in ("basis", "var_w", "ident", "pool_w", "last_row", "unit", "one")]
    if masked:
        loads += [(k["mask_in"][:], a[f"mask{n}"].rearrange("(b p) k -> p b k", p=P))]
    gn, vec, unit = k["gn"], k["vec"], k["unit"]
    mean, var, group_mean, off, power, std, scale, shift = (gn[:, q:q + 1] for q in range(8))
    mm, done, act_done, loaded = c["fold_mm"], c["fold_vec"], c["fold_act"], c["const_in0"]
    out_rows = P if normed_in else 32
    P_MEAN, P_VAR, P_SHIFT, P_PROJ, P_GATE, P_TURN, P_BIAS = (ps[q // 2][:, q % 2, :] for q in range(7))

    with fold_ctx, nc.Block() as block:
        @block.sync
        def _(sp):
            for dst, src in loads:
                sp.dma_start(dst, src).then_inc(loaded.sem, 16)

        @block.tensor
        def _(pe):
            pe.wait_ge(loaded.sem, loaded(16 * len(loads)))
            if masked:
                for kb in range(2):
                    for ib in range(2):
                        at = kb * S + ib * P
                        last = pe.transpose(P_TURN[:, at:at + P], k["mask_in"][:, ib, kb * P:kb * P + P], k["ident"][:])
            else:
                last = pe.matmul(P_BIAS[:, 0:1], k["w_out"][0:out_rows, :], vec[0:out_rows, V_ON_B:V_ON_B + 1],
                                 start=True, stop=True)
            last.then_inc(mm.sem, 1)
            pe.wait_ge(done.sem, done(1))
            pe.matmul(P_MEAN[:, 0:1], k["pool_w"][:], mean, start=True, stop=True).then_inc(mm.sem, 1)
            pe.wait_ge(done.sem, done(4))
            pe.matmul(P_VAR[:, 0:1], k["pool_w"][:], power, start=True, stop=True).then_inc(mm.sem, 1)
            if normed_in:
                pe.wait_ge(done.sem, done(6))
                pe.matmul(P_SHIFT[:, 0:1], k["basis"][:], shift, start=True, stop=True).then_inc(mm.sem, 1)
                pe.wait_ge(done.sem, done(12))
                for lo, hi, bank in ((0, 512, P_PROJ), (512, 640, P_GATE)):
                    w = hi - lo
                    pe.matmul(bank[:, 0:w], k["basis"][:], k["w_scaled"][:, lo:hi], start=True, stop=False)
                    pe.matmul(bank[:, 0:w], k["ln_sel"][:], k["w_raw"][:, lo:hi], start=False, stop=False)
                    last = pe.matmul(bank[:, 0:w], k["last_row"][:], k["b_rows"][:, lo:hi], start=False, stop=True)
                last.then_inc(mm.sem, 1)
            else:
                pe.matmul(P_PROJ, k["one"][:], k["b_rows"][0:1, 0:CH], start=True, stop=True).then_inc(mm.sem, 1)

        @block.scalar
        def _(act):
            act.wait_ge(mm.sem, mm(3))
            act.activation(std, P_VAR[:, 0:1], ACT.Sqrt, bias=unit[:, 2:3]).then_inc(act_done.sem, 1)

        @block.vector
        def _(dve):
            steps = [0]

            def step(ins):
                steps[0] += 1
                ins.then_inc(done.sem, 1)
                dve.wait_ge(done.sem, done(steps[0]))

            dve.wait_ge(loaded.sem, loaded(16 * len(loads)))
            step(dve.bn_aggr(gn[:, 0:2], k["gn_stats"][:].rearrange("p a b -> p (a b)")))
            dve.wait_ge(mm.sem, mm(2))
            step(dve.tensor_copy(group_mean, P_MEAN[:, 0:1]))
            step(dve.tensor_tensor(off, mean, group_mean, ALU.subtract))
            step(dve.scalar_tensor_tensor(power, off, off, var, ALU.mult, ALU.add))
            dve.wait_ge(act_done.sem, act_done(1))
            step(dve.reciprocal(scale, std))
            step(dve.scalar_tensor_tensor(shift, group_mean, -1.0, scale, ALU.mult, ALU.mult))
            if normed_in:
                step(dve.tensor_scalar(k["center"][:], k["basis"][:], scale, None, ALU.mult))
                dve.wait_ge(mm.sem, mm(4))
                step(dve.tensor_tensor(k["shift"][:], P_SHIFT[:, 0:1], unit[:, 0:1], ALU.add))
                step(dve.memset(k["ln_sel"][:], 0.0))
                for g in range(2):
                    half, last_col = slice(g * C, g * C + C), g * C + C - 1
                    step(dve.tensor_copy(k["ln_sel"][half, last_col:last_col + 1], vec[half, V_LN_B:V_LN_B + 1]))
                step(dve.tensor_scalar(k["w_scaled"][:], k["w_raw"][:], vec[:, V_LN_G:V_LN_G + 1], None, ALU.mult))
                dve.wait_ge(mm.sem, mm(5))
                step(dve.tensor_copy(k["w_proj"][:, 0:CH], P_PROJ))
                step(dve.tensor_copy(k["w_proj"][:, CH:640], P_GATE[:, 0:P]))
            else:
                step(dve.tensor_copy(k["w_proj"][:], k["w_raw"][:]))
                dve.wait_ge(mm.sem, mm(4))
                step(dve.tensor_copy(k["mask"][:].rearrange("p a b -> p (a b)"), P_PROJ))
            if masked:
                step(dve.tensor_copy(k["mask"][:].rearrange("p a b -> p (a b)"), P_TURN))
            else:
                step(dve.tensor_tensor(k["out_bias"][:], P_BIAS[:, 0:1], vec[:, V_OUT_B:V_OUT_B + 1], ALU.add))
                step(dve.tensor_scalar(k["w_out"][:], k["w_out"][:], vec[:, V_ON_G:V_ON_G + 1], None, ALU.mult))

    loaded.advance(16 * len(loads))
    mm.advance(5 if normed_in else 4)
    act_done.advance(1)
    done.advance((14 if normed_in else 8) + (1 if masked else 2))


def store_segment(sp, left_right, stage, seg, HG, done):
    for lr in range(2):
        groups = left_right[lr].rearrange("n k b s i h -> k n b s (i h)")
        for kb in range(2):
            for g in range(2):
                src = stage[:, kb, g, lr, :, :, :].rearrange("p n i h -> p n (i h)")
                dst = groups[:, :, kb, bass.ds(seg + g * (S // SEG // 2), 1), :].rearrange("k n s e -> k n (s e)")
                sp.dma_start(dst, src).then_inc(done.sem, 16)


def project(nc, n, masked, low, HG, x, gate, left_right, c, k, ps):
    with ExitStack() as ctx:
        def sb(name, shape, dt=F32):
            return ctx.enter_context(nc.sbuf_tensor(f"{name}_{n}", shape, dt))

        xs, zs, xn = sb("xs", [P, 8, CH]), sb("zs", [P, 8, CH]), sb("xn", [P, 8, CH])
        sq, log_var, r = sb("sq", [P, 2, CH]), sb("log_var", [P, 2, CH]), sb("r", [P, 4, CH])
        sig, gates = sb("sig", [P, 4, CH]), sb("gates", [P, 4, CH])
        stage = sb("stage", [P, 2, 2, 2, 2, C // HG, SEG, HG], low)
        Z = [ps[0][:, q, :] for q in range(2)]
        VAR, GATE, PAIR = ps[1][:, 0, :], ps[1][:, 1, :], [ps[2], ps[3]]
        block = ctx.enter_context(nc.Block())
        bodies = NCH // BODY


        def bodies_of(eng, lead, follow):
            lead(0, 0)
            with eng.Fori(0, bodies - 1) as i:
                for b in range(BODY // MINI):
                    lead(i, (b + 1) * MINI)
                    follow(i, b * MINI)
            for b in range(BODY // MINI):
                if (b + 1) * MINI < BODY:
                    lead(bodies - 1, (b + 1) * MINI)
                follow(bodies - 1, b * MINI)

        @block.sync
        def _(sp):
            def load(i, q):
                m = i * BODY + q
                sp.wait_ge(c["z_done"].sem, c["z_done"](m - 7))
                sp.dma_start(xs[:, q % 8, :], x[:, bass.ds(m * CH, CH)]).then_inc(c[f"x_in{q % 8}"].sem, 16)

            def store(i, q0):
                for q in range(q0, q0 + MINI):
                    m = i * BODY + q
                    sp.wait_ge(c["gate_done"].sem, c["gate_done"](m + 1))
                    sp.dma_start(gate[:, bass.ds(m * CH, CH)], gates[:, q % 4, :]).then_inc(c[f"gate_out{q % 4}"].sem, 16)
                if (q0 + MINI) % SCH == 0:
                    sp.wait_ge(c["lr_done"].sem, c["lr_done"]((i * BODY + q0 + MINI) * 2))
                    b = q0 // SCH
                    store_segment(sp, left_right, stage[:, b], i * 2 + b, HG, c[f"lr_out{b}"])

            for q in range(2 * MINI):
                load(0, q)
            with sp.Fori(0, bodies - 1) as i:
                for b in range(BODY // MINI):
                    for q in range((b + 2) * MINI, (b + 3) * MINI):
                        load(i, q)
                    store(i, b * MINI)
            for b in range(BODY // MINI):
                for q in range((b + 2) * MINI, min((b + 3) * MINI, BODY)):
                    load(bodies - 1, q)
                store(bodies - 1, b * MINI)
            for s in range(4):
                sp.wait_ge(c[f"gate_out{s}"].sem, c[f"gate_out{s}"](16 * NCH // 4))
            for s in range(2):
                sp.wait_ge(c[f"lr_out{s}"].sem, c[f"lr_out{s}"](16 * 8 * bodies))

        @block.tensor
        def _(pe):
            def center(i, q):
                m = i * BODY + q
                load = c[f"x_in{q % 8}"]
                pe.wait_ge(load.sem, load(i * 32 + (q // 8 + 1) * 16))
                pe.wait_ge(c["sq_done"].sem, c["sq_done"](m - 1))
                pe.matmul(Z[q % 2], k["center"][:], xs[:, q % 8, :], start=True, stop=True).then_inc(c["z_done"].sem, 1)

            def variance(i, q):
                m = i * BODY + q
                pe.wait_ge(c["sq_done"].sem, c["sq_done"](m + 1))
                pe.wait_ge(c["log_done"].sem, c["log_done"](m))
                pe.matmul(VAR, k["var_w"][:], sq[:, q % 2, :], start=True, stop=True).then_inc(c["var_done"].sem, 1)

            def lead(i, q0):
                center(i, q0)
                for q in range(q0 + 1, q0 + MINI):
                    center(i, q)
                    variance(i, q - 1)
                variance(i, q0 + MINI - 1)

            def follow(i, q0):
                for q in range(q0, q0 + MINI):
                    m = i * BODY + q
                    pe.wait_ge(c["xn_done"].sem, c["xn_done"](m + 1))
                    for row in range(ROWS):
                        pe.wait_ge(c["lr_done"].sem, c["lr_done"](m * 2 + row - 1))
                        for kb in range(2):
                            at = row * S + kb * P
                            last = pe.matmul(PAIR[row][:, kb, :], xn[:, q % 8, at:at + P], k["w_proj"][:, 0:CH],
                                             start=True, stop=True)
                        last.then_inc(c["proj_done"].sem, 1)
                    pe.wait_ge(c["gate_done"].sem, c["gate_done"](m))
                    pe.matmul(GATE, k["w_proj"][:, CH:CH + P], xn[:, q % 8, :],
                              start=True, stop=True).then_inc(c["gate_mm_done"].sem, 1)

            bodies_of(pe, lead, follow)

        @block.scalar
        def _(act):
            def square(i, q):
                m = i * BODY + q
                act.wait_ge(c["z_done"].sem, c["z_done"](m + 1))
                act.wait_ge(c["xn_done"].sem, c["xn_done"](m - 7))
                act.activation(zs[:, q % 8, :], Z[q % 2], ACT.Identity, bias=k["shift"][:])
                act.wait_ge(c["var_done"].sem, c["var_done"](m - 1))
                act.activation(sq[:, q % 2, :], Z[q % 2], ACT.Square, bias=k["shift"][:]).then_inc(c["sq_done"].sem, 1)

            def root(i, q):
                m = i * BODY + q
                act.wait_ge(c["var_done"].sem, c["var_done"](m + 1))
                act.wait_ge(c["r_done"].sem, c["r_done"](m - 1))
                act.activation(log_var[:, q % 2, :], VAR, ACT.Ln, bias=k["unit"][:, 1:2]).then_inc(c["log_done"].sem, 1)
                act.wait_ge(c["log_done"].sem, c["log_done"](m + 1))
                act.wait_ge(c["xn_done"].sem, c["xn_done"](m - 3))
                act.activation(r[:, q % 4, :], log_var[:, q % 2, :], ACT.Exp, scale=-0.5).then_inc(c["r_done"].sem, 1)

            def lead(i, q0):
                act.preload_act_table_set(LN_SET)
                square(i, q0)
                for q in range(q0 + 1, q0 + MINI):
                    square(i, q)
                    root(i, q - 1)
                root(i, q0 + MINI - 1)

            def follow(i, q0):
                for q in range(q0, q0 + MINI):
                    m = i * BODY + q
                    for row in range(ROWS):
                        slot = (2 * q + row) % 4
                        act.wait_ge(c["proj_done"].sem, c["proj_done"](m * 2 + row + 1))
                        act.wait_ge(c["lr_done"].sem, c["lr_done"](m * 2 + row - 3))
                        act.activation(sig[:, slot, :].rearrange("p (b e) -> p b e", b=2), PAIR[row][:, :, 0:256],
                                       ACT.Sigmoid).then_inc(c["sig_done"].sem, 1)
                    act.wait_ge(c["gate_mm_done"].sem, c["gate_mm_done"](m + 1))
                    stored = c[f"gate_out{q % 4}"]
                    act.wait_ge(stored.sem, stored(i * 64 + q // 4 * 16))
                    act.activation(gates[:, q % 4, :], GATE, ACT.Sigmoid).then_inc(c["gate_done"].sem, 1)

            bodies_of(act, lead, follow)

        @block.vector
        def _(dve):
            def lead(i, q0):
                for q in range(q0, q0 + MINI):
                    m = i * BODY + q
                    dve.wait_ge(c["r_done"].sem, c["r_done"](m + 1))
                    dve.wait_ge(c["gate_mm_done"].sem, c["gate_mm_done"](m - 7))
                    dve.tensor_tensor(xn[:, q % 8, :], zs[:, q % 8, :], r[:, q % 4, :], ALU.mult).then_inc(c["xn_done"].sem, 1)

            def follow(i, q0):
                for q in range(q0, q0 + MINI):
                    m = i * BODY + q
                    b = q // SCH
                    if q % SCH == 0:
                        dve.wait_ge(c[f"lr_out{b}"].sem, c[f"lr_out{b}"](i * 128))
                    for row in range(ROWS):
                        slot = (2 * q + row) % 4
                        ready = c["masked"] if masked else c["sig_done"]
                        dve.wait_ge(ready.sem, ready(m * 2 + row + 1))
                        at = q % SCH * ROWS + row
                        dst = stage[:, b, :, :, :, :, at, :].rearrange("p b g l n h -> p b (g l n) h")
                        dve.tensor_tensor(dst, PAIR[row][:, :, 256:512].rearrange("p b (n h) -> p b n h", h=HG),
                                          sig[:, slot, :].rearrange("p (b n h) -> p b n h", b=2, h=HG), ALU.mult).then_inc(c["lr_done"].sem, 1)

            bodies_of(dve, lead, follow)

        if masked:
            @block.gpsimd
            def _(pool):
                def pair(i, q, row):
                    slot = (2 * q + row) % 4
                    m = i * BODY + q
                    pool.wait_ge(c["sig_done"].sem, c["sig_done"](m * 2 + row + 1))
                    t = sig[:, slot, :].rearrange("p (b g e) -> p b g e", b=2, g=2)
                    by_g = k["mask"][:].rearrange("p b (g i) -> p b g i", g=2)
                    mk = by_g[:, :, :, bass.ds(m * ROWS + row, 1)].to_broadcast([P, 2, 2, P])
                    pool.tensor_tensor(t, t, mk, ALU.mult).then_inc(c["masked"].sem, 1)

                with pool.Fori(0, bodies) as i:
                    for q in range(BODY):
                        for row in range(ROWS):
                            pair(i, q, row)

    for s in range(8):
        c[f"x_in{s}"].advance(16 * NCH // 8)
    for s in range(4):
        c[f"gate_out{s}"].advance(16 * NCH // 4)
    for s in range(2):
        c[f"lr_out{s}"].advance(128 * bodies)
    for name in ("z_done", "sq_done", "var_done", "log_done", "r_done", "xn_done", "gate_mm_done", "gate_done"):
        c[name].advance(NCH)
    for name in ("proj_done", "sig_done", "lr_done") + (("masked",) if masked else ()):
        c[name].advance(2 * NCH)


def project_plain(nc, n, HG, x, gate, left_right, c, k, ps):
    with ExitStack() as ctx:
        def sb(name, shape, dt=F32):
            return ctx.enter_context(nc.sbuf_tensor(f"{name}_{n}", shape, dt))

        xs, xn = sb("xs", [P, 8, CH]), sb("xn", [P, 4, CH])
        biased, product, gates = sb("biased", [P, 2, 4, P]), sb("product", [P, 2, 4, C]), sb("gates", [P, 4, CH])
        stage = sb("stage", [P, 2, 2, 2, 2, 16 // HG, SEG, HG])
        TILES, GATE = [ps[0][:, q, :] for q in range(2)], [ps[1][:, q, :] for q in range(2)]
        block = ctx.enter_context(nc.Block())
        bodies = NCH // BODY

        @block.sync
        def _(sp):
            def load(i, q):
                m = i * BODY + q
                sp.wait_ge(c["xn_done"].sem, c["xn_done"](m - 7))
                sp.dma_start(xs[:, q % 8, :], x[:, bass.ds(m * CH, CH)]).then_inc(c[f"x_in{q % 8}"].sem, 16)

            def store(i, q):
                m = i * BODY + q
                sp.wait_ge(c["gate_done"].sem, c["gate_done"](m + 1))
                sp.dma_start(gate[:, bass.ds(m * CH, CH)], gates[:, q % 4, :]).then_inc(c[f"gate_out{q % 4}"].sem, 16)
                if q % SCH == SCH - 1:
                    sp.wait_ge(c["lr_done"].sem, c["lr_done"](m + 1))
                    b = q // SCH
                    store_segment(sp, left_right, stage[:, b], i * 2 + b, HG, c[f"lr_out{b}"])

            for q in range(6):
                load(0, q)
            with sp.Fori(0, bodies - 1) as i:
                for q in range(BODY):
                    load(i, q + 6)
                    store(i, q)
            for q in range(BODY):
                if q + 6 < BODY:
                    load(bodies - 1, q + 6)
                store(bodies - 1, q)
            for s in range(4):
                sp.wait_ge(c[f"gate_out{s}"].sem, c[f"gate_out{s}"](16 * NCH // 4))
            for s in range(2):
                sp.wait_ge(c[f"lr_out{s}"].sem, c[f"lr_out{s}"](16 * 8 * bodies))

        @block.tensor
        def _(pe):
            with pe.Fori(0, bodies) as i:
                for q in range(BODY):
                    m = i * BODY + q
                    pe.wait_ge(c["xn_done"].sem, c["xn_done"](m + 1))
                    pe.wait_ge(c["masked"].sem, c["masked"](m - 1))
                    for t in range(4):
                        last = pe.matmul(TILES[q % 2][:, t * P:t * P + P], xn[:, q % 4, t * P:t * P + P],
                                         k["w_proj"][:, 0:P], start=True, stop=True)
                    last.then_inc(c["proj_done"].sem, 1)
                    pe.wait_ge(c["gate_done"].sem, c["gate_done"](m - 1))
                    pe.matmul(GATE[q % 2], k["w_proj"][:, CH:CH + P], xn[:, q % 4, :],
                              start=True, stop=True).then_inc(c["gate_mm_done"].sem, 1)

        @block.vector
        def _(dve):
            def affine(i, q):
                m = i * BODY + q
                load = c[f"x_in{q % 8}"]
                dve.wait_ge(load.sem, load(i * 32 + (q // 8 + 1) * 16))
                dve.wait_ge(c["gate_mm_done"].sem, c["gate_mm_done"](m - 3))
                dve.tensor_scalar(xn[:, q % 4, :], xs[:, q % 8, :], k["gn"][:, 6:7], k["gn"][:, 7:8],
                                  ALU.mult, ALU.add).then_inc(c["xn_done"].sem, 1)

            def multiply(i, q):
                m = i * BODY + q
                dve.wait_ge(c["proj_done"].sem, c["proj_done"](m + 1))
                dve.wait_ge(c["sig_done"].sem, c["sig_done"](m - 1))
                dve.tensor_tensor(biased[:, q % 2].rearrange("p a b -> p (a b)"), TILES[q % 2],
                                  k["mask"][:].rearrange("p a b -> p (a b)"), ALU.add).then_inc(c["masked"].sem, 1)
                dve.wait_ge(c["masked"].sem, c["masked"](m + 1))
                dve.wait_ge(c["lr_done"].sem, c["lr_done"](m - 1))
                dve.tensor_tensor(product[:, q % 2], biased[:, q % 2, :, 0:C], biased[:, q % 2, :, C:P],
                                  ALU.mult).then_inc(c["sig_done"].sem, 1)

            affine(0, 0)
            affine(0, 1)
            with dve.Fori(0, bodies - 1) as i:
                for q in range(BODY):
                    affine(i, q + 2)
                    multiply(i, q)
            for q in range(BODY):
                if q + 2 < BODY:
                    affine(bodies - 1, q + 2)
                multiply(bodies - 1, q)

        @block.scalar
        def _(act):
            with act.Fori(0, bodies) as i:
                for q in range(BODY):
                    m = i * BODY + q
                    b = q // SCH
                    if q % SCH == 0:
                        act.wait_ge(c[f"lr_out{b}"].sem, c[f"lr_out{b}"](i * 128))
                    act.wait_ge(c["sig_done"].sem, c["sig_done"](m + 1))
                    for row in range(ROWS):
                        at = q % SCH * ROWS + row
                        dst = stage[:, b, :, :, :, :, at, :].rearrange("p b g l n h -> p b (g l n) h")
                        last = act.activation(dst, product[:, q % 2, 2 * row:2 * row + 2, :].rearrange("p b (n h) -> p b n h", h=HG),
                                              ACT.Sigmoid)
                    last.then_inc(c["lr_done"].sem, 1)
                    act.wait_ge(c["gate_mm_done"].sem, c["gate_mm_done"](m + 1))
                    stored = c[f"gate_out{q % 4}"]
                    act.wait_ge(stored.sem, stored(i * 64 + q // 4 * 16))
                    act.activation(gates[:, q % 4, :], GATE[q % 2], ACT.Sigmoid,
                                   bias=k["vec"][:, V_GATE_B:V_GATE_B + 1]).then_inc(c["gate_done"].sem, 1)

    for s in range(8):
        c[f"x_in{s}"].advance(16 * NCH // 8)
    for s in range(4):
        c[f"gate_out{s}"].advance(16 * NCH // 4)
    for s in range(2):
        c[f"lr_out{s}"].advance(128 * bodies)
    for name in ("xn_done", "proj_done", "masked", "sig_done", "lr_done", "gate_mm_done", "gate_done"):
        c[name].advance(NCH)


def triangle(nc, n, turned, low, H, HG, left_right, O, c, k, ps):
    turns = H // HG // 2
    with ExitStack() as ctx:
        left = ctx.enter_context(nc.sbuf_tensor(f"left{n}", [P, 2, 2, S, HG], low))
        right = ctx.enter_context(nc.sbuf_tensor(f"right{n}", [P, 2, 2, S, HG], low))
        right_t = ctx.enter_context(nc.sbuf_tensor(f"right_t{n}", [P, 2, 2, S], F32)) if turned else None
        block = ctx.enter_context(nc.Block())

        def channel(t, s, h):
            return t * (2 * HG) + (s * HG + h)

        @block.sync
        def _(sp):
            with sp.Fori(0, turns) as t:
                for s in range(2):
                    sp.wait_ge(c["tri_done"].sem, c["tri_done"](channel(t, s, 0) - HG))
                    for lr, dst in ((0, left), (1, right)):
                        sp.dma_start(dst[:, s].rearrange("p b i h -> p (b i h)"),
                                     left_right[lr, bass.ds(t * 2 + s, 1)].rearrange("n k b s i h -> k (n b s i h)")
                                     ).then_inc(c[f"lr_in{s}"].sem, 16)

        @block.tensor
        def _(pe):
            def turn(t, s, h):
                ch = channel(t, s, h)
                pe.wait_ge(c["tr_copied"].sem, c["tr_copied"](ch - 1))
                for kb in range(2):
                    for jb in range(2):
                        at = kb * S + jb * P
                        last = pe.transpose(ps[2 + h % 2][:, 0, at:at + P],
                                            right[:, s, jb, kb * P:kb * P + P, h], k["ident"][:])
                last.then_inc(c["tr_done"].sem, 1)

            def contract(t, s, h):
                ch = channel(t, s, h)
                if turned:
                    pe.wait_ge(c["tr_copied"].sem, c["tr_copied"](ch + 1))
                pe.wait_ge(c["o_copied"].sem, c["o_copied"](ch - 3))
                for jb in range(2):
                    for kb in range(2):
                        stationary = (right_t[:, h % 2, kb, jb * P:jb * P + P] if turned
                                      else right[:, s, kb, jb * P:jb * P + P, h])
                        last = pe.matmul(ps[h % 4 // 2][:, h % 2, jb * S:jb * S + S], stationary,
                                         left[:, s, kb, :, h], start=(kb == 0), stop=(kb == 1))
                last.then_inc(c["tri_done"].sem, 1)

            with pe.Fori(0, turns) as t:
                for s in range(2):
                    load = c[f"lr_in{s}"]
                    pe.wait_ge(load.sem, load(t * 32 + 32))
                    if turned:
                        turn(t, s, 0)
                    for h in range(HG):
                        if turned and h + 1 < HG:
                            turn(t, s, h + 1)
                        contract(t, s, h)

        if turned:
            @block.vector
            def _(dve):
                with dve.Fori(0, turns) as t:
                    for s in range(2):
                        for h in range(HG):
                            ch = channel(t, s, h)
                            dve.wait_ge(c["tr_done"].sem, c["tr_done"](ch + 1))
                            dve.wait_ge(c["tri_done"].sem, c["tri_done"](ch - 1))
                            dve.tensor_copy(right_t[:, h % 2].rearrange("p b j -> p (b j)"),
                                            ps[2 + h % 2][:, 0, :]).then_inc(c["tr_copied"].sem, 1)

        @block.scalar
        def _(act):
            with act.Fori(0, turns) as t:
                for s in range(2):
                    for h in range(HG):
                        ch = channel(t, s, h)
                        act.wait_ge(c["tri_done"].sem, c["tri_done"](ch + 1))
                        dst = O[:].rearrange("p b i g h -> p b g i h")[:, :, :, :, bass.ds(ch, 1)].rearrange("p b g i h -> p b g (i h)")
                        act.activation(dst, ps[h % 4 // 2][:, h % 2, :].rearrange("p (b g i) -> p b g i", b=2, g=2),
                                       ACT.Copy).then_inc(c["o_copied"].sem, 1)

    for s in range(2):
        c[f"lr_in{s}"].advance(32 * turns)
    for name in ("tri_done", "o_copied") + (("tr_done", "tr_copied") if turned else ()):
        c[name].advance(H)


def output(nc, n, gate_first, H, O, x, gate, x_new, c, k, ps):
    counted = n < 3
    HH = 2 * H
    TOK = 4 * SEG
    STAT, CENTER, SCALE, TURN, GATED, OUTMM, OUTGATED = 14, 5, 4, 3, 2, 1 if gate_first else 2, 1
    LOAD_X, LOAD_G = 4, 6 if gate_first else 5
    RING = 4
    with ExitStack() as ctx:
        def sb(name, shape, dt=F32):
            return ctx.enter_context(nc.sbuf_tensor(f"out_{name}_{n}", shape, dt))

        xs, gs, xo = sb("xs", [P, RING, CH]), sb("gs", [P, RING, CH]), sb("xo", [P, RING, CH])
        centered, scaled = sb("centered", [P, RING, 2, 4, H]), sb("scaled", [P, RING, 2, 4, H])
        if gate_first:
            wt, u = sb("wt", [P, RING, CH]), sb("u", [P, RING, CH])
        else:
            u, og = sb("u", [HH, RING, CH]), sb("og", [P, RING, CH])
        bn = sb("bn", [P, 2, 2, 2 * SEG, 6])
        small = sb("small", [P, 4, TOK])
        mu, std, rs = sb("mu", [P, 2, 2, 2 * SEG]), sb("std", [P, 2, TOK]), sb("rs", [P, 2, 2, 2 * SEG])
        var = sb("var", [P, 2, TOK])
        TURNED, OUT = [ps[q // 2][0:HH, q % 2, :] for q in range(4)], [ps[2 + q // 2][:, q % 2, :] for q in range(4)]
        block = ctx.enter_context(nc.Block())
        bodies = NCH // BODY
        rows = O[:].rearrange("p b i g h -> p b (i g) h")

        def bodies_of(eng, step):
            with eng.Fori(0, bodies - 1) as i:
                for q in range(BODY):
                    step(i, q, lambda lead: True)
            for q in range(BODY):
                step(bodies - 1, q, lambda lead: q + lead < BODY)

        @block.sync
        def _(sp):
            def load_x(i, q):
                m = i * BODY + q
                free = c["out_mm_done"] if gate_first else c["x_new"]
                sp.wait_ge(free.sem, free(m - 3))
                sp.dma_start(xs[:, q % RING, :], x[:, bass.ds(m * CH, CH)]).then_inc(c[f"xc_in{q % RING}"].sem, 16)

            def load_g(i, q):
                m = i * BODY + q
                free = c["gated"] if gate_first else c["out_gated"]
                sp.wait_ge(free.sem, free(m - 3))
                sp.dma_start(gs[:, q % RING, :], gate[:, bass.ds(m * CH, CH)]).then_inc(c[f"gc_in{q % RING}"].sem, 16)

            def step(i, q, more):
                if more(LOAD_G):
                    load_g(i, q + LOAD_G)
                if more(LOAD_X):
                    load_x(i, q + LOAD_X)
                m = i * BODY + q
                sp.wait_ge(c["x_new"].sem, c["x_new"](m + 1))
                sp.dma_start(x_new[:, bass.ds(m * CH, CH)], xo[:, q % RING, :]).then_inc(c[f"x_out{q % RING}"].sem, 16)

            for q in range(4):
                load_g(0, q)
                load_x(0, q)
            for q in range(4, LOAD_G):
                load_g(0, q)
            bodies_of(sp, step)
            for s in range(RING):
                sp.wait_ge(c[f"x_out{s}"].sem, c[f"x_out{s}"](16 * NCH // RING))

        @block.vector
        def _(dve):
            def statistics(i, q):
                b = q // SCH % 2
                for jb in range(2):
                    for t in range(2 * ROWS):
                        at = q % SCH * 2 * ROWS + t
                        last = dve.bn_stats(bn[:, b, jb, at, :],
                                            rows[:, jb, bass.ds(i * (BODY * 2 * ROWS) + q * 2 * ROWS + t, 1), :].rearrange("p a h -> p (a h)"))
                last.then_inc(c["ln_stat"].sem, 1)

            def moments(i, b):
                batch = i * (BODY // SCH) + b
                v = bn[:, b % 2].rearrange("p b t s -> p (b t) s")
                col = [v[:, :, q:q + 1].rearrange("p t s -> p (t s)") for q in range(6)]
                dve.wait_ge(c["ln_stat"].sem, c["ln_stat"](batch * SCH + SCH))
                dve.tensor_tensor(small[:, 0], col[1], col[4], ALU.add)
                dve.tensor_tensor(small[:, 1], col[1], col[4], ALU.subtract)
                dve.tensor_tensor(small[:, 2], col[2], col[5], ALU.add).then_inc(c["ln_small"].sem, 1)
                dve.wait_ge(c["ln_small"].sem, c["ln_small"](batch * 2 + 1))
                dve.wait_ge(c["centered"].sem, c["centered"](batch * SCH - SCH))
                dve.tensor_scalar(mu[:, b % 2].rearrange("p b t -> p (b t)"), small[:, 0], 0.5, None, ALU.mult)
                dve.scalar_tensor_tensor(small[:, 3], small[:, 1], 0.25, small[:, 1], ALU.mult, ALU.mult).then_inc(c["ln_small"].sem, 1)
                dve.wait_ge(c["ln_small"].sem, c["ln_small"](batch * 2 + 2))
                dve.scalar_tensor_tensor(var[:, b % 2], small[:, 2], 1.0 / H, small[:, 3], ALU.mult, ALU.add).then_inc(c["ln_var"].sem, 1)

            def invert(i, b):
                batch = i * (BODY // SCH) + b
                dve.wait_ge(c["ln_root"].sem, c["ln_root"](batch + 1))
                dve.reciprocal(rs[:, b % 2].rearrange("p b t -> p (b t)"), std[:, b % 2]).then_inc(c["ln_scale"].sem, 1)
                dve.wait_ge(c["ln_scale"].sem, c["ln_scale"](batch + 1))

            def scale(i, q):
                m = i * BODY + q
                dve.wait_ge(c["centered"].sem, c["centered"](m + 1))
                dve.wait_ge(c["wt_done"].sem, c["wt_done"](m - 3))
                at = q % SCH * 2 * ROWS
                r4 = rs[:, q // SCH % 2, :, at:at + 2 * ROWS].unsqueeze(3).to_broadcast([P, 2, 2 * ROWS, H])
                dve.tensor_tensor(scaled[:, q % RING], centered[:, q % RING], r4, ALU.mult).then_inc(c["scaled"].sem, 1)

            def gate_output(i, q):
                m = i * BODY + q
                dve.wait_ge(c["out_mm_done"].sem, c["out_mm_done"](m + 1))
                load = c[f"gc_in{q % RING}"]
                dve.wait_ge(load.sem, load(i * 64 + (q // RING + 1) * 16))
                dve.wait_ge(c["x_new"].sem, c["x_new"](m - 3))
                dve.scalar_tensor_tensor(og[:, q % RING], OUT[q % 4], k["out_bias"][:], gs[:, q % RING, :],
                                         ALU.add, ALU.mult).then_inc(c["out_gated"].sem, 1)

            def count(i, q):
                m = i * BODY + q
                dve.wait_ge(c["x_new"].sem, c["x_new"](m + 1))
                dve.bn_stats(k["gn_stats"][:, bass.ds(m, 1), :].rearrange("p a b -> p (a b)"), xo[:, q % RING, :]).then_inc(c["counted"].sem, 1)

            def step(i, q, more):
                if more(STAT):
                    statistics(i, q + STAT)
                    if (q + STAT) % SCH == SCH - 1:
                        moments(i, (q + STAT) // SCH)
                if more(SCALE):
                    if (q + SCALE) % SCH == 0:
                        invert(i, (q + SCALE) // SCH)
                    scale(i, q + SCALE)
                if not gate_first and more(OUTGATED):
                    gate_output(i, q + OUTGATED)
                if counted:
                    count(i, q)

            for q in range(SCH):
                statistics(0, q)
            moments(0, 0)
            for q in range(STAT - SCH):
                statistics(0, q + SCH)
                if q == 0:
                    invert(0, 0)
                if q < SCALE:
                    scale(0, q)
            if not gate_first:
                for q in range(OUTGATED):
                    gate_output(0, q)
            bodies_of(dve, step)

        @block.gpsimd
        def _(pool):
            def center(i, q):
                m = i * BODY + q
                if q % SCH == 0:
                    batch = i * (BODY // SCH) + q // SCH
                    pool.wait_ge(c["ln_var"].sem, c["ln_var"](batch + 1))
                pool.wait_ge(c["scaled"].sem, c["scaled"](m - 3))
                at = q % SCH * 2 * ROWS
                mu4 = mu[:, q // SCH % 2, :, at:at + 2 * ROWS].unsqueeze(3).to_broadcast([P, 2, 2 * ROWS, H])
                pool.tensor_tensor(centered[:, q % RING], rows[:, :, bass.ds(m * 2 * ROWS, 2 * ROWS), :], mu4,
                                   ALU.subtract).then_inc(c["centered"].sem, 1)

            def gate_input(i, q):
                m = i * BODY + q
                pool.wait_ge(c["wt_copied"].sem, c["wt_copied"](m + 1))
                load = c[f"gc_in{q % RING}"]
                pool.wait_ge(load.sem, load(i * 64 + (q // RING + 1) * 16))
                pool.wait_ge(c["out_mm_done"].sem, c["out_mm_done"](m - 3))
                pool.tensor_tensor(u[:, q % RING], wt[:, q % RING], gs[:, q % RING, :], ALU.mult).then_inc(c["gated"].sem, 1)

            def add_residual(i, q):
                m = i * BODY + q
                pool.wait_ge(c["out_gated"].sem, c["out_gated"](m + 1))
                load, stored = c[f"xc_in{q % RING}"], c[f"x_out{q % RING}"]
                pool.wait_ge(load.sem, load(i * 64 + (q // RING + 1) * 16))
                pool.wait_ge(stored.sem, stored(i * 64 + q // RING * 16))
                if counted:
                    pool.wait_ge(c["counted"].sem, c["counted"](m - 3))
                pool.tensor_tensor(xo[:, q % RING, :], og[:, q % RING], xs[:, q % RING, :], ALU.add).then_inc(c["x_new"].sem, 1)

            def step(i, q, more):
                if more(CENTER):
                    center(i, q + CENTER)
                if gate_first:
                    if more(GATED):
                        gate_input(i, q + GATED)
                else:
                    add_residual(i, q)

            for q in range(CENTER):
                center(0, q)
            if gate_first:
                for q in range(GATED):
                    gate_input(0, q)
            bodies_of(pool, step)

        @block.tensor
        def _(pe):
            def turn(i, q):
                m = i * BODY + q
                pe.wait_ge(c["scaled"].sem, c["scaled"](m + 1))
                pe.wait_ge(c["wt_copied"].sem, c["wt_copied"](m - 3))
                for row in range(ROWS):
                    for jb in range(2):
                        at = row * S + jb * P
                        last = pe.transpose(TURNED[q % 4][:, at:at + P],
                                            scaled[:, q % RING, jb, 2 * row:2 * row + 2, :].rearrange("p g h -> p (g h)"), k["ident"][:])
                last.then_inc(c["wt_done"].sem, 1)

            def multiply(i, q):
                m = i * BODY + q
                ready = c["gated"] if gate_first else c["wt_copied"]
                pe.wait_ge(ready.sem, ready(m + 1))
                bank_free = c["x_new"] if gate_first else c["out_gated"]
                pe.wait_ge(bank_free.sem, bank_free(m - 3))
                if gate_first:
                    pe.matmul(OUT[q % 4], k["w_out"][:], u[:, q % RING], start=True, stop=False)
                    load = c[f"xc_in{q % RING}"]
                    pe.wait_ge(load.sem, load(i * 64 + (q // RING + 1) * 16))
                    mm = pe.matmul(OUT[q % 4], k["ident"][:], xs[:, q % RING, :], start=False, stop=True)
                else:
                    mm = pe.matmul(OUT[q % 4], k["w_out"][0:HH, :], u[:, q % RING], start=True, stop=True)
                mm.then_inc(c["out_mm_done"].sem, 1)

            def step(i, q, more):
                if more(TURN):
                    turn(i, q + TURN)
                if more(OUTMM):
                    multiply(i, q + OUTMM)

            for q in range(TURN):
                turn(0, q)
            for q in range(OUTMM):
                multiply(0, q)
            bodies_of(pe, step)

        @block.scalar
        def _(act):
            def copy(i, q):
                m = i * BODY + q
                act.wait_ge(c["wt_done"].sem, c["wt_done"](m + 1))
                free = c["gated"] if gate_first else c["out_mm_done"]
                act.wait_ge(free.sem, free(m - 3))
                if gate_first:
                    ins = act.activation(wt[:, q % RING], TURNED[q % 4], ACT.Identity, scale=k["vec"][:, V_ON_G:V_ON_G + 1],
                                         bias=k["vec"][:, V_ON_B:V_ON_B + 1])
                else:
                    ins = act.activation(u[:, q % RING], TURNED[q % 4], ACT.Copy)
                ins.then_inc(c["wt_copied"].sem, 1)

            def root(i, b):
                batch = i * (BODY // SCH) + b
                act.wait_ge(c["ln_var"].sem, c["ln_var"](batch + 1))
                act.wait_ge(c["ln_scale"].sem, c["ln_scale"](batch - 1))
                act.activation(std[:, b % 2], var[:, b % 2], ACT.Sqrt, bias=k["unit"][:, 2:3]).then_inc(c["ln_root"].sem, 1)

            def step(i, q, more):
                if more(TURN):
                    copy(i, q + TURN)
                if gate_first:
                    m = i * BODY + q
                    act.wait_ge(c["out_mm_done"].sem, c["out_mm_done"](m + 1))
                    stored = c[f"x_out{q % RING}"]
                    act.wait_ge(stored.sem, stored(i * 64 + q // RING * 16))
                    act.wait_ge(c["counted"].sem, c["counted"](m - 3))
                    act.activation(xo[:, q % RING, :], OUT[q % 4], ACT.Copy).then_inc(c["x_new"].sem, 1)
                if more(STAT) and (q + STAT) % SCH == SCH - 1:
                    root(i, (q + STAT) // SCH)

            root(0, 0)
            for q in range(TURN):
                copy(0, q)
            bodies_of(act, step)

    for s in range(RING):
        for name in ("xc_in", "gc_in", "x_out"):
            c[f"{name}{s}"].advance(16 * NCH // RING)
    batches = NCH // SCH
    for name in ("ln_var", "ln_root", "ln_scale"):
        c[name].advance(batches)
    c["ln_small"].advance(2 * batches)
    for name in ("ln_stat", "centered", "scaled", "wt_done", "wt_copied", "out_mm_done", "x_new",
                 "gated" if gate_first else "out_gated") + (("counted",) if counted else ()):
        c[name].advance(NCH)


def constants():
    basis = np.zeros((C, C), np.float32)
    for m in range(C - 1):
        basis[:m + 1, m] = 1 / np.sqrt((m + 1) * (m + 2))
        basis[m + 1, m] = -(m + 1) / np.sqrt((m + 1) * (m + 2))
    both = np.kron(np.eye(2), np.ones((C, C)))
    live = (np.arange(P) % C != C - 1)
    group = np.arange(P) % C // 2
    unit = np.zeros((P, 3), np.float32)
    unit[:, 0] = ~live
    unit[:, 1] = np.where(live, EPS, 1)
    unit[:, 2] = EPS
    last_row = np.zeros((2, P), np.float32)
    last_row[0, C - 1] = last_row[1, P - 1] = 1
    return {
        "basis": np.kron(np.eye(2), basis), "var_w": both * live[:, None] * live[None, :] / C, "ident": np.eye(P),
        "pool_w": (group[:, None] == group[None, :]) / 4, "last_row": last_row, "unit": unit, "one": np.ones((1, P)),
    }


def twice(w):
    out = np.zeros((2, w.shape[0], 2, w.shape[1]), np.float32)
    for g in range(2):
        out[g, :, g, :] = w
    return out.reshape(2 * w.shape[0], 2 * w.shape[1])


def layouts(inputs):
    v = {name: np.asarray(value) for name, value in inputs.items()}
    x = v["x"].reshape(2, HALF * S, C).transpose(0, 2, 1).reshape(P, HALF * S)
    arrays = {"x": x}
    arrays.update(constants())

    columns = {"LN_G": V_LN_G, "LN_B": V_LN_B, "ON_G": V_ON_G, "ON_B": V_ON_B, "GATE_B": V_GATE_B, "OUT_B": V_OUT_B}

    def vectors(**by_column):
        out = np.zeros((P, NVEC), np.float32)
        for name, w in by_column.items():
            w = np.concatenate([w, w])
            out[:len(w), columns[name]] = w
        return out

    def add(n, gates, projections, out_gate, w_out, vec, gate_bias=None, proj_bias=None, out_gate_bias=None):
        w = [twice(np.concatenate(part, axis=1)) for part in (gates, projections)] + [twice(out_gate)]
        arrays[f"w_proj{n}"] = np.concatenate(w, axis=1)
        rows = np.zeros((2, 640), np.float32)
        if gate_bias is not None:
            for at, bias in ((0, np.concatenate(gate_bias)), (256, np.concatenate(proj_bias)), (512, out_gate_bias)):
                for g in range(2):
                    rows[g, at + g * len(bias):at + (g + 1) * len(bias)] = bias
        arrays[f"b_rows{n}"] = rows
        arrays[f"w_out{n}"] = twice(w_out)
        arrays[f"vec{n}"] = vec

    l0 = {q: v["L0_conv_" + q] for q in ("norm_g", "norm_b", "Wl", "Wr", "Wlg", "Wrg", "Wog", "out_norm_g", "out_norm_b", "Wout")}
    add(0, (l0["Wlg"].T, l0["Wrg"].T), (l0["Wl"].T, l0["Wr"].T), l0["Wog"].T, l0["Wout"].T,
        vectors(LN_G=l0["norm_g"], LN_B=l0["norm_b"], ON_G=l0["out_norm_g"], ON_B=l0["out_norm_b"]))
    arrays["mask0"] = v["L0_conv_mask"].reshape(S, S)
    l1 = {q: v["L1_conv_" + q] for q in ("norm_w", "norm_b", "w_left", "w_right", "w_lgate", "w_rgate", "w_ogate", "onorm_w", "onorm_b", "w_out")}
    add(1, (l1["w_lgate"].T, l1["w_rgate"].T), (l1["w_left"].T, l1["w_right"].T), l1["w_ogate"].T, l1["w_out"].T,
        vectors(LN_G=l1["norm_w"], LN_B=l1["norm_b"], ON_G=l1["onorm_w"], ON_B=l1["onorm_b"]))
    arrays["mask1"] = v["L1_conv_mask"].reshape(S, S)
    l2 = {q: v["L2_conv_" + q] for q in ("Wa1", "ba1", "Wa2", "ba2", "Wb1", "bb1", "Wb2", "bb2", "ln2_g", "ln2_b", "Wg", "bg", "Wz", "bz")}
    w = np.zeros((P, 640), np.float32)
    for half, parts in enumerate((("Wa1", "Wb1"), ("Wa2", "Wb2"))):
        w[:, half * C:half * C + C] = twice(np.concatenate([l2[q] for q in parts], axis=1))
    w[:, 512:640] = twice(l2["Wg"])
    arrays["w_proj2"] = w
    rows = np.zeros((2, 640), np.float32)
    tile = np.concatenate([np.concatenate([l2[q] for q in parts] * 2) for parts in (("ba1", "bb1"), ("ba2", "bb2"))])
    rows[0, 0:512] = np.concatenate([tile] * 4)
    arrays["b_rows2"] = rows
    w_out = np.zeros((P, P), np.float32)
    w_out[:32] = twice(l2["Wz"])
    arrays["w_out2"] = w_out
    arrays["vec2"] = vectors(ON_G=l2["ln2_g"], ON_B=l2["ln2_b"], GATE_B=l2["bg"], OUT_B=l2["bz"])
    l3 = {q: v["L3_conv_" + q] for q in ("ln_in_w", "ln_in_b", "Wga", "bga", "Wla", "bla", "Wgb", "bgb", "Wlb", "blb", "ln_o_w", "ln_o_b", "Wgo", "bgo", "Wlo", "blo")}
    add(3, (l3["Wga"], l3["Wgb"]), (l3["Wla"], l3["Wlb"]), l3["Wgo"], l3["Wlo"],
        vectors(LN_G=l3["ln_in_w"], LN_B=l3["ln_in_b"], ON_G=l3["ln_o_w"], ON_B=l3["ln_o_b"], OUT_B=l3["blo"]),
        (l3["bga"], l3["bgb"]), (l3["bla"], l3["blb"]), l3["bgo"])
    return {name: np.ascontiguousarray(value, dtype=np.float32) for name, value in arrays.items()}


def scratch(nc):
    out = {}
    for name in ("x_dram0", "x_dram1", "gate"):
        out[name] = nc.dram_tensor(name, [P, HALF * S], F32, kind="Internal").ap()
    for n, (groups, per, dt) in enumerate(((8, 8, F32), (4, 16, BF16), (2, 8, F32), (8, 8, F32))):
        out[f"left_right{n}"] = nc.dram_tensor(f"left_right{n}", [2, groups, P, 2, S // SEG, SEG, per], dt, kind="Internal").ap()
    return out


def kernel(**inputs):
    import concourse.bacc as bacc
    from concourse.bass_utils import run_bass_kernel_spmd

    nc = bacc.Bacc("TRN2", target_bir_lowering=False, num_devices=1)
    arrays = layouts(inputs)
    a = {name: nc.dram_tensor(f"in_{name}", list(v.shape), F32, kind="ExternalInput").ap() for name, v in arrays.items()}
    a.update(scratch(nc))
    out = nc.dram_tensor("out", [P, HALF * S], F32, kind="ExternalOutput").ap()
    build(nc, a, out)
    r = run_bass_kernel_spmd(nc, [{f"in_{name}": v for name, v in arrays.items()}], core_ids=[0])
    y = np.asarray(r.results[0]["out"])
    return y.reshape(2, C, HALF * S).transpose(0, 2, 1).reshape(1, S, S, C)
```

```python
from contextlib import ExitStack

import numpy as np

import concourse.bass as bass
from concourse import mybir

F32 = mybir.dt.float32
BF16 = mybir.dt.bfloat16
F16 = mybir.dt.float16
ALU = mybir.AluOpType
ACT = mybir.ActivationFunctionType
AXIS = mybir.AxisListType

P = 128
S = 256
C = 64
HALF = S // 2
CH = 512
NCH = HALF * S // CH
ROWS = CH // S
SEG = 16
SCH = SEG // ROWS
BODY = 2 * SCH
BATCH = 8
R_PART, R_ONE = 32, 96
EPS = 1e-5
FIRST = 16
LN_SET = "natural_log_exp_and_others"

V_LN_G, V_LN_B, V_ON_G, V_ON_B, V_GATE_B, V_OUT_B, NVEC = range(7)


class Counter:

    def __init__(self, handle, base):
        self.sem, self.base = handle, base

    def __call__(self, n):
        return n + self.base

    def advance(self, n):
        self.base += n


def build(nc, a, out):
    with ExitStack() as ctx:
        def sb(name, shape, dt=F32):
            return ctx.enter_context(nc.sbuf_tensor(name, shape, dt))

        def counter(name, base=FIRST):
            return Counter(ctx.enter_context(nc.semaphore(name)), base)

        k = {
            "basis": sb("basis", [P, P]), "var_w": sb("var_w", [P, 4 * BATCH - 2]), "ident": sb("ident", [P, P]),
            "pool_w": sb("pool_w", [P, P]), "last_row": sb("last_row", [2, P]), "unit": sb("unit", [P, 3]),
            "gn": sb("gn", [P, 12]), "gn_stats": sb("gn_stats", [P, NCH, 6]),
            "vec": sb("vec", [P, NVEC]), "center": sb("center", [P, P]), "shift": sb("shift", [P, 1]),
            "w_out": sb("w_out", [P, P]),
            "out_bias": sb("out_bias", [P, 1]), "one": sb("one", [1, P]),
            "mask": sb("mask", [P, 2, S]),
        }
        ps = [ctx.enter_context(nc.psum_tensor(f"ps{n}", [P, 2, 512], F32)) for n in range(4)]
        c = {n: counter(n) for n in (
            "fold_vec", "fold_mm", "fold_act", "stat_done", "z_done", "sq_done", "var_done", "log_done", "r_done", "r_part", "r_split", "spread_done",
            "xn_done", "hi_done", "lo_done", "proj_done", "gate_mm_done", "sig_done", "gate_done", "masked", "lr_done", "pair_read",
            "tr_done", "tr_copied", "tri_done", "o_copied",
            "ln_stat", "ln_small", "ln_var", "ln_root", "ln_scale", "centered", "scaled", "wt_done", "wt_copied", "gated",
            "out_mm_done", "u_cleared", "out_gated", "x_new", "counted")}
        for n, ring in (("const_in", 1), ("x_in", 8), ("stacked", 4), ("lr_out", 2), ("gate_out", 4), ("lr_in", 2),
                        ("xc_in", 4), ("gc_in", 4), ("x_out", 4)):
            for i in range(ring):
                c[f"{n}{i}"] = counter(f"{n}{i}", 16)
        start_counters(nc, c, k, a)
        first_statistics(nc, a["x"], c, k)
        x = a["x"]
        for n, kind in enumerate(("masked", "masked_bf16", "plain", "normed")):
            x_new = out if n == 3 else a[f"x_dram{n % 2}"]
            layer(nc, n, kind, a, x, x_new, c, k, ps)
            x = x_new


def start_counters(nc, c, k, a):
    with nc.Block() as block:
        @block.sync
        def _(sp):
            for name, counter in c.items():
                sp.sem_inc(counter.sem, counter.base)


def first_statistics(nc, x, c, k):
    wide = 4 * CH
    turns = HALF * S // wide
    with ExitStack() as ctx:
        xin = ctx.enter_context(nc.sbuf_tensor("xin", [P, 4, wide], F32))
        block = ctx.enter_context(nc.Block())

        @block.sync
        def _(sp):
            with sp.Fori(0, turns // 4) as t:
                for s in range(4):
                    sp.wait_ge(c["stat_done"].sem, c["stat_done"](t * 4 + s - 3))
                    sp.dma_start(xin[:, s, :], x[:, bass.ds((t * 4 + s) * wide, wide)]).then_inc(c[f"xc_in{s}"].sem, 16)

        @block.vector
        def _(dve):
            with dve.Fori(0, turns // 4) as t:
                for s in range(4):
                    load = c[f"xc_in{s}"]
                    dve.wait_ge(load.sem, load(t * 16 + 16))
                    for q in range(4):
                        last = dve.bn_stats(k["gn_stats"][:, bass.ds(t * 16 + s * 4 + q, 1), :].rearrange("p a b -> p (a b)"),
                                            xin[:, s, q * CH:(q + 1) * CH])
                    last.then_inc(c["stat_done"].sem, 1)
    for s in range(4):
        c[f"xc_in{s}"].advance(16 * turns // 4)
    c["stat_done"].advance(turns)


def layer(nc, n, kind, a, x, x_new, c, k, ps):
    normed_in = kind != "plain"
    masked = kind in ("masked", "masked_bf16")
    low = BF16 if kind == "masked_bf16" else F32
    H = 16 if kind == "plain" else C
    HG = 16 if low == BF16 else 8
    left_right = a[f"left_right{n}"]
    with ExitStack() as ctx:
        shapes = ({"w_heads": ([P, 2, S], F16), "w_gate": ([P, 2, P], F16), "largest": ([P, 3], F32), "spread": ([P, BATCH, P], BF16)}
                  if normed_in else {"w_proj": ([P, 640], F32)})
        w = {name: ctx.enter_context(nc.sbuf_tensor(f"{name}{n}", *shape)) for name, shape in shapes.items()}
        fold(nc, n, kind, a, c, {**k, **w}, ps)
        if normed_in:
            project(nc, n, masked, low, HG, x, a["gate"], left_right, c, {**k, **w}, ps)
        else:
            project_plain(nc, n, HG, x, a["gate"], left_right, c, {**k, **w}, ps)
    with ExitStack() as ctx:
        O = ctx.enter_context(nc.sbuf_tensor(f"O{n}", [P, 2, HALF, 2, H], low))
        triangle(nc, n, not masked, low, H, HG, left_right, O, c, k, ps)
        output(nc, n, masked, H, O, x, a["gate"], x_new, c, k, ps)


def fold(nc, n, kind, a, c, k, ps):
    normed_in = kind != "plain"
    masked = kind in ("masked", "masked_bf16")
    fold_ctx = ExitStack()
    local = {name: fold_ctx.enter_context(nc.sbuf_tensor(f"{name}_{n}", shape, F32)) for name, shape in (
        ("w_raw", [P, 640]), ("w_scaled", [P, 640]), ("b_rows", [2, 640]), ("ln_sel", [P, P]), ("mask_in", [P, 2, S]),
        ("folded", [P, 640]), ("spread_in", [P, BATCH * P]), ("w_both", [P, 2, P]), ("size", [P, 3]), ("size_t", [3, 1]),
        ("h_center", [P, P]), ("size_diag", [3, 3]), ("ones3", [3, P]), ("inverse", [P, 3]))}
    k = {**k, **local}
    loads = [(k["vec"][:], a[f"vec{n}"]), (k["w_raw"][:], a[f"w_proj{n}"]), (k["w_out"][:], a[f"w_out{n}"]),
             (k["b_rows"][:], a[f"b_rows{n}"])]
    if n == 0:
        loads += [(k[x][:], a[x]) for x in ("basis", "var_w", "ident", "pool_w", "last_row", "unit", "one")]
    if not masked:
        loads += [(k["h_center"][:], a[f"h_center{n}"])]
    if normed_in:
        loads += [(k["spread_in"][:], a["spread"])]
    if masked:
        loads += [(k["mask_in"][:], a[f"mask{n}"].rearrange("(b p) k -> p b k", p=P))]
    gn, vec, unit = k["gn"], k["vec"], k["unit"]
    mean, var, group_mean, off, power, std, scale, shift = (gn[:, q:q + 1] for q in range(8))
    mm, done, act_done, loaded = c["fold_mm"], c["fold_vec"], c["fold_act"], c["const_in0"]
    out_rows = P if normed_in else 32
    P_MEAN, P_VAR, P_SHIFT, P_PROJ, P_GATE, P_TURN, P_BIAS, P_SIZE = (ps[q // 2][:, q % 2, :] for q in range(8))
    steps = [0]
    scaled_step, centered_mm = (32, 8) if normed_in else (10, 5)

    with fold_ctx, nc.Block() as block:
        @block.sync
        def _(sp):
            for dst, src in loads:
                sp.dma_start(dst, src).then_inc(loaded.sem, 16)

        @block.tensor
        def _(pe):
            pe.wait_ge(loaded.sem, loaded(16 * len(loads)))
            if masked:
                for kb in range(2):
                    for ib in range(2):
                        at = kb * S + ib * P
                        last = pe.transpose(P_TURN[:, at:at + P], k["mask_in"][:, ib, kb * P:kb * P + P], k["ident"][:])
            else:
                last = pe.matmul(P_BIAS[:, 0:1], k["w_out"][0:out_rows, :], vec[0:out_rows, V_ON_B:V_ON_B + 1],
                                 start=True, stop=True)
            last.then_inc(mm.sem, 1)
            pe.wait_ge(done.sem, done(1))
            pe.matmul(P_MEAN[:, 0:1], k["pool_w"][:], mean, start=True, stop=True).then_inc(mm.sem, 1)
            pe.wait_ge(done.sem, done(4))
            pe.matmul(P_VAR[:, 0:1], k["pool_w"][:], power, start=True, stop=True).then_inc(mm.sem, 1)
            if normed_in:
                pe.wait_ge(done.sem, done(6))
                pe.matmul(P_SHIFT[:, 0:1], k["basis"][:], shift, start=True, stop=True).then_inc(mm.sem, 1)
                pe.wait_ge(done.sem, done(12))
                for lo, hi, bank in ((0, 512, P_PROJ), (512, 640, P_GATE)):
                    w = hi - lo
                    pe.matmul(bank[:, 0:w], k["basis"][:], k["w_scaled"][:, lo:hi], start=True, stop=False)
                    pe.matmul(bank[:, 0:w], k["ln_sel"][:], k["w_raw"][:, lo:hi], start=False, stop=False)
                    last = pe.matmul(bank[:, 0:w], k["last_row"][:], k["b_rows"][:, lo:hi], start=False, stop=True)
                last.then_inc(mm.sem, 1)
                pe.wait_ge(done.sem, done(16))
                pe.transpose(P_SIZE[0:3, 0:P], k["size"][:], k["ident"][:]).then_inc(mm.sem, 1)
                pe.wait_ge(done.sem, done(19))
                pe.matmul(P_SIZE[:, P:P + 3], k["ones3"][:], k["size_diag"][:], start=True, stop=True).then_inc(mm.sem, 1)
            else:
                pe.matmul(P_PROJ, k["one"][:], k["b_rows"][0:1, 0:CH], start=True, stop=True).then_inc(mm.sem, 1)
            if not masked:
                pe.wait_ge(done.sem, done(scaled_step))
                pe.matmul(P_BIAS[:, P:2 * P], k["h_center"][:], k["w_out"][:], start=True, stop=True).then_inc(mm.sem, 1)

        @block.scalar
        def _(act):
            act.wait_ge(mm.sem, mm(3))
            act.activation(std, P_VAR[:, 0:1], ACT.Sqrt, bias=unit[:, 2:3]).then_inc(act_done.sem, 1)

        @block.vector
        def _(dve):
            def step(ins):
                steps[0] += 1
                ins.then_inc(done.sem, 1)
                dve.wait_ge(done.sem, done(steps[0]))

            dve.wait_ge(loaded.sem, loaded(16 * len(loads)))
            step(dve.bn_aggr(gn[:, 0:2], k["gn_stats"][:].rearrange("p a b -> p (a b)")))
            dve.wait_ge(mm.sem, mm(2))
            step(dve.tensor_copy(group_mean, P_MEAN[:, 0:1]))
            step(dve.tensor_tensor(off, mean, group_mean, ALU.subtract))
            step(dve.scalar_tensor_tensor(power, off, off, var, ALU.mult, ALU.add))
            dve.wait_ge(act_done.sem, act_done(1))
            step(dve.reciprocal(scale, std))
            step(dve.scalar_tensor_tensor(shift, group_mean, -1.0, scale, ALU.mult, ALU.mult))
            if normed_in:
                step(dve.tensor_scalar(k["center"][:], k["basis"][:], scale, None, ALU.mult))
                dve.wait_ge(mm.sem, mm(4))
                step(dve.tensor_tensor(k["shift"][:], P_SHIFT[:, 0:1], unit[:, 0:1], ALU.add))
                step(dve.memset(k["ln_sel"][:], 0.0))
                for g in range(2):
                    half, last_col = slice(g * C, g * C + C), g * C + C - 1
                    step(dve.tensor_copy(k["ln_sel"][half, last_col:last_col + 1], vec[half, V_LN_B:V_LN_B + 1]))
                step(dve.tensor_scalar(k["w_scaled"][:], k["w_raw"][:], vec[:, V_LN_G:V_LN_G + 1], None, ALU.mult))
                dve.wait_ge(mm.sem, mm(5))
                folded = k["folded"]
                step(dve.tensor_copy(folded[:, 0:CH], P_PROJ))
                step(dve.tensor_copy(folded[:, CH:640], P_GATE[:, 0:P]))
                step(dve.tensor_reduce(k["size"][:, 0:2], folded[:, 0:CH].rearrange("p (a e) -> p a e", a=2), AXIS.X, ALU.max,
                                       apply_absolute_value=True))
                step(dve.tensor_reduce(k["size"][:, 2:3], folded[:, CH:640], AXIS.X, ALU.max, apply_absolute_value=True))
                step(dve.memset(k["ones3"][:], 1.0))
                dve.wait_ge(mm.sem, mm(6))
                step(dve.tensor_reduce(k["size_t"][:], P_SIZE[0:3, 0:P], AXIS.X, ALU.max))
                step(dve.tensor_scalar(k["size_diag"][:], k["ident"][0:3, 0:3], k["size_t"][:], None, ALU.mult))
                dve.wait_ge(mm.sem, mm(7))
                step(dve.tensor_scalar(k["largest"][:], P_SIZE[:, P:P + 3], 1e-30, None, ALU.max))
                step(dve.reciprocal(k["inverse"][:], k["largest"][:]))
                for group, (lo, hi) in enumerate(((0, S), (S, CH), (CH, 640))):
                    step(dve.tensor_scalar(folded[:, lo:hi], folded[:, lo:hi], k["inverse"][:, group:group + 1], None, ALU.mult))
                parts = folded[:, 0:CH].rearrange("p (a g e) -> p a g e", a=2, g=2)
                step(dve.tensor_tensor(k["w_both"][:], parts[:, :, 0, :], parts[:, :, 1, :], ALU.add))
                for w, halves in ((k["w_both"][:].rearrange("p a e -> p (a e)"), k["w_heads"]), (folded[:, CH:640], k["w_gate"])):
                    step(dve.tensor_copy(halves[:, 0, :], w))
                    step(dve.tensor_tensor(halves[:, 1, :], w, halves[:, 0, :], ALU.subtract))
                step(dve.tensor_copy(k["spread"][:].rearrange("p a b -> p (a b)"), k["spread_in"][:]))
            else:
                step(dve.tensor_copy(k["w_proj"][:], k["w_raw"][:]))
                dve.wait_ge(mm.sem, mm(4))
                step(dve.tensor_copy(k["mask"][:].rearrange("p a b -> p (a b)"), P_PROJ))
            if masked:
                step(dve.tensor_copy(k["mask"][:].rearrange("p a b -> p (a b)"), P_TURN))
            else:
                step(dve.tensor_tensor(k["out_bias"][:], P_BIAS[:, 0:1], vec[:, V_OUT_B:V_OUT_B + 1], ALU.add))
                step(dve.tensor_scalar(k["w_out"][:], k["w_out"][:], vec[:, V_ON_G:V_ON_G + 1], None, ALU.mult))
                assert steps[0] == scaled_step
                dve.wait_ge(mm.sem, mm(centered_mm))
                step(dve.tensor_copy(k["w_out"][:], P_BIAS[:, P:2 * P]))

    loaded.advance(16 * len(loads))
    mm.advance((7 if normed_in else 4) + (0 if masked else 1))
    act_done.advance(1)
    done.advance(steps[0])


SEG_PARTS = 8


def store_part(sp, left_right, stage, seg, HG, part, done):
    lr, kb, g = part // 4, part // 2 % 2, part % 2
    groups = left_right[lr].rearrange("n k b s i h -> k n b s (i h)")
    src = stage[:, kb, g, lr, :, :, :].rearrange("p n i h -> p n (i h)")
    dst = groups[:, :, kb, bass.ds(seg + g * (S // SEG // 2), 1), :].rearrange("k n s e -> k n (s e)")
    sp.dma_start(dst, src).then_inc(done.sem, 16)


def project(nc, n, masked, low, HG, x, gate, left_right, c, k, ps):
    LOAD, CENTER, VARIANCE, SPLIT, NORM = 16, 14, 13, 5, 4
    with ExitStack() as ctx:
        def sb(name, shape, dt=F32):
            return ctx.enter_context(nc.sbuf_tensor(f"{name}_{n}", shape, dt))

        xs, zs, sq = sb("xs", [P, 8, CH]), sb("zs", [P, 16, CH]), sb("sq", [P, 4, CH])
        log_var, r, r_rest, r_mid = (sb(name, [2 * BATCH, CH], dt) for name, dt in
                                     (("log_var", F32), ("r", F32), ("r_rest", F32), ("r_mid", BF16)))
        r_terms = sb("r_terms", [P, 2, CH], BF16)
        xn, hi, lo = sb("xn", [P, 2, CH]), sb("hi", [P, 8, CH], F16), sb("lo", [P, 8, CH], F16)
        stacked = sb("stacked", [P, 8, 2, CH], F16)
        sig, gates = sb("sig", [P, 4, CH]), sb("gates", [P, 4, CH])
        stage = sb("stage", [P, 2, 2, 2, 2, C // HG, SEG, HG], low)
        Z, VAR, R, GATE = ps[0][:, 0, :], ps[0][0:2 * BATCH, 1, :], ps[1][:, 0, :], ps[1][:, 1, :]
        PAIR = [ps[2], ps[3]]
        AHEAD_Z = [Z, GATE]
        pair_read = c["pair_read"] if masked else c["lr_done"]
        block = ctx.enter_context(nc.Block())
        bodies = NCH // BODY


        def staged(b, q, row):
            return stage[:, b, :, :, :, :, q % SCH * ROWS + row, :]

        def bodies_of(eng, step):
            with eng.Fori(0, bodies - 1) as i:
                for q in range(BODY):
                    step(i, q, lambda lead: True)
            for q in range(BODY):
                step(bodies - 1, q, lambda lead: q + lead < BODY)

        @block.sync
        def _(sp):

            def load(i, q):
                m = i * BODY + q
                sp.wait_ge(c["z_done"].sem, c["z_done"](m - 6))
                sp.dma_start(xs[:, q % 8:q % 8 + 2, :].rearrange("p a b -> p (a b)"),
                             x[:, bass.ds(m * CH, 2 * CH)]).then_inc(c[f"x_in{q % 8 // 2}"].sem, 16)

            def stack(i, q):
                m = i * BODY + q
                sp.wait_ge(c["lo_done"].sem, c["lo_done"](m + 2))
                slots = slice(q % 8, q % 8 + 2)
                for part, src in enumerate((hi, lo)):
                    for g in range(2):
                        sp.dma_start(stacked[part * C:part * C + C, slots, g, :],
                                     src[g * C:g * C + C, slots, :]).then_inc(c[f"stacked{q % 8 // 2}"].sem, 16)

            def store_gate(i, q):
                m = i * BODY + q
                sp.wait_ge(c["gate_done"].sem, c["gate_done"](m + 2))
                sp.dma_start(gate[:, bass.ds(m * CH, 2 * CH)],
                             gates[:, q % 4:q % 4 + 2, :].rearrange("p a b -> p (a b)")).then_inc(c[f"gate_out{q % 4 // 2}"].sem, 16)

            def store_parts(i, q):
                if q % SCH < SEG_PARTS // 2:
                    seg = q // SCH - 1
                    if q % SCH == 0:
                        sp.wait_ge(c["lr_done"].sem, c["lr_done"]((i * BODY + q) * 2))
                    for part in (q % SCH * 2, q % SCH * 2 + 1):
                        store_part(sp, left_right, stage[:, seg % 2], i * 2 + seg, HG, part, c[f"lr_out{seg % 2}"])

            def step(i, q, more, first=False):
                if q % 2 == 1:
                    if more(NORM):
                        stack(i, q + NORM - 1)
                elif more(LOAD):
                    load(i, q + LOAD)
                if not (first and q < SCH):
                    store_parts(i, q)
                if q % 2 == 1:
                    store_gate(i, q - 1)

            for q in range(0, LOAD, 2):
                load(0, q)
            for q in range(0, NORM, 2):
                stack(0, q)
            for q in range(BODY):
                step(0, q, lambda lead: True, first=True)
            with sp.Fori(1, bodies - 1) as i:
                for q in range(BODY):
                    step(i, q, lambda lead: True)
            for q in range(BODY):
                step(bodies - 1, q, lambda lead: q + lead < BODY)
            for q in range(SEG_PARTS // 2):
                store_parts(bodies, q)
            for s in range(2):
                sp.wait_ge(c[f"gate_out{s}"].sem, c[f"gate_out{s}"](16 * NCH // 4))
            for s in range(2):
                sp.wait_ge(c[f"lr_out{s}"].sem, c[f"lr_out{s}"](16 * SEG_PARTS * bodies))

        @block.tensor
        def _(pe):
            def center(i, q, bank, readers):
                m = i * BODY + q
                load = c[f"x_in{q % 8 // 2}"]
                pe.wait_ge(load.sem, load(i * 32 + (q // 8 + 1) * 16))
                pe.wait_ge(c["sq_done"].sem, c["sq_done"](readers))
                pe.matmul(bank, k["center"][:], xs[:, q % 8, :], start=True, stop=True).then_inc(c["z_done"].sem, 1)

            def variance(i, q):
                m = i * BODY + q
                pe.wait_ge(c["sq_done"].sem, c["sq_done"](m + 1))
                at = q % BATCH
                if at == 0:
                    batch = i * (BODY // BATCH) + q // BATCH
                    pe.wait_ge(c["log_done"].sem, c["log_done"](batch))
                w = k["var_w"][:, 2 * (BATCH - 1 - at):2 * (2 * BATCH - 1 - at)]
                pe.matmul(VAR, w, sq[:, q % 4, :], start=(at == 0), stop=(at == BATCH - 1)).then_inc(c["var_done"].sem, 1)

            def spread(i, q):
                m = i * BODY + q
                b = q // BATCH
                pe.wait_ge(c["r_split"].sem, c["r_split"](i * (BODY // BATCH) + b + 1))
                pe.wait_ge(c["xn_done"].sem, c["xn_done"](m))
                pe.matmul(R, k["spread"][:, q % BATCH, :], r_terms[:, b % 2, :], start=True, stop=True).then_inc(c["spread_done"].sem, 1)

            def heads(i, q, row):
                m = i * BODY + q
                if row == 0:
                    stack = c[f"stacked{q % 8 // 2}"]
                    pe.wait_ge(stack.sem, stack(i * 128 + (q // 8 + 1) * 64))
                pe.wait_ge(pair_read.sem, pair_read(m * 2 + row - 1))
                for kb in range(2):
                    bank = PAIR[row][:, kb, :].rearrange("p (a g e) -> p a g e", a=2, g=2)
                    at = row * S + kb * P
                    for g in range(2):
                        for part in range(2):
                            last = pe.matmul(bank[:, :, g, :], stacked[:, q % 8, g, at:at + P], k["w_heads"][:, part, :],
                                             start=(part == 0), stop=(part == 1))
                last.then_inc(c["proj_done"].sem, 1)

            def out_gate(i, q):
                m = i * BODY + q
                pe.wait_ge(c["gate_done"].sem, c["gate_done"](m))
                pe.matmul(GATE, k["w_gate"][:, 0, :], hi[:, q % 8, :], start=True, stop=False)
                pe.matmul(GATE, k["w_gate"][:, 0, :], lo[:, q % 8, :], start=False, stop=False)
                pe.matmul(GATE, k["w_gate"][:, 1, :], hi[:, q % 8, :], start=False, stop=True).then_inc(c["gate_mm_done"].sem, 1)

            def step(i, q, more):
                if more(NORM):
                    spread(i, q + NORM)
                if more(CENTER):
                    center(i, q + CENTER, Z, i * BODY + q + CENTER)
                heads(i, q, 0)
                if more(VARIANCE):
                    variance(i, q + VARIANCE)
                heads(i, q, 1)
                out_gate(i, q)

            for q in range(CENTER):
                center(0, q, AHEAD_Z[q % 2], q - 1)
                if q > 0:
                    variance(0, q - 1)
                if q >= CENTER - NORM:
                    spread(0, q - (CENTER - NORM))
            bodies_of(pe, step)

        @block.scalar
        def _(act):
            def square(i, q, bank):
                m = i * BODY + q
                act.wait_ge(c["z_done"].sem, c["z_done"](m + 1))
                act.wait_ge(c["xn_done"].sem, c["xn_done"](m - 15))
                act.activation(zs[:, q % 16, :], bank, ACT.Identity, bias=k["shift"][:])
                act.wait_ge(c["var_done"].sem, c["var_done"](m - 3))
                act.activation(sq[:, q % 4, :], bank, ACT.Square, bias=k["shift"][:]).then_inc(c["sq_done"].sem, 1)

            def root(i, b):
                batch = i * (BODY // BATCH) + b
                act.preload_act_table_set(LN_SET)
                act.wait_ge(c["var_done"].sem, c["var_done"](batch * BATCH + BATCH))
                act.activation(log_var[:], VAR, ACT.Ln, bias=k["unit"][0:2 * BATCH, 2:3]).then_inc(c["log_done"].sem, 1)
                act.wait_ge(c["log_done"].sem, c["log_done"](batch + 1))
                act.wait_ge(c["r_split"].sem, c["r_split"](batch))
                act.activation(r[:], log_var[:], ACT.Exp, scale=-0.5).then_inc(c["r_done"].sem, 1)

            def gate_pair(i, q, row):
                m = i * BODY + q
                slot = (2 * q + row) % 4
                act.wait_ge(c["proj_done"].sem, c["proj_done"](m * 2 + row + 1))
                act.wait_ge(c["lr_done"].sem, c["lr_done"](m * 2 + row - 3))
                act.activation(sig[:, slot, :].rearrange("p (b e) -> p b e", b=2), PAIR[row][:, :, 0:S],
                               ACT.Sigmoid, scale=k["largest"][:, 0:1]).then_inc(c["sig_done"].sem, 1)

            def step(i, q, more):
                m = i * BODY + q
                if more(CENTER):
                    square(i, q + CENTER, Z)
                gate_pair(i, q, 0)
                gate_pair(i, q, 1)
                act.wait_ge(c["gate_mm_done"].sem, c["gate_mm_done"](m + 1))
                stored = c[f"gate_out{q % 4 // 2}"]
                act.wait_ge(stored.sem, stored(i * 64 + q // 4 * 16))
                act.activation(gates[:, q % 4, :], GATE, ACT.Sigmoid, scale=k["largest"][:, 2:3]).then_inc(c["gate_done"].sem, 1)
                if more(VARIANCE) and (q + VARIANCE) % BATCH == BATCH - 1:
                    root(i, (q + VARIANCE) // BATCH)

            for q in range(CENTER):
                square(0, q, AHEAD_Z[q % 2])
                if q == BATCH:
                    root(0, 0)
            bodies_of(act, step)

        @block.vector
        def _(dve):
            def split_r(i, b):
                batch = i * (BODY // BATCH) + b
                parts, split = c["r_part"], c["r_split"]
                terms = [r_terms[R_PART * part:R_PART * part + 2 * BATCH, b % 2, :] for part in range(3)]
                dve.wait_ge(c["r_done"].sem, c["r_done"](batch + 1))
                dve.wait_ge(c["spread_done"].sem, c["spread_done"](batch * BATCH - BATCH))
                dve.tensor_copy(terms[0], r[:]).then_inc(parts.sem, 1)
                dve.wait_ge(parts.sem, parts(batch * 3 + 1))
                dve.tensor_tensor(r_rest[:], r[:], terms[0], ALU.subtract).then_inc(parts.sem, 1)
                dve.wait_ge(parts.sem, parts(batch * 3 + 2))
                dve.tensor_copy(r_mid[:], r_rest[:]).then_inc(parts.sem, 1)
                dve.wait_ge(parts.sem, parts(batch * 3 + 3))
                dve.tensor_copy(terms[1], r_mid[:])
                dve.tensor_tensor(terms[2], r_rest[:], r_mid[:], ALU.subtract).then_inc(split.sem, 1)
                dve.wait_ge(split.sem, split(batch + 1))

            def norm(i, q):
                m = i * BODY + q
                dve.wait_ge(c["spread_done"].sem, c["spread_done"](m + 1))
                dve.wait_ge(c["lo_done"].sem, c["lo_done"](m - 1))
                dve.tensor_tensor(xn[:, q % 2, :], zs[:, q % 16, :], R, ALU.mult).then_inc(c["xn_done"].sem, 1)
                dve.wait_ge(c["xn_done"].sem, c["xn_done"](m + 1))
                dve.wait_ge(c["gate_mm_done"].sem, c["gate_mm_done"](m - 7))
                dve.tensor_copy(hi[:, q % 8, :], xn[:, q % 2, :]).then_inc(c["hi_done"].sem, 1)
                dve.wait_ge(c["hi_done"].sem, c["hi_done"](m + 1))
                dve.tensor_tensor(lo[:, q % 8, :], xn[:, q % 2, :], hi[:, q % 8, :], ALU.subtract).then_inc(c["lo_done"].sem, 1)

            def left_and_right(i, q):
                m = i * BODY + q
                b = q // SCH
                if q % SCH == 0 and not masked:
                    dve.wait_ge(c[f"lr_out{b}"].sem, c[f"lr_out{b}"](i * 16 * SEG_PARTS))
                for row in range(ROWS):
                    factor = sig[:, (2 * q + row) % 4, :].rearrange("p (b n h) -> p b n h", b=2, h=HG)
                    dst = factor if masked else staged(b, q, row).rearrange("p b g l n h -> p b (g l n) h")
                    dve.wait_ge(c["sig_done"].sem, c["sig_done"](m * 2 + row + 1))
                    dve.scalar_tensor_tensor(dst, PAIR[row][:, :, S:CH].rearrange("p b (n h) -> p b n h", h=HG),
                                             k["largest"][:, 1:2], factor, ALU.mult, ALU.mult).then_inc(pair_read.sem, 1)

            def step(i, q, more):
                if more(NORM):
                    norm(i, q + NORM)
                if more(SPLIT) and (q + SPLIT) % BATCH == 0:
                    split_r(i, (q + SPLIT) // BATCH)
                left_and_right(i, q)

            dve.memset(r_terms[:], 0.0).then_inc(c["r_part"].sem, 1)
            dve.wait_ge(c["r_part"].sem, c["r_part"](1))
            c["r_part"].advance(1)
            dve.memset(r_terms[R_ONE:R_ONE + 1, :, :], 1.0).then_inc(c["r_part"].sem, 1)
            c["r_part"].advance(1)
            split_r(0, 0)
            for q in range(NORM):
                norm(0, q)
            bodies_of(dve, step)

        if masked:
            @block.gpsimd
            def _(pool):
                def pair(i, q, row):
                    m = i * BODY + q
                    b = q // SCH
                    if q % SCH == 0 and row == 0:
                        pool.wait_ge(c[f"lr_out{b}"].sem, c[f"lr_out{b}"](i * 16 * SEG_PARTS))
                    pool.wait_ge(c["pair_read"].sem, c["pair_read"](m * 2 + row + 1))
                    product = sig[:, (2 * q + row) % 4, :].rearrange("p (a n h) -> p a n h", a=4, h=HG)
                    by_g = k["mask"][:].rearrange("p b (g i) -> p (b g) i", g=2)
                    mk = by_g[:, :, bass.ds(m * ROWS + row, 1)].unsqueeze(3).to_broadcast([P, 4, P // HG, HG])
                    pool.tensor_tensor(staged(b, q, row).rearrange("p b g l n h -> p (b g) (l n) h"), product, mk,
                                       ALU.mult).then_inc(c["lr_done"].sem, 1)

                with pool.Fori(0, bodies) as i:
                    for q in range(BODY):
                        for row in range(ROWS):
                            pair(i, q, row)

    for s in range(4):
        c[f"x_in{s}"].advance(16 * NCH // 8)
        c[f"stacked{s}"].advance(64 * NCH // 8)
    for s in range(2):
        c[f"gate_out{s}"].advance(16 * NCH // 4)
        c[f"lr_out{s}"].advance(128 * bodies)
    batches = NCH // BATCH
    for name in ("log_done", "r_done", "r_split"):
        c[name].advance(batches)
    c["r_part"].advance(3 * batches)
    for name in ("z_done", "sq_done", "var_done", "spread_done", "xn_done", "hi_done", "lo_done", "gate_mm_done", "gate_done"):
        c[name].advance(NCH)
    for name in ("proj_done", "sig_done", "lr_done") + (("pair_read",) if masked else ()):
        c[name].advance(2 * NCH)


def project_plain(nc, n, HG, x, gate, left_right, c, k, ps):
    with ExitStack() as ctx:
        def sb(name, shape, dt=F32):
            return ctx.enter_context(nc.sbuf_tensor(f"{name}_{n}", shape, dt))

        xs, xn = sb("xs", [P, 8, CH]), sb("xn", [P, 4, CH])
        biased, product, gates = sb("biased", [P, 2, 4, P]), sb("product", [P, 2, 4, C]), sb("gates", [P, 4, CH])
        stage = sb("stage", [P, 2, 2, 2, 2, 16 // HG, SEG, HG])
        TILES, GATE = [ps[0][:, q, :] for q in range(2)], [ps[1][:, q, :] for q in range(2)]
        block = ctx.enter_context(nc.Block())
        bodies = NCH // BODY

        @block.sync
        def _(sp):
            def load(i, q):
                m = i * BODY + q
                sp.wait_ge(c["xn_done"].sem, c["xn_done"](m - 7))
                sp.dma_start(xs[:, q % 8, :], x[:, bass.ds(m * CH, CH)]).then_inc(c[f"x_in{q % 8}"].sem, 16)

            def store(i, q):
                m = i * BODY + q
                sp.wait_ge(c["gate_done"].sem, c["gate_done"](m + 1))
                sp.dma_start(gate[:, bass.ds(m * CH, CH)], gates[:, q % 4, :]).then_inc(c[f"gate_out{q % 4}"].sem, 16)
                if q % SCH == SCH - 1:
                    sp.wait_ge(c["lr_done"].sem, c["lr_done"](m + 1))
                    b = q // SCH
                    for part in range(SEG_PARTS):
                        store_part(sp, left_right, stage[:, b], i * 2 + b, HG, part, c[f"lr_out{b}"])

            for q in range(6):
                load(0, q)
            with sp.Fori(0, bodies - 1) as i:
                for q in range(BODY):
                    load(i, q + 6)
                    store(i, q)
            for q in range(BODY):
                if q + 6 < BODY:
                    load(bodies - 1, q + 6)
                store(bodies - 1, q)
            for s in range(4):
                sp.wait_ge(c[f"gate_out{s}"].sem, c[f"gate_out{s}"](16 * NCH // 4))
            for s in range(2):
                sp.wait_ge(c[f"lr_out{s}"].sem, c[f"lr_out{s}"](16 * 8 * bodies))

        @block.tensor
        def _(pe):
            with pe.Fori(0, bodies) as i:
                for q in range(BODY):
                    m = i * BODY + q
                    pe.wait_ge(c["xn_done"].sem, c["xn_done"](m + 1))
                    pe.wait_ge(c["masked"].sem, c["masked"](m - 1))
                    for t in range(4):
                        last = pe.matmul(TILES[q % 2][:, t * P:t * P + P], xn[:, q % 4, t * P:t * P + P],
                                         k["w_proj"][:, 0:P], start=True, stop=True)
                    last.then_inc(c["proj_done"].sem, 1)
                    pe.wait_ge(c["gate_done"].sem, c["gate_done"](m - 1))
                    pe.matmul(GATE[q % 2], k["w_proj"][:, CH:CH + P], xn[:, q % 4, :],
                              start=True, stop=True).then_inc(c["gate_mm_done"].sem, 1)

        @block.vector
        def _(dve):
            def affine(i, q):
                m = i * BODY + q
                load = c[f"x_in{q % 8}"]
                dve.wait_ge(load.sem, load(i * 32 + (q // 8 + 1) * 16))
                dve.wait_ge(c["gate_mm_done"].sem, c["gate_mm_done"](m - 3))
                dve.tensor_scalar(xn[:, q % 4, :], xs[:, q % 8, :], k["gn"][:, 6:7], k["gn"][:, 7:8],
                                  ALU.mult, ALU.add).then_inc(c["xn_done"].sem, 1)

            def multiply(i, q):
                m = i * BODY + q
                dve.wait_ge(c["proj_done"].sem, c["proj_done"](m + 1))
                dve.wait_ge(c["sig_done"].sem, c["sig_done"](m - 1))
                dve.tensor_tensor(biased[:, q % 2].rearrange("p a b -> p (a b)"), TILES[q % 2],
                                  k["mask"][:].rearrange("p a b -> p (a b)"), ALU.add).then_inc(c["masked"].sem, 1)
                dve.wait_ge(c["masked"].sem, c["masked"](m + 1))
                dve.wait_ge(c["lr_done"].sem, c["lr_done"](m - 1))
                dve.tensor_tensor(product[:, q % 2], biased[:, q % 2, :, 0:C], biased[:, q % 2, :, C:P],
                                  ALU.mult).then_inc(c["sig_done"].sem, 1)

            affine(0, 0)
            affine(0, 1)
            with dve.Fori(0, bodies - 1) as i:
                for q in range(BODY):
                    affine(i, q + 2)
                    multiply(i, q)
            for q in range(BODY):
                if q + 2 < BODY:
                    affine(bodies - 1, q + 2)
                multiply(bodies - 1, q)

        @block.scalar
        def _(act):
            with act.Fori(0, bodies) as i:
                for q in range(BODY):
                    m = i * BODY + q
                    b = q // SCH
                    if q % SCH == 0:
                        act.wait_ge(c[f"lr_out{b}"].sem, c[f"lr_out{b}"](i * 128))
                    act.wait_ge(c["sig_done"].sem, c["sig_done"](m + 1))
                    for row in range(ROWS):
                        at = q % SCH * ROWS + row
                        dst = stage[:, b, :, :, :, :, at, :].rearrange("p b g l n h -> p b (g l n) h")
                        last = act.activation(dst, product[:, q % 2, 2 * row:2 * row + 2, :].rearrange("p b (n h) -> p b n h", h=HG),
                                              ACT.Sigmoid)
                    last.then_inc(c["lr_done"].sem, 1)
                    act.wait_ge(c["gate_mm_done"].sem, c["gate_mm_done"](m + 1))
                    stored = c[f"gate_out{q % 4}"]
                    act.wait_ge(stored.sem, stored(i * 64 + q // 4 * 16))
                    act.activation(gates[:, q % 4, :], GATE[q % 2], ACT.Sigmoid,
                                   bias=k["vec"][:, V_GATE_B:V_GATE_B + 1]).then_inc(c["gate_done"].sem, 1)

    for s in range(8):
        c[f"x_in{s}"].advance(16 * NCH // 8)
    for s in range(4):
        c[f"gate_out{s}"].advance(16 * NCH // 4)
    for s in range(2):
        c[f"lr_out{s}"].advance(128 * bodies)
    for name in ("xn_done", "proj_done", "masked", "sig_done", "lr_done", "gate_mm_done", "gate_done"):
        c[name].advance(NCH)


def triangle(nc, n, turned, low, H, HG, left_right, O, c, k, ps):
    turns = H // HG // 2
    with ExitStack() as ctx:
        left = ctx.enter_context(nc.sbuf_tensor(f"left{n}", [P, 2, 2, S, HG], low))
        right = ctx.enter_context(nc.sbuf_tensor(f"right{n}", [P, 2, 2, S, HG], low))
        right_t = ctx.enter_context(nc.sbuf_tensor(f"right_t{n}", [P, 2, 2, S], F32)) if turned else None
        block = ctx.enter_context(nc.Block())

        def channel(t, s, h):
            return t * (2 * HG) + (s * HG + h)

        @block.sync
        def _(sp):
            with sp.Fori(0, turns) as t:
                for s in range(2):
                    sp.wait_ge(c["tri_done"].sem, c["tri_done"](channel(t, s, 0) - HG))
                    for lr, dst in ((0, left), (1, right)):
                        sp.dma_start(dst[:, s].rearrange("p b i h -> p (b i h)"),
                                     left_right[lr, bass.ds(t * 2 + s, 1)].rearrange("n k b s i h -> k (n b s i h)")
                                     ).then_inc(c[f"lr_in{s}"].sem, 16)

        @block.tensor
        def _(pe):
            def turn(t, s, h):
                ch = channel(t, s, h)
                pe.wait_ge(c["tr_copied"].sem, c["tr_copied"](ch - 1))
                for kb in range(2):
                    for jb in range(2):
                        at = kb * S + jb * P
                        last = pe.transpose(ps[2 + h % 2][:, 0, at:at + P],
                                            right[:, s, jb, kb * P:kb * P + P, h], k["ident"][:])
                last.then_inc(c["tr_done"].sem, 1)

            def contract(t, s, h):
                ch = channel(t, s, h)
                if turned:
                    pe.wait_ge(c["tr_copied"].sem, c["tr_copied"](ch + 1))
                pe.wait_ge(c["o_copied"].sem, c["o_copied"](ch - 3))
                for jb in range(2):
                    for kb in range(2):
                        stationary = (right_t[:, h % 2, kb, jb * P:jb * P + P] if turned
                                      else right[:, s, kb, jb * P:jb * P + P, h])
                        last = pe.matmul(ps[h % 4 // 2][:, h % 2, jb * S:jb * S + S], stationary,
                                         left[:, s, kb, :, h], start=(kb == 0), stop=(kb == 1))
                last.then_inc(c["tri_done"].sem, 1)

            with pe.Fori(0, turns) as t:
                for s in range(2):
                    load = c[f"lr_in{s}"]
                    pe.wait_ge(load.sem, load(t * 32 + 32))
                    if turned:
                        turn(t, s, 0)
                    for h in range(HG):
                        if turned and h + 1 < HG:
                            turn(t, s, h + 1)
                        contract(t, s, h)

        if turned:
            @block.vector
            def _(dve):
                with dve.Fori(0, turns) as t:
                    for s in range(2):
                        for h in range(HG):
                            ch = channel(t, s, h)
                            dve.wait_ge(c["tr_done"].sem, c["tr_done"](ch + 1))
                            dve.wait_ge(c["tri_done"].sem, c["tri_done"](ch - 1))
                            dve.tensor_copy(right_t[:, h % 2].rearrange("p b j -> p (b j)"),
                                            ps[2 + h % 2][:, 0, :]).then_inc(c["tr_copied"].sem, 1)

        @block.scalar
        def _(act):
            with act.Fori(0, turns) as t:
                for s in range(2):
                    for h in range(HG):
                        ch = channel(t, s, h)
                        act.wait_ge(c["tri_done"].sem, c["tri_done"](ch + 1))
                        dst = O[:].rearrange("p b i g h -> p b g i h")[:, :, :, :, bass.ds(ch, 1)].rearrange("p b g i h -> p b g (i h)")
                        act.activation(dst, ps[h % 4 // 2][:, h % 2, :].rearrange("p (b g i) -> p b g i", b=2, g=2),
                                       ACT.Copy).then_inc(c["o_copied"].sem, 1)

    for s in range(2):
        c[f"lr_in{s}"].advance(32 * turns)
    for name in ("tri_done", "o_copied") + (("tr_done", "tr_copied") if turned else ()):
        c[name].advance(H)


def output(nc, n, gate_first, H, O, x, gate, x_new, c, k, ps):
    counted = n < 3
    HH = 2 * H
    TOK = 4 * SEG
    STAT, CENTER, SCALE, TURN, GATED, OUTMM, OUTGATED = 14, 5, 4, 3, 2, 1 if gate_first else 2, 1
    LOAD_X, LOAD_G = 4, 6 if gate_first else 5
    RING = 4
    with ExitStack() as ctx:
        def sb(name, shape, dt=F32):
            return ctx.enter_context(nc.sbuf_tensor(f"out_{name}_{n}", shape, dt))

        xs, gs, xo = sb("xs", [P, RING, CH]), sb("gs", [P, RING, CH]), sb("xo", [P, RING, CH])
        centered = sb("centered", [P, RING, 2, 4, H]) if gate_first else None
        scaled = sb("scaled", [P, RING, 2, 4, H])
        if gate_first:
            wt, u = sb("wt", [P, RING, CH]), sb("u", [P, RING, CH])
        else:
            u, og = sb("u", [P, RING, CH]), sb("og", [P, RING, CH])
        bn = sb("bn", [P, 2, 2, 2 * SEG, 6])
        small = sb("small", [P, 4, TOK])
        mu, std, rs = sb("mu", [P, 2, 2, 2 * SEG]), sb("std", [P, 2, TOK]), sb("rs", [P, 2, 2, 2 * SEG])
        var = sb("var", [P, 2, TOK])
        TURNED, OUT = [ps[q // 2][0:HH, q % 2, :] for q in range(4)], [ps[2 + q // 2][:, q % 2, :] for q in range(4)]
        block = ctx.enter_context(nc.Block())
        bodies = NCH // BODY
        rows = O[:].rearrange("p b i g h -> p b (i g) h")

        def per_token(values, q):
            at = q % SCH * 2 * ROWS
            return values[:, q // SCH % 2, :, at:at + 2 * ROWS].unsqueeze(3).to_broadcast([P, 2, 2 * ROWS, H])

        def bodies_of(eng, step):
            with eng.Fori(0, bodies - 1) as i:
                for q in range(BODY):
                    step(i, q, lambda lead: True)
            for q in range(BODY):
                step(bodies - 1, q, lambda lead: q + lead < BODY)

        @block.sync
        def _(sp):
            def load_x(i, q):
                m = i * BODY + q
                free = c["out_mm_done"] if gate_first else c["x_new"]
                sp.wait_ge(free.sem, free(m - 3))
                sp.dma_start(xs[:, q % RING, :], x[:, bass.ds(m * CH, CH)]).then_inc(c[f"xc_in{q % RING}"].sem, 16)

            def load_g(i, q):
                m = i * BODY + q
                free = c["gated"] if gate_first else c["out_gated"]
                sp.wait_ge(free.sem, free(m - 3))
                sp.dma_start(gs[:, q % RING, :], gate[:, bass.ds(m * CH, CH)]).then_inc(c[f"gc_in{q % RING}"].sem, 16)

            def step(i, q, more):
                if more(LOAD_G):
                    load_g(i, q + LOAD_G)
                if more(LOAD_X):
                    load_x(i, q + LOAD_X)
                m = i * BODY + q
                sp.wait_ge(c["x_new"].sem, c["x_new"](m + 1))
                sp.dma_start(x_new[:, bass.ds(m * CH, CH)], xo[:, q % RING, :]).then_inc(c[f"x_out{q % RING}"].sem, 16)

            for q in range(4):
                load_g(0, q)
                load_x(0, q)
            for q in range(4, LOAD_G):
                load_g(0, q)
            bodies_of(sp, step)
            for s in range(RING):
                sp.wait_ge(c[f"x_out{s}"].sem, c[f"x_out{s}"](16 * NCH // RING))

        @block.vector
        def _(dve):
            def statistics(i, q):
                b = q // SCH % 2
                for jb in range(2):
                    for t in range(2 * ROWS):
                        at = q % SCH * 2 * ROWS + t
                        last = dve.bn_stats(bn[:, b, jb, at, :],
                                            rows[:, jb, bass.ds(i * (BODY * 2 * ROWS) + q * 2 * ROWS + t, 1), :].rearrange("p a h -> p (a h)"))
                last.then_inc(c["ln_stat"].sem, 1)

            def moments(i, b):
                batch = i * (BODY // SCH) + b
                v = bn[:, b % 2].rearrange("p b t s -> p (b t) s")
                col = [v[:, :, q:q + 1].rearrange("p t s -> p (t s)") for q in range(6)]
                dve.wait_ge(c["ln_stat"].sem, c["ln_stat"](batch * SCH + SCH))
                dve.tensor_tensor(small[:, 0], col[1], col[4], ALU.add)
                dve.tensor_tensor(small[:, 1], col[1], col[4], ALU.subtract)
                dve.tensor_tensor(small[:, 2], col[2], col[5], ALU.add).then_inc(c["ln_small"].sem, 1)
                dve.wait_ge(c["ln_small"].sem, c["ln_small"](batch * 2 + 1))
                if gate_first:
                    dve.wait_ge(c["centered"].sem, c["centered"](batch * SCH - SCH))
                    dve.tensor_scalar(mu[:, b % 2].rearrange("p b t -> p (b t)"), small[:, 0], 0.5, None, ALU.mult)
                dve.scalar_tensor_tensor(small[:, 3], small[:, 1], 0.25, small[:, 1], ALU.mult, ALU.mult).then_inc(c["ln_small"].sem, 1)
                dve.wait_ge(c["ln_small"].sem, c["ln_small"](batch * 2 + 2))
                dve.scalar_tensor_tensor(var[:, b % 2], small[:, 2], 1.0 / H, small[:, 3], ALU.mult, ALU.add).then_inc(c["ln_var"].sem, 1)

            def invert(i, b):
                batch = i * (BODY // SCH) + b
                dve.wait_ge(c["ln_root"].sem, c["ln_root"](batch + 1))
                dve.wait_ge(c["scaled"].sem, c["scaled"](batch * SCH - SCH))
                dve.reciprocal(rs[:, b % 2].rearrange("p b t -> p (b t)"), std[:, b % 2]).then_inc(c["ln_scale"].sem, 1)
                dve.wait_ge(c["ln_scale"].sem, c["ln_scale"](batch + 1))

            def scale(i, q):
                m = i * BODY + q
                dve.wait_ge(c["centered"].sem, c["centered"](m + 1))
                dve.wait_ge(c["wt_done"].sem, c["wt_done"](m - 3))
                dve.tensor_tensor(scaled[:, q % RING], centered[:, q % RING], per_token(rs, q),
                                  ALU.mult).then_inc(c["scaled"].sem, 1)

            def gate_output(i, q):
                m = i * BODY + q
                dve.wait_ge(c["out_mm_done"].sem, c["out_mm_done"](m + 1))
                load = c[f"gc_in{q % RING}"]
                dve.wait_ge(load.sem, load(i * 64 + (q // RING + 1) * 16))
                dve.wait_ge(c["x_new"].sem, c["x_new"](m - 3))
                dve.scalar_tensor_tensor(og[:, q % RING], OUT[q % 4], k["out_bias"][:], gs[:, q % RING, :],
                                         ALU.add, ALU.mult).then_inc(c["out_gated"].sem, 1)

            def count(i, q):
                m = i * BODY + q
                dve.wait_ge(c["x_new"].sem, c["x_new"](m + 1))
                dve.bn_stats(k["gn_stats"][:, bass.ds(m, 1), :].rearrange("p a b -> p (a b)"), xo[:, q % RING, :]).then_inc(c["counted"].sem, 1)

            def step(i, q, more):
                if more(STAT):
                    statistics(i, q + STAT)
                    if (q + STAT) % SCH == SCH - 1:
                        moments(i, (q + STAT) // SCH)
                if more(CENTER) and (q + CENTER) % SCH == 0:
                    invert(i, (q + CENTER) // SCH)
                if gate_first and more(SCALE):
                    scale(i, q + SCALE)
                if not gate_first and more(OUTGATED):
                    gate_output(i, q + OUTGATED)
                if counted:
                    count(i, q)

            if HH < P:
                dve.memset(u[:], 0.0).then_inc(c["u_cleared"].sem, 1)
            for q in range(SCH):
                statistics(0, q)
            moments(0, 0)
            for q in range(STAT - SCH):
                statistics(0, q + SCH)
                if q == 0:
                    invert(0, 0)
                if gate_first and q < SCALE:
                    scale(0, q)
            if not gate_first:
                for q in range(OUTGATED):
                    gate_output(0, q)
            bodies_of(dve, step)

        @block.gpsimd
        def _(pool):
            def center(i, q):
                m = i * BODY + q
                if q % SCH == 0:
                    batch = i * (BODY // SCH) + q // SCH
                    pool.wait_ge(c["ln_var"].sem, c["ln_var"](batch + 1))
                pool.wait_ge(c["scaled"].sem, c["scaled"](m - 3))
                pool.tensor_tensor(centered[:, q % RING], rows[:, :, bass.ds(m * 2 * ROWS, 2 * ROWS), :], per_token(mu, q),
                                   ALU.subtract).then_inc(c["centered"].sem, 1)

            def scale(i, q):
                m = i * BODY + q
                if q % SCH == 0:
                    batch = i * (BODY // SCH) + q // SCH
                    pool.wait_ge(c["ln_scale"].sem, c["ln_scale"](batch + 1))
                pool.wait_ge(c["wt_done"].sem, c["wt_done"](m - 3))
                pool.tensor_tensor(scaled[:, q % RING], rows[:, :, bass.ds(m * 2 * ROWS, 2 * ROWS), :], per_token(rs, q),
                                   ALU.mult).then_inc(c["scaled"].sem, 1)

            def gate_input(i, q):
                m = i * BODY + q
                pool.wait_ge(c["wt_copied"].sem, c["wt_copied"](m + 1))
                load = c[f"gc_in{q % RING}"]
                pool.wait_ge(load.sem, load(i * 64 + (q // RING + 1) * 16))
                pool.wait_ge(c["out_mm_done"].sem, c["out_mm_done"](m - 3))
                pool.tensor_tensor(u[:, q % RING], wt[:, q % RING], gs[:, q % RING, :], ALU.mult).then_inc(c["gated"].sem, 1)

            def add_residual(i, q):
                m = i * BODY + q
                pool.wait_ge(c["out_gated"].sem, c["out_gated"](m + 1))
                load, stored = c[f"xc_in{q % RING}"], c[f"x_out{q % RING}"]
                pool.wait_ge(load.sem, load(i * 64 + (q // RING + 1) * 16))
                pool.wait_ge(stored.sem, stored(i * 64 + q // RING * 16))
                if counted:
                    pool.wait_ge(c["counted"].sem, c["counted"](m - 3))
                pool.tensor_tensor(xo[:, q % RING, :], og[:, q % RING], xs[:, q % RING, :], ALU.add).then_inc(c["x_new"].sem, 1)

            def step(i, q, more):
                if gate_first and more(CENTER):
                    center(i, q + CENTER)
                if not gate_first and more(SCALE):
                    scale(i, q + SCALE)
                if gate_first:
                    if more(GATED):
                        gate_input(i, q + GATED)
                else:
                    add_residual(i, q)

            for q in range(CENTER if gate_first else SCALE):
                (center if gate_first else scale)(0, q)
            if gate_first:
                for q in range(GATED):
                    gate_input(0, q)
            bodies_of(pool, step)

        @block.tensor
        def _(pe):
            def turn(i, q):
                m = i * BODY + q
                pe.wait_ge(c["scaled"].sem, c["scaled"](m + 1))
                pe.wait_ge(c["wt_copied"].sem, c["wt_copied"](m - 3))
                for row in range(ROWS):
                    for jb in range(2):
                        at = row * S + jb * P
                        last = pe.transpose(TURNED[q % 4][:, at:at + P],
                                            scaled[:, q % RING, jb, 2 * row:2 * row + 2, :].rearrange("p g h -> p (g h)"), k["ident"][:])
                last.then_inc(c["wt_done"].sem, 1)

            def multiply(i, q):
                m = i * BODY + q
                ready = c["gated"] if gate_first else c["wt_copied"]
                pe.wait_ge(ready.sem, ready(m + 1))
                bank_free = c["x_new"] if gate_first else c["out_gated"]
                pe.wait_ge(bank_free.sem, bank_free(m - 3))
                if gate_first:
                    pe.matmul(OUT[q % 4], k["w_out"][:], u[:, q % RING], start=True, stop=False)
                    load = c[f"xc_in{q % RING}"]
                    pe.wait_ge(load.sem, load(i * 64 + (q // RING + 1) * 16))
                    mm = pe.matmul(OUT[q % 4], k["ident"][:], xs[:, q % RING, :], start=False, stop=True)
                else:
                    mm = pe.matmul(OUT[q % 4], k["w_out"][:], u[:, q % RING], start=True, stop=True)
                mm.then_inc(c["out_mm_done"].sem, 1)

            def step(i, q, more):
                if more(TURN):
                    turn(i, q + TURN)
                if more(OUTMM):
                    multiply(i, q + OUTMM)

            for q in range(TURN):
                turn(0, q)
            for q in range(OUTMM):
                multiply(0, q)
            bodies_of(pe, step)

        @block.scalar
        def _(act):
            def copy(i, q):
                m = i * BODY + q
                act.wait_ge(c["wt_done"].sem, c["wt_done"](m + 1))
                free = c["gated"] if gate_first else c["out_mm_done"]
                act.wait_ge(free.sem, free(m - 3))
                if gate_first:
                    ins = act.activation(wt[:, q % RING], TURNED[q % 4], ACT.Identity, scale=k["vec"][:, V_ON_G:V_ON_G + 1],
                                         bias=k["vec"][:, V_ON_B:V_ON_B + 1])
                else:
                    ins = act.activation(u[0:HH, q % RING], TURNED[q % 4], ACT.Copy)
                ins.then_inc(c["wt_copied"].sem, 1)

            def root(i, b):
                batch = i * (BODY // SCH) + b
                act.wait_ge(c["ln_var"].sem, c["ln_var"](batch + 1))
                act.wait_ge(c["ln_scale"].sem, c["ln_scale"](batch - 1))
                act.activation(std[:, b % 2], var[:, b % 2], ACT.Sqrt, bias=k["unit"][:, 2:3]).then_inc(c["ln_root"].sem, 1)

            def step(i, q, more):
                if more(TURN):
                    copy(i, q + TURN)
                if gate_first:
                    m = i * BODY + q
                    act.wait_ge(c["out_mm_done"].sem, c["out_mm_done"](m + 1))
                    stored = c[f"x_out{q % RING}"]
                    act.wait_ge(stored.sem, stored(i * 64 + q // RING * 16))
                    act.wait_ge(c["counted"].sem, c["counted"](m - 3))
                    act.activation(xo[:, q % RING, :], OUT[q % 4], ACT.Copy).then_inc(c["x_new"].sem, 1)
                if more(STAT) and (q + STAT) % SCH == SCH - 1:
                    root(i, (q + STAT) // SCH)

            root(0, 0)
            if HH < P:
                act.wait_ge(c["u_cleared"].sem, c["u_cleared"](1))
            for q in range(TURN):
                copy(0, q)
            bodies_of(act, step)

    for s in range(RING):
        for name in ("xc_in", "gc_in", "x_out"):
            c[f"{name}{s}"].advance(16 * NCH // RING)
    if HH < P:
        c["u_cleared"].advance(1)
    batches = NCH // SCH
    for name in ("ln_var", "ln_root", "ln_scale"):
        c[name].advance(batches)
    c["ln_small"].advance(2 * batches)
    for name in ("ln_stat", "scaled", "wt_done", "wt_copied", "out_mm_done", "x_new",
                 *(("centered", "gated") if gate_first else ("out_gated",))) + (("counted",) if counted else ()):
        c[name].advance(NCH)


def constants():
    basis = np.zeros((C, C), np.float32)
    for m in range(C - 1):
        basis[:m + 1, m] = 1 / np.sqrt((m + 1) * (m + 2))
        basis[m + 1, m] = -(m + 1) / np.sqrt((m + 1) * (m + 2))
    live = (np.arange(P) % C != C - 1)
    group = np.arange(P) % C // 2
    var_w = np.zeros((P, 4 * BATCH - 2), np.float32)
    spread = np.zeros((P, BATCH, P), np.float32)
    for g in range(2):
        half = slice(g * C, g * C + C)
        var_w[half, 2 * BATCH - 2 + g] = live[half] / C
        for q in range(BATCH):
            for part in range(3):
                spread[R_PART * part + 2 * q + g, q, half] = live[half]
    spread[R_ONE] = ~live
    unit = np.zeros((P, 3), np.float32)
    unit[:, 0] = ~live
    unit[:, 1] = np.where(live, EPS, 1)
    unit[:, 2] = EPS
    h_center = {}
    for n, H in ((2, 16), (3, C)):
        h_center[f"h_center{n}"] = np.zeros((P, P), np.float32)
        h_center[f"h_center{n}"][:2 * H, :2 * H] = np.kron(np.eye(2), np.eye(H) - 1 / H)
    last_row = np.zeros((2, P), np.float32)
    last_row[0, C - 1] = last_row[1, P - 1] = 1
    return {
        **h_center, "basis": np.kron(np.eye(2), basis), "var_w": var_w, "spread": spread.reshape(P, BATCH * P), "ident": np.eye(P),
        "pool_w": (group[:, None] == group[None, :]) / 4, "last_row": last_row, "unit": unit, "one": np.ones((1, P)),
    }


def twice(w):
    out = np.zeros((2, w.shape[0], 2, w.shape[1]), np.float32)
    for g in range(2):
        out[g, :, g, :] = w
    return out.reshape(2 * w.shape[0], 2 * w.shape[1])


def layouts(inputs):
    v = {name: np.asarray(value) for name, value in inputs.items()}
    x = v["x"].reshape(2, HALF * S, C).transpose(0, 2, 1).reshape(P, HALF * S)
    arrays = {"x": x}
    arrays.update(constants())

    columns = {"LN_G": V_LN_G, "LN_B": V_LN_B, "ON_G": V_ON_G, "ON_B": V_ON_B, "GATE_B": V_GATE_B, "OUT_B": V_OUT_B}

    def vectors(**by_column):
        out = np.zeros((P, NVEC), np.float32)
        for name, w in by_column.items():
            w = np.concatenate([w, w])
            out[:len(w), columns[name]] = w
        return out

    def add(n, gates, projections, out_gate, w_out, vec, gate_bias=None, proj_bias=None, out_gate_bias=None):
        w = [twice(np.concatenate(part, axis=1)) for part in (gates, projections)] + [twice(out_gate)]
        arrays[f"w_proj{n}"] = np.concatenate(w, axis=1)
        rows = np.zeros((2, 640), np.float32)
        if gate_bias is not None:
            for at, bias in ((0, np.concatenate(gate_bias)), (256, np.concatenate(proj_bias)), (512, out_gate_bias)):
                for g in range(2):
                    rows[g, at + g * len(bias):at + (g + 1) * len(bias)] = bias
        arrays[f"b_rows{n}"] = rows
        arrays[f"w_out{n}"] = twice(w_out)
        arrays[f"vec{n}"] = vec

    l0 = {q: v["L0_conv_" + q] for q in ("norm_g", "norm_b", "Wl", "Wr", "Wlg", "Wrg", "Wog", "out_norm_g", "out_norm_b", "Wout")}
    add(0, (l0["Wlg"].T, l0["Wrg"].T), (l0["Wl"].T, l0["Wr"].T), l0["Wog"].T, l0["Wout"].T,
        vectors(LN_G=l0["norm_g"], LN_B=l0["norm_b"], ON_G=l0["out_norm_g"], ON_B=l0["out_norm_b"]))
    arrays["mask0"] = v["L0_conv_mask"].reshape(S, S)
    l1 = {q: v["L1_conv_" + q] for q in ("norm_w", "norm_b", "w_left", "w_right", "w_lgate", "w_rgate", "w_ogate", "onorm_w", "onorm_b", "w_out")}
    add(1, (l1["w_lgate"].T, l1["w_rgate"].T), (l1["w_left"].T, l1["w_right"].T), l1["w_ogate"].T, l1["w_out"].T,
        vectors(LN_G=l1["norm_w"], LN_B=l1["norm_b"], ON_G=l1["onorm_w"], ON_B=l1["onorm_b"]))
    arrays["mask1"] = v["L1_conv_mask"].reshape(S, S)
    l2 = {q: v["L2_conv_" + q] for q in ("Wa1", "ba1", "Wa2", "ba2", "Wb1", "bb1", "Wb2", "bb2", "ln2_g", "ln2_b", "Wg", "bg", "Wz", "bz")}
    w = np.zeros((P, 640), np.float32)
    for half, parts in enumerate((("Wa1", "Wb1"), ("Wa2", "Wb2"))):
        w[:, half * C:half * C + C] = twice(np.concatenate([l2[q] for q in parts], axis=1))
    w[:, 512:640] = twice(l2["Wg"])
    arrays["w_proj2"] = w
    rows = np.zeros((2, 640), np.float32)
    tile = np.concatenate([np.concatenate([l2[q] for q in parts] * 2) for parts in (("ba1", "bb1"), ("ba2", "bb2"))])
    rows[0, 0:512] = np.concatenate([tile] * 4)
    arrays["b_rows2"] = rows
    w_out = np.zeros((P, P), np.float32)
    w_out[:32] = twice(l2["Wz"])
    arrays["w_out2"] = w_out
    arrays["vec2"] = vectors(ON_G=l2["ln2_g"], ON_B=l2["ln2_b"], GATE_B=l2["bg"], OUT_B=l2["bz"])
    l3 = {q: v["L3_conv_" + q] for q in ("ln_in_w", "ln_in_b", "Wga", "bga", "Wla", "bla", "Wgb", "bgb", "Wlb", "blb", "ln_o_w", "ln_o_b", "Wgo", "bgo", "Wlo", "blo")}
    add(3, (l3["Wga"], l3["Wgb"]), (l3["Wla"], l3["Wlb"]), l3["Wgo"], l3["Wlo"],
        vectors(LN_G=l3["ln_in_w"], LN_B=l3["ln_in_b"], ON_G=l3["ln_o_w"], ON_B=l3["ln_o_b"], OUT_B=l3["blo"]),
        (l3["bga"], l3["bgb"]), (l3["bla"], l3["blb"]), l3["bgo"])
    return {name: np.ascontiguousarray(value, dtype=np.float32) for name, value in arrays.items()}


def scratch(nc):
    out = {}
    for name in ("x_dram0", "x_dram1", "gate"):
        out[name] = nc.dram_tensor(name, [P, HALF * S], F32, kind="Internal").ap()
    for n, (groups, per, dt) in enumerate(((8, 8, F32), (4, 16, BF16), (2, 8, F32), (8, 8, F32))):
        out[f"left_right{n}"] = nc.dram_tensor(f"left_right{n}", [2, groups, P, 2, S // SEG, SEG, per], dt, kind="Internal").ap()
    return out


def kernel(**inputs):
    import concourse.bacc as bacc
    from concourse.bass_utils import run_bass_kernel_spmd

    nc = bacc.Bacc("TRN2", target_bir_lowering=False, num_devices=1)
    arrays = layouts(inputs)
    a = {name: nc.dram_tensor(f"in_{name}", list(v.shape), F32, kind="ExternalInput").ap() for name, v in arrays.items()}
    a.update(scratch(nc))
    out = nc.dram_tensor("out", [P, HALF * S], F32, kind="ExternalOutput").ap()
    build(nc, a, out)
    r = run_bass_kernel_spmd(nc, [{f"in_{name}": v for name, v in arrays.items()}], core_ids=[0])
    y = np.asarray(r.results[0]["out"])
    return y.reshape(2, C, HALF * S).transpose(0, 2, 1).reshape(1, S, S, C)
```

```python
from contextlib import ExitStack

import numpy as np

import concourse.bass as bass
from concourse import mybir

F32 = mybir.dt.float32
BF16 = mybir.dt.bfloat16
F16 = mybir.dt.float16
ALU = mybir.AluOpType
ACT = mybir.ActivationFunctionType
AXIS = mybir.AxisListType

P = 128
S = 256
C = 64
HALF = S // 2
CH = 512
NCH = HALF * S // CH
ROWS = CH // S
SEG = 16
SCH = SEG // ROWS
BODY = 2 * SCH
BATCH = 8
R_PART, R_ONE = 32, 96
EPS = 1e-5
FIRST = 16
LN_SET = "natural_log_exp_and_others"

V_LN_G, V_LN_B, V_ON_G, V_ON_B, V_GATE_B, V_OUT_B, NVEC = range(7)


class Counter:

    def __init__(self, handle, base):
        self.sem, self.base = handle, base

    def __call__(self, n):
        return n + self.base

    def advance(self, n):
        self.base += n


def build(nc, a, out):
    with ExitStack() as ctx:
        def sb(name, shape, dt=F32):
            return ctx.enter_context(nc.sbuf_tensor(name, shape, dt))

        def counter(name, base=FIRST):
            return Counter(ctx.enter_context(nc.semaphore(name)), base)

        k = {
            "basis": sb("basis", [P, P]), "var_w": sb("var_w", [P, 4 * BATCH - 2]), "ident": sb("ident", [P, P]),
            "pool_w": sb("pool_w", [P, P]), "last_row": sb("last_row", [2, P]), "unit": sb("unit", [P, 3]),
            "gn": sb("gn", [P, 12]), "gn_stats": sb("gn_stats", [P, NCH, 6]),
            "vec": sb("vec", [P, NVEC]), "center": sb("center", [P, P]), "shift": sb("shift", [P, 1]),
            "w_out": sb("w_out", [P, P]),
            "out_bias": sb("out_bias", [P, 1]), "one": sb("one", [1, P]),
            "mask": sb("mask", [P, 2, S]),
        }
        ps = [ctx.enter_context(nc.psum_tensor(f"ps{n}", [P, 2, 512], F32)) for n in range(4)]
        c = {n: counter(n) for n in (
            "fold_vec", "fold_mm", "fold_act", "stat_done", "z_done", "sq_done", "var_done", "log_done", "r_done", "r_part", "r_split", "spread_done",
            "xn_done", "hi_done", "lo_done", "proj_done", "gate_mm_done", "sig_done", "gate_done", "masked", "lr_done", "pair_read",
            "tr_done", "tr_copied", "tri_done", "o_copied",
            "ln_stat", "ln_small", "ln_var", "ln_root", "ln_scale", "centered", "scaled", "wt_done", "wt_copied", "gated",
            "out_mm_done", "u_cleared", "out_gated", "x_new", "counted")}
        for n, ring in (("const_in", 1), ("x_in", 8), ("stacked", 4), ("lr_out", 2), ("gate_out", 4), ("lr_in", 2),
                        ("xc_in", 4), ("gc_in", 4), ("x_out", 4)):
            for i in range(ring):
                c[f"{n}{i}"] = counter(f"{n}{i}", 16)
        start_counters(nc, c, k, a)
        first_statistics(nc, a, c, k)
        x = a["x"]
        for n, kind in enumerate(("masked", "masked_bf16", "plain", "normed")):
            x_new = out if n == 3 else a[f"x_dram{n % 2}"]
            layer(nc, n, kind, a, x, x_new, c, k, ps)
            x = x_new


def start_counters(nc, c, k, a):
    with nc.Block() as block:
        @block.sync
        def _(sp):
            for name, counter in c.items():
                sp.sem_inc(counter.sem, counter.base)


def first_statistics(nc, a, c, k):
    x, lasting = a["x"], ("basis", "var_w", "ident", "pool_w", "last_row", "unit", "one")
    wide = 4 * CH
    turns = HALF * S // wide
    with ExitStack() as ctx:
        xin = ctx.enter_context(nc.sbuf_tensor("xin", [P, 4, wide], F32))
        block = ctx.enter_context(nc.Block())

        @block.sync
        def _(sp):
            with sp.Fori(0, turns // 4) as t:
                for s in range(4):
                    sp.wait_ge(c["stat_done"].sem, c["stat_done"](t * 4 + s - 3))
                    sp.dma_start(xin[:, s, :], x[:, bass.ds((t * 4 + s) * wide, wide)]).then_inc(c[f"xc_in{s}"].sem, 16)
            for name in lasting:
                sp.dma_start(k[name][:], a[name]).then_inc(c["const_in0"].sem, 16)
            sp.wait_ge(c["const_in0"].sem, c["const_in0"](16 * len(lasting)))

        @block.vector
        def _(dve):
            with dve.Fori(0, turns // 4) as t:
                for s in range(4):
                    load = c[f"xc_in{s}"]
                    dve.wait_ge(load.sem, load(t * 16 + 16))
                    for q in range(4):
                        last = dve.bn_stats(k["gn_stats"][:, bass.ds(t * 16 + s * 4 + q, 1), :].rearrange("p a b -> p (a b)"),
                                            xin[:, s, q * CH:(q + 1) * CH])
                    last.then_inc(c["stat_done"].sem, 1)
    for s in range(4):
        c[f"xc_in{s}"].advance(16 * turns // 4)
    c["stat_done"].advance(turns)
    c["const_in0"].advance(16 * len(lasting))


def layer(nc, n, kind, a, x, x_new, c, k, ps):
    normed_in = kind != "plain"
    masked = kind in ("masked", "masked_bf16")
    low = BF16 if kind == "masked_bf16" else F32
    H = 16 if kind == "plain" else C
    HG = 16 if low == BF16 else 8
    left_right = a[f"left_right{n}"]
    with ExitStack() as ctx:
        shapes = ({"w_heads": ([P, 2, S], F16), "w_gate": ([P, 2, P], F16), "largest": ([P, 3], F32), "spread": ([P, BATCH, P], BF16)}
                  if normed_in else {"w_proj": ([P, 640], F32)})
        w = {**k, **{name: ctx.enter_context(nc.sbuf_tensor(f"{name}{n}", *shape)) for name, shape in shapes.items()}}
        if normed_in:
            project(nc, n, kind, low, HG, x, a, left_right, c, w, ps)
        else:
            with ExitStack() as fold_ctx, nc.Block() as block:
                fold = Fold(nc, fold_ctx, n, kind, a, c, w, ps)
                block.sync(fold.load)

                @block.tensor
                def _(pe):
                    fold.multiply_statistics(pe)
                    fold.multiply_bias(pe)
                    fold.center_output(pe)

                block.scalar(fold.root)

                @block.vector
                def _(dve):
                    fold.scale_and_shift(dve)
                    fold.plain_weights(dve)
                    fold.output_weights(dve)
            fold.finish()
            project_plain(nc, n, HG, x, a["gate"], left_right, c, w, ps)
    with ExitStack() as ctx:
        O = ctx.enter_context(nc.sbuf_tensor(f"O{n}", [P, 2, HALF, 2, H], low))
        triangle(nc, n, not masked, low, H, HG, left_right, O, c, k, ps)
        output(nc, n, masked, H, O, x, a["gate"], x_new, c, k, ps)


class Fold:

    def __init__(self, nc, ctx, n, kind, a, c, k, ps):
        self.normed_in, self.masked = kind != "plain", kind in ("masked", "masked_bf16")
        shapes = [("w_raw", [P, 640]), ("b_rows", [2, 640])]
        if self.normed_in:
            shapes += [("w_scaled", [P, 640]), ("ln_sel", [P, P]), ("w_both", [P, 2, P]), ("size", [P, 3]),
                       ("size_t", [3, 1]), ("size_diag", [3, 3]), ("ones3", [3, P]), ("inverse", [P, 3])]
        shapes += [("mask_in", [P, 2, S])] if self.masked else [("h_center", [P, P])]
        self.k = k = {**k, **{name: ctx.enter_context(nc.sbuf_tensor(f"{name}_{n}", shape, F32)) for name, shape in shapes}}
        self.loads = [(k["vec"][:], a[f"vec{n}"]), (k["w_raw"][:], a[f"w_proj{n}"]), (k["b_rows"][:], a[f"b_rows{n}"]),
                      (k["w_out"][:], a[f"w_out{n}"])]
        if self.masked:
            self.loads += [(k["mask_in"][:], a[f"mask{n}"].rearrange("(b p) k -> p b k", p=P))]
        else:
            self.loads += [(k["h_center"][:], a[f"h_center{n}"])]
        if self.normed_in:
            self.loads += [(k["spread_in"], a["spread"])]
        (self.mean, self.var, self.group_mean, self.off, self.power, self.std, self.scale,
         self.shift) = (k["gn"][:, q:q + 1] for q in range(8))
        self.mm, self.done, self.rooted, self.loaded = c["fold_mm"], c["fold_vec"], c["fold_act"], c["const_in0"]
        self.out_rows = P if self.normed_in else 32
        self.mm_count, self.steps = 0, 0
        self.weight_steps = 30 if self.normed_in else 8
        self.all_steps = self.weight_steps + (1 if self.masked else 3)
        self.P_MEAN, self.P_VAR, self.P_SHIFT = ps[0][:, 0, :], ps[0][:, 1, :], ps[1][:, 0, :]
        self.P_PROJ, self.P_GATE, self.P_TURN = ps[2][:, 0, :], ps[2][:, 1, :], ps[3][:, 0, :]
        self.P_BIAS, self.P_CENTER, self.P_SIZE, self.P_LARGEST = (ps[3][:, 1, at:at + w] for at, w in ((0, 1), (P, P), (2 * P, P), (3 * P, 3)))

    def load(self, sp):
        for dst, src in self.loads:
            sp.dma_start(dst, src).then_inc(self.loaded.sem, 16)

    def counted(self, ins):
        self.mm_count += 1
        ins.then_inc(self.mm.sem, 1)

    def step(self, dve, ins):
        self.steps += 1
        ins.then_inc(self.done.sem, 1)
        dve.wait_ge(self.done.sem, self.done(self.steps))


    def multiply_statistics(self, pe):
        k = self.k
        pe.wait_ge(self.done.sem, self.done(1))
        self.counted(pe.matmul(self.P_MEAN[:, 0:1], k["pool_w"][:], self.mean, start=True, stop=True))
        pe.wait_ge(self.done.sem, self.done(4))
        self.counted(pe.matmul(self.P_VAR[:, 0:1], k["pool_w"][:], self.power, start=True, stop=True))
        if self.normed_in:
            pe.wait_ge(self.done.sem, self.done(6))
            self.counted(pe.matmul(self.P_SHIFT[:, 0:1], k["basis"][:], self.shift, start=True, stop=True))

    def multiply_bias(self, pe):
        k = self.k
        pe.wait_ge(self.loaded.sem, self.loaded(16 * len(self.loads)))
        if self.masked:
            for kb in range(2):
                for ib in range(2):
                    at = kb * S + ib * P
                    last = pe.transpose(self.P_TURN[:, at:at + P], k["mask_in"][:, ib, kb * P:kb * P + P], k["ident"][:])
        else:
            last = pe.matmul(self.P_BIAS, k["w_out"][0:self.out_rows, :], k["vec"][0:self.out_rows, V_ON_B:V_ON_B + 1],
                             start=True, stop=True)
        self.counted(last)
        if not self.normed_in:
            self.counted(pe.matmul(self.P_PROJ, k["one"][:], k["b_rows"][0:1, 0:CH], start=True, stop=True))

    def multiply_weights(self, pe):
        k = self.k
        pe.wait_ge(self.done.sem, self.done(12))
        for lo, hi, bank in ((0, 512, self.P_PROJ), (512, 640, self.P_GATE)):
            w = hi - lo
            pe.matmul(bank[:, 0:w], k["basis"][:], k["w_scaled"][:, lo:hi], start=True, stop=False)
            pe.matmul(bank[:, 0:w], k["ln_sel"][:], k["w_raw"][:, lo:hi], start=False, stop=False)
            last = pe.matmul(bank[:, 0:w], k["last_row"][:], k["b_rows"][:, lo:hi], start=False, stop=True)
        self.counted(last)

    def turn_sizes(self, pe):
        pe.wait_ge(self.done.sem, self.done(17))
        self.counted(pe.transpose(self.P_SIZE[0:3, :], self.k["size"][:], self.k["ident"][:]))

    def spread_sizes(self, pe):
        pe.wait_ge(self.done.sem, self.done(19))
        self.counted(pe.matmul(self.P_LARGEST, self.k["ones3"][:], self.k["size_diag"][:], start=True, stop=True))

    def center_output(self, pe):
        if not self.masked:
            pe.wait_ge(self.done.sem, self.done(self.weight_steps + 2))
            self.counted(pe.matmul(self.P_CENTER, self.k["h_center"][:], self.k["w_out"][:], start=True, stop=True))


    def root(self, act):
        act.wait_ge(self.mm.sem, self.mm(2))
        act.activation(self.std, self.P_VAR[:, 0:1], ACT.Sqrt, bias=self.k["unit"][:, 2:3]).then_inc(self.rooted.sem, 1)


    def scale_and_shift(self, dve):
        k, step, mm = self.k, self.step, self.mm
        step(dve, dve.bn_aggr(k["gn"][:, 0:2], k["gn_stats"][:].rearrange("p a b -> p (a b)")))
        dve.wait_ge(mm.sem, mm(1))
        step(dve, dve.tensor_copy(self.group_mean, self.P_MEAN[:, 0:1]))
        step(dve, dve.tensor_tensor(self.off, self.mean, self.group_mean, ALU.subtract))
        step(dve, dve.scalar_tensor_tensor(self.power, self.off, self.off, self.var, ALU.mult, ALU.add))
        dve.wait_ge(self.rooted.sem, self.rooted(1))
        step(dve, dve.reciprocal(self.scale, self.std))
        step(dve, dve.scalar_tensor_tensor(self.shift, self.group_mean, -1.0, self.scale, ALU.mult, ALU.mult))

    def plain_weights(self, dve):
        k, step, mm = self.k, self.step, self.mm
        dve.wait_ge(self.loaded.sem, self.loaded(16 * len(self.loads)))
        step(dve, dve.tensor_copy(k["w_proj"][:], k["w_raw"][:]))
        dve.wait_ge(mm.sem, mm(4))
        step(dve, dve.tensor_copy(k["mask"][:].rearrange("p a b -> p (a b)"), self.P_PROJ))

    def centering(self, dve):
        k, step, mm = self.k, self.step, self.mm
        step(dve, dve.tensor_scalar(k["center"][:], k["basis"][:], self.scale, None, ALU.mult))
        dve.wait_ge(mm.sem, mm(3))
        step(dve, dve.tensor_tensor(k["shift"][:], self.P_SHIFT[:, 0:1], k["unit"][:, 0:1], ALU.add))

    def normed_weights(self, dve):
        k, mm, vec = self.k, self.mm, self.k["vec"]

        def step(ins):
            self.step(dve, ins)

        dve.wait_ge(self.loaded.sem, self.loaded(16 * len(self.loads)))
        step(dve.memset(k["ln_sel"][:], 0.0))
        for g in range(2):
            half, last_col = slice(g * C, g * C + C), g * C + C - 1
            step(dve.tensor_copy(k["ln_sel"][half, last_col:last_col + 1], vec[half, V_LN_B:V_LN_B + 1]))
        step(dve.tensor_scalar(k["w_scaled"][:], k["w_raw"][:], vec[:, V_LN_G:V_LN_G + 1], None, ALU.mult))
        dve.wait_ge(mm.sem, mm(5))
        folded = k["w_scaled"]
        step(dve.tensor_copy(folded[:, 0:CH], self.P_PROJ))
        step(dve.tensor_copy(folded[:, CH:640], self.P_GATE[:, 0:P]))
        step(dve.tensor_reduce(k["size"][:, 0:2], folded[:, 0:CH].rearrange("p (a e) -> p a e", a=2), AXIS.X, ALU.max,
                               apply_absolute_value=True))
        step(dve.tensor_reduce(k["size"][:, 2:3], folded[:, CH:640], AXIS.X, ALU.max, apply_absolute_value=True))
        step(dve.memset(k["ones3"][:], 1.0))
        dve.wait_ge(mm.sem, mm(6))
        step(dve.tensor_reduce(k["size_t"][:], self.P_SIZE[0:3, :], AXIS.X, ALU.max))
        step(dve.tensor_scalar(k["size_diag"][:], k["ident"][0:3, 0:3], k["size_t"][:], None, ALU.mult))
        dve.wait_ge(mm.sem, mm(7))
        step(dve.tensor_scalar(k["largest"][:], self.P_LARGEST, 1e-30, None, ALU.max))
        step(dve.reciprocal(k["inverse"][:], k["largest"][:]))
        for group, (lo, hi) in enumerate(((0, S), (S, CH), (CH, 640))):
            step(dve.tensor_scalar(folded[:, lo:hi], folded[:, lo:hi], k["inverse"][:, group:group + 1], None, ALU.mult))
        parts = folded[:, 0:CH].rearrange("p (a g e) -> p a g e", a=2, g=2)
        step(dve.tensor_tensor(k["w_both"][:], parts[:, :, 0, :], parts[:, :, 1, :], ALU.add))
        for w, halves in ((k["w_both"][:].rearrange("p a e -> p (a e)"), k["w_heads"]), (folded[:, CH:640], k["w_gate"])):
            step(dve.tensor_copy(halves[:, 0, :], w))
            step(dve.tensor_tensor(halves[:, 1, :], w, halves[:, 0, :], ALU.subtract))
        step(dve.tensor_copy(k["spread"][:].rearrange("p a b -> p (a b)"), k["spread_in"]))

    def output_weights(self, dve):
        k, step, mm, vec = self.k, self.step, self.mm, self.k["vec"]
        assert self.steps == self.weight_steps
        if self.masked:
            step(dve, dve.tensor_copy(k["mask"][:].rearrange("p a b -> p (a b)"), self.P_TURN))
        else:
            step(dve, dve.tensor_tensor(k["out_bias"][:], self.P_BIAS, vec[:, V_OUT_B:V_OUT_B + 1], ALU.add))
            step(dve, dve.tensor_scalar(k["w_out"][:], k["w_out"][:], vec[:, V_ON_G:V_ON_G + 1], None, ALU.mult))
            dve.wait_ge(mm.sem, mm(8 if self.normed_in else 5))
            step(dve, dve.tensor_copy(k["w_out"][:], self.P_CENTER))

    def finish(self):
        assert self.steps == self.all_steps
        self.loaded.advance(16 * len(self.loads))
        self.mm.advance(self.mm_count)
        self.rooted.advance(1)
        self.done.advance(self.steps)


SEG_PARTS = 8


def store_part(sp, left_right, stage, seg, HG, part, done):
    lr, kb, g = part // 4, part // 2 % 2, part % 2
    groups = left_right[lr].rearrange("n k b s i h -> k n b s (i h)")
    src = stage[:, kb, g, lr, :, :, :].rearrange("p n i h -> p n (i h)")
    dst = groups[:, :, kb, bass.ds(seg + g * (S // SEG // 2), 1), :].rearrange("k n s e -> k n (s e)")
    sp.dma_start(dst, src).then_inc(done.sem, 16)


def project(nc, n, kind, low, HG, x, a, left_right, c, k, ps):
    LOAD, CENTER, VARIANCE, SPLIT, NORM = 16, 14, 13, 5, 4
    masked, gate = kind != "normed", a["gate"]
    with ExitStack() as ctx:
        def sb(name, shape, dt=F32):
            return ctx.enter_context(nc.sbuf_tensor(f"{name}_{n}", shape, dt))

        xs, zs, sq = sb("xs", [P, 8, CH]), sb("zs", [P, 16, CH]), sb("sq", [P, 2, CH])
        log_var, r, r_rest, r_mid = (sb(name, [2 * BATCH, CH], dt) for name, dt in
                                     (("log_var", F32), ("r", F32), ("r_rest", F32), ("r_mid", BF16)))
        r_terms = sb("r_terms", [P, 2, CH], BF16)
        xn, hi, lo = sb("xn", [P, 2, CH]), sb("hi", [P, 8, CH], F16), sb("lo", [P, 8, CH], F16)
        stacked = sb("stacked", [P, 8, 2, CH], F16)
        sig, gates = sb("sig", [P, 4, CH]), sb("gates", [P, 4, CH])
        stage = sb("stage", [P, 2, 2, 2, 2, C // HG, SEG, HG], low)
        Z, VAR, R, GATE = ps[0][:, 0, :], ps[0][0:2 * BATCH, 1, :], ps[1][:, 0, :], ps[1][:, 1, :]
        PAIR = [ps[2], ps[3]]
        AHEAD_Z = [Z, GATE]
        pair_read = c["pair_read"] if masked else c["lr_done"]
        fold = Fold(nc, ctx, n, kind, a, c, {**k, "spread_in": xn[:].rearrange("p a b -> p (a b)")}, ps)
        block = ctx.enter_context(nc.Block())
        bodies = NCH // BODY


        def staged(b, q, row):
            return stage[:, b, :, :, :, :, q % SCH * ROWS + row, :]

        def bodies_of(eng, step):
            with eng.Fori(0, bodies - 1) as i:
                for q in range(BODY):
                    step(i, q, lambda lead: True)
            for q in range(BODY):
                step(bodies - 1, q, lambda lead: q + lead < BODY)

        @block.sync
        def _(sp):

            def load(i, q):
                m = i * BODY + q
                sp.wait_ge(c["z_done"].sem, c["z_done"](m - 6))
                sp.dma_start(xs[:, q % 8:q % 8 + 2, :].rearrange("p a b -> p (a b)"),
                             x[:, bass.ds(m * CH, 2 * CH)]).then_inc(c[f"x_in{q % 8 // 2}"].sem, 16)

            def stack(i, q):
                m = i * BODY + q
                sp.wait_ge(c["lo_done"].sem, c["lo_done"](m + 2))
                slots = slice(q % 8, q % 8 + 2)
                for part, src in enumerate((hi, lo)):
                    for g in range(2):
                        sp.dma_start(stacked[part * C:part * C + C, slots, g, :],
                                     src[g * C:g * C + C, slots, :]).then_inc(c[f"stacked{q % 8 // 2}"].sem, 16)

            def store_gate(i, q):
                m = i * BODY + q
                sp.wait_ge(c["gate_done"].sem, c["gate_done"](m + 2))
                sp.dma_start(gate[:, bass.ds(m * CH, 2 * CH)],
                             gates[:, q % 4:q % 4 + 2, :].rearrange("p a b -> p (a b)")).then_inc(c[f"gate_out{q % 4 // 2}"].sem, 16)

            def store_parts(i, q):
                if q % SCH < SEG_PARTS // 2:
                    seg = q // SCH - 1
                    if q % SCH == 0:
                        sp.wait_ge(c["lr_done"].sem, c["lr_done"]((i * BODY + q) * 2))
                    for part in (q % SCH * 2, q % SCH * 2 + 1):
                        store_part(sp, left_right, stage[:, seg % 2], i * 2 + seg, HG, part, c[f"lr_out{seg % 2}"])

            def step(i, q, more, first=False):
                if q % 2 == 1:
                    if more(NORM):
                        stack(i, q + NORM - 1)
                elif more(LOAD):
                    load(i, q + LOAD)
                if not (first and q < SCH):
                    store_parts(i, q)
                if q % 2 == 1:
                    store_gate(i, q - 1)

            fold.load(sp)
            for q in range(0, LOAD, 2):
                load(0, q)
            for q in range(0, NORM, 2):
                stack(0, q)
            for q in range(BODY):
                step(0, q, lambda lead: True, first=True)
            with sp.Fori(1, bodies - 1) as i:
                for q in range(BODY):
                    step(i, q, lambda lead: True)
            for q in range(BODY):
                step(bodies - 1, q, lambda lead: q + lead < BODY)
            for q in range(SEG_PARTS // 2):
                store_parts(bodies, q)
            for s in range(2):
                sp.wait_ge(c[f"gate_out{s}"].sem, c[f"gate_out{s}"](16 * NCH // 4))
            for s in range(2):
                sp.wait_ge(c[f"lr_out{s}"].sem, c[f"lr_out{s}"](16 * SEG_PARTS * bodies))

        @block.tensor
        def _(pe):
            def center(i, q, bank, readers):
                m = i * BODY + q
                load = c[f"x_in{q % 8 // 2}"]
                pe.wait_ge(load.sem, load(i * 32 + (q // 8 + 1) * 16))
                pe.wait_ge(c["sq_done"].sem, c["sq_done"](readers))
                pe.matmul(bank, k["center"][:], xs[:, q % 8, :], start=True, stop=True).then_inc(c["z_done"].sem, 1)

            def variance(i, q):
                m = i * BODY + q
                pe.wait_ge(c["sq_done"].sem, c["sq_done"](m + 1))
                at = q % BATCH
                if at == 0:
                    batch = i * (BODY // BATCH) + q // BATCH
                    pe.wait_ge(c["log_done"].sem, c["log_done"](batch))
                w = k["var_w"][:, 2 * (BATCH - 1 - at):2 * (2 * BATCH - 1 - at)]
                pe.matmul(VAR, w, sq[:, q % 2, :], start=(at == 0), stop=(at == BATCH - 1)).then_inc(c["var_done"].sem, 1)

            def spread(i, q):
                m = i * BODY + q
                b = q // BATCH
                pe.wait_ge(c["r_split"].sem, c["r_split"](i * (BODY // BATCH) + b + 1))
                pe.wait_ge(c["xn_done"].sem, c["xn_done"](m))
                pe.matmul(R, k["spread"][:, q % BATCH, :], r_terms[:, b % 2, :], start=True, stop=True).then_inc(c["spread_done"].sem, 1)

            def heads(i, q, row):
                m = i * BODY + q
                if row == 0:
                    stack = c[f"stacked{q % 8 // 2}"]
                    pe.wait_ge(stack.sem, stack(i * 128 + (q // 8 + 1) * 64))
                pe.wait_ge(pair_read.sem, pair_read(m * 2 + row - 1))
                for kb in range(2):
                    bank = PAIR[row][:, kb, :].rearrange("p (a g e) -> p a g e", a=2, g=2)
                    at = row * S + kb * P
                    for g in range(2):
                        for part in range(2):
                            last = pe.matmul(bank[:, :, g, :], stacked[:, q % 8, g, at:at + P], k["w_heads"][:, part, :],
                                             start=(part == 0), stop=(part == 1))
                last.then_inc(c["proj_done"].sem, 1)

            def out_gate(i, q):
                m = i * BODY + q
                pe.wait_ge(c["gate_done"].sem, c["gate_done"](m))
                pe.matmul(GATE, k["w_gate"][:, 0, :], hi[:, q % 8, :], start=True, stop=False)
                pe.matmul(GATE, k["w_gate"][:, 0, :], lo[:, q % 8, :], start=False, stop=False)
                pe.matmul(GATE, k["w_gate"][:, 1, :], hi[:, q % 8, :], start=False, stop=True).then_inc(c["gate_mm_done"].sem, 1)

            def step(i, q, more):
                if more(NORM):
                    spread(i, q + NORM)
                if more(CENTER):
                    center(i, q + CENTER, Z, i * BODY + q + CENTER)
                heads(i, q, 0)
                if more(VARIANCE):
                    variance(i, q + VARIANCE)
                heads(i, q, 1)
                out_gate(i, q)

            fold.multiply_statistics(pe)
            pe.wait_ge(fold.done.sem, fold.done(8))
            between = {0: (fold.multiply_bias,), 1: (fold.multiply_weights,), 4: (fold.turn_sizes,), 5: (fold.spread_sizes,),
                       9: (fold.center_output,)}
            for q in range(CENTER):
                center(0, q, AHEAD_Z[q % 2], q - 1)
                if q > 0:
                    variance(0, q - 1)
                for part in between.get(q, ()):
                    part(pe)
                if q >= CENTER - NORM:
                    spread(0, q - (CENTER - NORM))
            pe.wait_ge(fold.done.sem, fold.done(fold.all_steps))
            bodies_of(pe, step)

        @block.scalar
        def _(act):
            def square(i, q, bank):
                m = i * BODY + q
                act.wait_ge(c["z_done"].sem, c["z_done"](m + 1))
                act.wait_ge(c["xn_done"].sem, c["xn_done"](m - 15))
                act.activation(zs[:, q % 16, :], bank, ACT.Identity, bias=k["shift"][:])
                act.wait_ge(c["var_done"].sem, c["var_done"](m - 1))
                act.activation(sq[:, q % 2, :], bank, ACT.Square, bias=k["shift"][:]).then_inc(c["sq_done"].sem, 1)

            def root(i, b):
                batch = i * (BODY // BATCH) + b
                act.preload_act_table_set(LN_SET)
                act.wait_ge(c["var_done"].sem, c["var_done"](batch * BATCH + BATCH))
                act.activation(log_var[:], VAR, ACT.Ln, bias=k["unit"][0:2 * BATCH, 2:3]).then_inc(c["log_done"].sem, 1)
                act.wait_ge(c["log_done"].sem, c["log_done"](batch + 1))
                act.wait_ge(c["r_split"].sem, c["r_split"](batch))
                act.activation(r[:], log_var[:], ACT.Exp, scale=-0.5).then_inc(c["r_done"].sem, 1)

            def gate_pair(i, q, row):
                m = i * BODY + q
                slot = (2 * q + row) % 4
                act.wait_ge(c["proj_done"].sem, c["proj_done"](m * 2 + row + 1))
                act.wait_ge(c["lr_done"].sem, c["lr_done"](m * 2 + row - 3))
                act.activation(sig[:, slot, :].rearrange("p (b e) -> p b e", b=2), PAIR[row][:, :, 0:S],
                               ACT.Sigmoid, scale=k["largest"][:, 0:1]).then_inc(c["sig_done"].sem, 1)

            def step(i, q, more):
                m = i * BODY + q
                if more(CENTER):
                    square(i, q + CENTER, Z)
                gate_pair(i, q, 0)
                gate_pair(i, q, 1)
                act.wait_ge(c["gate_mm_done"].sem, c["gate_mm_done"](m + 1))
                stored = c[f"gate_out{q % 4 // 2}"]
                act.wait_ge(stored.sem, stored(i * 64 + q // 4 * 16))
                act.activation(gates[:, q % 4, :], GATE, ACT.Sigmoid, scale=k["largest"][:, 2:3]).then_inc(c["gate_done"].sem, 1)
                if more(VARIANCE) and (q + VARIANCE) % BATCH == BATCH - 1:
                    root(i, (q + VARIANCE) // BATCH)

            fold.root(act)
            act.wait_ge(fold.done.sem, fold.done(8))
            for q in range(CENTER):
                square(0, q, AHEAD_Z[q % 2])
                if q == BATCH:
                    root(0, 0)
            bodies_of(act, step)

        @block.vector
        def _(dve):
            def split_r(i, b):
                batch = i * (BODY // BATCH) + b
                parts, split = c["r_part"], c["r_split"]
                terms = [r_terms[R_PART * part:R_PART * part + 2 * BATCH, b % 2, :] for part in range(3)]
                dve.wait_ge(c["r_done"].sem, c["r_done"](batch + 1))
                dve.wait_ge(c["spread_done"].sem, c["spread_done"](batch * BATCH - BATCH))
                dve.tensor_copy(terms[0], r[:]).then_inc(parts.sem, 1)
                dve.wait_ge(parts.sem, parts(batch * 3 + 1))
                dve.tensor_tensor(r_rest[:], r[:], terms[0], ALU.subtract).then_inc(parts.sem, 1)
                dve.wait_ge(parts.sem, parts(batch * 3 + 2))
                dve.tensor_copy(r_mid[:], r_rest[:]).then_inc(parts.sem, 1)
                dve.wait_ge(parts.sem, parts(batch * 3 + 3))
                dve.tensor_copy(terms[1], r_mid[:])
                dve.tensor_tensor(terms[2], r_rest[:], r_mid[:], ALU.subtract).then_inc(split.sem, 1)
                dve.wait_ge(split.sem, split(batch + 1))

            def norm(i, q):
                m = i * BODY + q
                dve.wait_ge(c["spread_done"].sem, c["spread_done"](m + 1))
                dve.wait_ge(c["lo_done"].sem, c["lo_done"](m - 1))
                dve.tensor_tensor(xn[:, q % 2, :], zs[:, q % 16, :], R, ALU.mult).then_inc(c["xn_done"].sem, 1)
                dve.wait_ge(c["xn_done"].sem, c["xn_done"](m + 1))
                dve.wait_ge(c["gate_mm_done"].sem, c["gate_mm_done"](m - 7))
                dve.tensor_copy(hi[:, q % 8, :], xn[:, q % 2, :]).then_inc(c["hi_done"].sem, 1)
                dve.wait_ge(c["hi_done"].sem, c["hi_done"](m + 1))
                dve.tensor_tensor(lo[:, q % 8, :], xn[:, q % 2, :], hi[:, q % 8, :], ALU.subtract).then_inc(c["lo_done"].sem, 1)

            def left_and_right(i, q):
                m = i * BODY + q
                b = q // SCH
                if q % SCH == 0 and not masked:
                    dve.wait_ge(c[f"lr_out{b}"].sem, c[f"lr_out{b}"](i * 16 * SEG_PARTS))
                for row in range(ROWS):
                    factor = sig[:, (2 * q + row) % 4, :].rearrange("p (b n h) -> p b n h", b=2, h=HG)
                    dst = factor if masked else staged(b, q, row).rearrange("p b g l n h -> p b (g l n) h")
                    dve.wait_ge(c["sig_done"].sem, c["sig_done"](m * 2 + row + 1))
                    dve.scalar_tensor_tensor(dst, PAIR[row][:, :, S:CH].rearrange("p b (n h) -> p b n h", h=HG),
                                             k["largest"][:, 1:2], factor, ALU.mult, ALU.mult).then_inc(pair_read.sem, 1)

            def step(i, q, more):
                if more(NORM):
                    norm(i, q + NORM)
                if more(SPLIT) and (q + SPLIT) % BATCH == 0:
                    split_r(i, (q + SPLIT) // BATCH)
                left_and_right(i, q)

            fold.scale_and_shift(dve)
            fold.centering(dve)
            fold.normed_weights(dve)
            fold.output_weights(dve)
            dve.memset(r_terms[:], 0.0).then_inc(c["r_part"].sem, 1)
            dve.wait_ge(c["r_part"].sem, c["r_part"](1))
            c["r_part"].advance(1)
            dve.memset(r_terms[R_ONE:R_ONE + 1, :, :], 1.0).then_inc(c["r_part"].sem, 1)
            c["r_part"].advance(1)
            split_r(0, 0)
            for q in range(NORM):
                norm(0, q)
            bodies_of(dve, step)

        if masked:
            @block.gpsimd
            def _(pool):
                def pair(i, q, row):
                    m = i * BODY + q
                    b = q // SCH
                    if q % SCH == 0 and row == 0:
                        pool.wait_ge(c[f"lr_out{b}"].sem, c[f"lr_out{b}"](i * 16 * SEG_PARTS))
                    pool.wait_ge(c["pair_read"].sem, c["pair_read"](m * 2 + row + 1))
                    product = sig[:, (2 * q + row) % 4, :].rearrange("p (a n h) -> p a n h", a=4, h=HG)
                    by_g = k["mask"][:].rearrange("p b (g i) -> p (b g) i", g=2)
                    mk = by_g[:, :, bass.ds(m * ROWS + row, 1)].unsqueeze(3).to_broadcast([P, 4, P // HG, HG])
                    pool.tensor_tensor(staged(b, q, row).rearrange("p b g l n h -> p (b g) (l n) h"), product, mk,
                                       ALU.mult).then_inc(c["lr_done"].sem, 1)

                with pool.Fori(0, bodies) as i:
                    for q in range(BODY):
                        for row in range(ROWS):
                            pair(i, q, row)

    fold.finish()
    for s in range(4):
        c[f"x_in{s}"].advance(16 * NCH // 8)
        c[f"stacked{s}"].advance(64 * NCH // 8)
    for s in range(2):
        c[f"gate_out{s}"].advance(16 * NCH // 4)
        c[f"lr_out{s}"].advance(128 * bodies)
    batches = NCH // BATCH
    for name in ("log_done", "r_done", "r_split"):
        c[name].advance(batches)
    c["r_part"].advance(3 * batches)
    for name in ("z_done", "sq_done", "var_done", "spread_done", "xn_done", "hi_done", "lo_done", "gate_mm_done", "gate_done"):
        c[name].advance(NCH)
    for name in ("proj_done", "sig_done", "lr_done") + (("pair_read",) if masked else ()):
        c[name].advance(2 * NCH)


def project_plain(nc, n, HG, x, gate, left_right, c, k, ps):
    with ExitStack() as ctx:
        def sb(name, shape, dt=F32):
            return ctx.enter_context(nc.sbuf_tensor(f"{name}_{n}", shape, dt))

        xs, xn = sb("xs", [P, 8, CH]), sb("xn", [P, 4, CH])
        biased, product, gates = sb("biased", [P, 2, 4, P]), sb("product", [P, 2, 4, C]), sb("gates", [P, 4, CH])
        stage = sb("stage", [P, 2, 2, 2, 2, 16 // HG, SEG, HG])
        TILES, GATE = [ps[0][:, q, :] for q in range(2)], [ps[1][:, q, :] for q in range(2)]
        block = ctx.enter_context(nc.Block())
        bodies = NCH // BODY

        @block.sync
        def _(sp):
            def load(i, q):
                m = i * BODY + q
                sp.wait_ge(c["xn_done"].sem, c["xn_done"](m - 7))
                sp.dma_start(xs[:, q % 8, :], x[:, bass.ds(m * CH, CH)]).then_inc(c[f"x_in{q % 8}"].sem, 16)

            def store(i, q):
                m = i * BODY + q
                sp.wait_ge(c["gate_done"].sem, c["gate_done"](m + 1))
                sp.dma_start(gate[:, bass.ds(m * CH, CH)], gates[:, q % 4, :]).then_inc(c[f"gate_out{q % 4}"].sem, 16)
                if q % SCH == SCH - 1:
                    sp.wait_ge(c["lr_done"].sem, c["lr_done"](m + 1))
                    b = q // SCH
                    for part in range(SEG_PARTS):
                        store_part(sp, left_right, stage[:, b], i * 2 + b, HG, part, c[f"lr_out{b}"])

            for q in range(6):
                load(0, q)
            with sp.Fori(0, bodies - 1) as i:
                for q in range(BODY):
                    load(i, q + 6)
                    store(i, q)
            for q in range(BODY):
                if q + 6 < BODY:
                    load(bodies - 1, q + 6)
                store(bodies - 1, q)
            for s in range(4):
                sp.wait_ge(c[f"gate_out{s}"].sem, c[f"gate_out{s}"](16 * NCH // 4))
            for s in range(2):
                sp.wait_ge(c[f"lr_out{s}"].sem, c[f"lr_out{s}"](16 * 8 * bodies))

        @block.tensor
        def _(pe):
            with pe.Fori(0, bodies) as i:
                for q in range(BODY):
                    m = i * BODY + q
                    pe.wait_ge(c["xn_done"].sem, c["xn_done"](m + 1))
                    pe.wait_ge(c["masked"].sem, c["masked"](m - 1))
                    for t in range(4):
                        last = pe.matmul(TILES[q % 2][:, t * P:t * P + P], xn[:, q % 4, t * P:t * P + P],
                                         k["w_proj"][:, 0:P], start=True, stop=True)
                    last.then_inc(c["proj_done"].sem, 1)
                    pe.wait_ge(c["gate_done"].sem, c["gate_done"](m - 1))
                    pe.matmul(GATE[q % 2], k["w_proj"][:, CH:CH + P], xn[:, q % 4, :],
                              start=True, stop=True).then_inc(c["gate_mm_done"].sem, 1)

        @block.vector
        def _(dve):
            def affine(i, q):
                m = i * BODY + q
                load = c[f"x_in{q % 8}"]
                dve.wait_ge(load.sem, load(i * 32 + (q // 8 + 1) * 16))
                dve.wait_ge(c["gate_mm_done"].sem, c["gate_mm_done"](m - 3))
                dve.tensor_scalar(xn[:, q % 4, :], xs[:, q % 8, :], k["gn"][:, 6:7], k["gn"][:, 7:8],
                                  ALU.mult, ALU.add).then_inc(c["xn_done"].sem, 1)

            def multiply(i, q):
                m = i * BODY + q
                dve.wait_ge(c["proj_done"].sem, c["proj_done"](m + 1))
                dve.wait_ge(c["sig_done"].sem, c["sig_done"](m - 1))
                dve.tensor_tensor(biased[:, q % 2].rearrange("p a b -> p (a b)"), TILES[q % 2],
                                  k["mask"][:].rearrange("p a b -> p (a b)"), ALU.add).then_inc(c["masked"].sem, 1)
                dve.wait_ge(c["masked"].sem, c["masked"](m + 1))
                dve.wait_ge(c["lr_done"].sem, c["lr_done"](m - 1))
                dve.tensor_tensor(product[:, q % 2], biased[:, q % 2, :, 0:C], biased[:, q % 2, :, C:P],
                                  ALU.mult).then_inc(c["sig_done"].sem, 1)

            affine(0, 0)
            affine(0, 1)
            with dve.Fori(0, bodies - 1) as i:
                for q in range(BODY):
                    affine(i, q + 2)
                    multiply(i, q)
            for q in range(BODY):
                if q + 2 < BODY:
                    affine(bodies - 1, q + 2)
                multiply(bodies - 1, q)

        @block.scalar
        def _(act):
            with act.Fori(0, bodies) as i:
                for q in range(BODY):
                    m = i * BODY + q
                    b = q // SCH
                    if q % SCH == 0:
                        act.wait_ge(c[f"lr_out{b}"].sem, c[f"lr_out{b}"](i * 128))
                    act.wait_ge(c["sig_done"].sem, c["sig_done"](m + 1))
                    for row in range(ROWS):
                        at = q % SCH * ROWS + row
                        dst = stage[:, b, :, :, :, :, at, :].rearrange("p b g l n h -> p b (g l n) h")
                        last = act.activation(dst, product[:, q % 2, 2 * row:2 * row + 2, :].rearrange("p b (n h) -> p b n h", h=HG),
                                              ACT.Sigmoid)
                    last.then_inc(c["lr_done"].sem, 1)
                    act.wait_ge(c["gate_mm_done"].sem, c["gate_mm_done"](m + 1))
                    stored = c[f"gate_out{q % 4}"]
                    act.wait_ge(stored.sem, stored(i * 64 + q // 4 * 16))
                    act.activation(gates[:, q % 4, :], GATE[q % 2], ACT.Sigmoid,
                                   bias=k["vec"][:, V_GATE_B:V_GATE_B + 1]).then_inc(c["gate_done"].sem, 1)

    for s in range(8):
        c[f"x_in{s}"].advance(16 * NCH // 8)
    for s in range(4):
        c[f"gate_out{s}"].advance(16 * NCH // 4)
    for s in range(2):
        c[f"lr_out{s}"].advance(128 * bodies)
    for name in ("xn_done", "proj_done", "masked", "sig_done", "lr_done", "gate_mm_done", "gate_done"):
        c[name].advance(NCH)


def triangle(nc, n, turned, low, H, HG, left_right, O, c, k, ps):
    turns = H // HG // 2
    with ExitStack() as ctx:
        left = ctx.enter_context(nc.sbuf_tensor(f"left{n}", [P, 2, 2, S, HG], low))
        right = ctx.enter_context(nc.sbuf_tensor(f"right{n}", [P, 2, 2, S, HG], low))
        right_t = ctx.enter_context(nc.sbuf_tensor(f"right_t{n}", [P, 2, 2, S], F32)) if turned else None
        block = ctx.enter_context(nc.Block())

        def channel(t, s, h):
            return t * (2 * HG) + (s * HG + h)

        @block.sync
        def _(sp):
            with sp.Fori(0, turns) as t:
                for s in range(2):
                    sp.wait_ge(c["tri_done"].sem, c["tri_done"](channel(t, s, 0) - HG))
                    for lr, dst in ((0, left), (1, right)):
                        sp.dma_start(dst[:, s].rearrange("p b i h -> p (b i h)"),
                                     left_right[lr, bass.ds(t * 2 + s, 1)].rearrange("n k b s i h -> k (n b s i h)")
                                     ).then_inc(c[f"lr_in{s}"].sem, 16)

        @block.tensor
        def _(pe):
            def turn(t, s, h):
                ch = channel(t, s, h)
                pe.wait_ge(c["tr_copied"].sem, c["tr_copied"](ch - 1))
                for kb in range(2):
                    for jb in range(2):
                        at = kb * S + jb * P
                        last = pe.transpose(ps[2 + h % 2][:, 0, at:at + P],
                                            right[:, s, jb, kb * P:kb * P + P, h], k["ident"][:])
                last.then_inc(c["tr_done"].sem, 1)

            def contract(t, s, h):
                ch = channel(t, s, h)
                if turned:
                    pe.wait_ge(c["tr_copied"].sem, c["tr_copied"](ch + 1))
                pe.wait_ge(c["o_copied"].sem, c["o_copied"](ch - 3))
                for jb in range(2):
                    for kb in range(2):
                        stationary = (right_t[:, h % 2, kb, jb * P:jb * P + P] if turned
                                      else right[:, s, kb, jb * P:jb * P + P, h])
                        last = pe.matmul(ps[h % 4 // 2][:, h % 2, jb * S:jb * S + S], stationary,
                                         left[:, s, kb, :, h], start=(kb == 0), stop=(kb == 1))
                last.then_inc(c["tri_done"].sem, 1)

            with pe.Fori(0, turns) as t:
                for s in range(2):
                    load = c[f"lr_in{s}"]
                    pe.wait_ge(load.sem, load(t * 32 + 32))
                    if turned:
                        turn(t, s, 0)
                    for h in range(HG):
                        if turned and h + 1 < HG:
                            turn(t, s, h + 1)
                        contract(t, s, h)

        if turned:
            @block.vector
            def _(dve):
                with dve.Fori(0, turns) as t:
                    for s in range(2):
                        for h in range(HG):
                            ch = channel(t, s, h)
                            dve.wait_ge(c["tr_done"].sem, c["tr_done"](ch + 1))
                            dve.wait_ge(c["tri_done"].sem, c["tri_done"](ch - 1))
                            dve.tensor_copy(right_t[:, h % 2].rearrange("p b j -> p (b j)"),
                                            ps[2 + h % 2][:, 0, :]).then_inc(c["tr_copied"].sem, 1)

        @block.scalar
        def _(act):
            with act.Fori(0, turns) as t:
                for s in range(2):
                    for h in range(HG):
                        ch = channel(t, s, h)
                        act.wait_ge(c["tri_done"].sem, c["tri_done"](ch + 1))
                        dst = O[:].rearrange("p b i g h -> p b g i h")[:, :, :, :, bass.ds(ch, 1)].rearrange("p b g i h -> p b g (i h)")
                        act.activation(dst, ps[h % 4 // 2][:, h % 2, :].rearrange("p (b g i) -> p b g i", b=2, g=2),
                                       ACT.Copy).then_inc(c["o_copied"].sem, 1)

    for s in range(2):
        c[f"lr_in{s}"].advance(32 * turns)
    for name in ("tri_done", "o_copied") + (("tr_done", "tr_copied") if turned else ()):
        c[name].advance(H)


def output(nc, n, gate_first, H, O, x, gate, x_new, c, k, ps):
    counted = n < 3
    HH = 2 * H
    TOK = 4 * SEG
    STAT, CENTER, SCALE, TURN, GATED, OUTMM, OUTGATED = 14, 5, 4, 3, 2, 1 if gate_first else 2, 1
    LOAD_X, LOAD_G = 4, 6 if gate_first else 5
    RING = 4
    with ExitStack() as ctx:
        def sb(name, shape, dt=F32):
            return ctx.enter_context(nc.sbuf_tensor(f"out_{name}_{n}", shape, dt))

        xs, gs, xo = sb("xs", [P, RING, CH]), sb("gs", [P, RING, CH]), sb("xo", [P, RING, CH])
        centered = sb("centered", [P, RING, 2, 4, H]) if gate_first else None
        scaled = sb("scaled", [P, RING, 2, 4, H])
        if gate_first:
            wt, u = sb("wt", [P, RING, CH]), sb("u", [P, RING, CH])
        else:
            u, og = sb("u", [P, RING, CH]), sb("og", [P, RING, CH])
        bn = sb("bn", [P, 2, 2, 2 * SEG, 6])
        small = sb("small", [P, 4, TOK])
        mu, std, rs = sb("mu", [P, 2, 2, 2 * SEG]), sb("std", [P, 2, TOK]), sb("rs", [P, 2, 2, 2 * SEG])
        var = sb("var", [P, 2, TOK])
        TURNED, OUT = [ps[q // 2][0:HH, q % 2, :] for q in range(4)], [ps[2 + q // 2][:, q % 2, :] for q in range(4)]
        block = ctx.enter_context(nc.Block())
        bodies = NCH // BODY
        rows = O[:].rearrange("p b i g h -> p b (i g) h")

        def per_token(values, q):
            at = q % SCH * 2 * ROWS
            return values[:, q // SCH % 2, :, at:at + 2 * ROWS].unsqueeze(3).to_broadcast([P, 2, 2 * ROWS, H])

        def bodies_of(eng, step):
            with eng.Fori(0, bodies - 1) as i:
                for q in range(BODY):
                    step(i, q, lambda lead: True)
            for q in range(BODY):
                step(bodies - 1, q, lambda lead: q + lead < BODY)

        @block.sync
        def _(sp):
            def load_x(i, q):
                m = i * BODY + q
                free = c["out_mm_done"] if gate_first else c["x_new"]
                sp.wait_ge(free.sem, free(m - 3))
                sp.dma_start(xs[:, q % RING, :], x[:, bass.ds(m * CH, CH)]).then_inc(c[f"xc_in{q % RING}"].sem, 16)

            def load_g(i, q):
                m = i * BODY + q
                free = c["gated"] if gate_first else c["out_gated"]
                sp.wait_ge(free.sem, free(m - 3))
                sp.dma_start(gs[:, q % RING, :], gate[:, bass.ds(m * CH, CH)]).then_inc(c[f"gc_in{q % RING}"].sem, 16)

            def step(i, q, more):
                if more(LOAD_G):
                    load_g(i, q + LOAD_G)
                if more(LOAD_X):
                    load_x(i, q + LOAD_X)
                m = i * BODY + q
                sp.wait_ge(c["x_new"].sem, c["x_new"](m + 1))
                sp.dma_start(x_new[:, bass.ds(m * CH, CH)], xo[:, q % RING, :]).then_inc(c[f"x_out{q % RING}"].sem, 16)

            for q in range(4):
                load_g(0, q)
                load_x(0, q)
            for q in range(4, LOAD_G):
                load_g(0, q)
            bodies_of(sp, step)
            for s in range(RING):
                sp.wait_ge(c[f"x_out{s}"].sem, c[f"x_out{s}"](16 * NCH // RING))

        @block.vector
        def _(dve):
            def statistics(i, q):
                b = q // SCH % 2
                for jb in range(2):
                    for t in range(2 * ROWS):
                        at = q % SCH * 2 * ROWS + t
                        last = dve.bn_stats(bn[:, b, jb, at, :],
                                            rows[:, jb, bass.ds(i * (BODY * 2 * ROWS) + q * 2 * ROWS + t, 1), :].rearrange("p a h -> p (a h)"))
                last.then_inc(c["ln_stat"].sem, 1)

            def moments(i, b):
                batch = i * (BODY // SCH) + b
                v = bn[:, b % 2].rearrange("p b t s -> p (b t) s")
                col = [v[:, :, q:q + 1].rearrange("p t s -> p (t s)") for q in range(6)]
                dve.wait_ge(c["ln_stat"].sem, c["ln_stat"](batch * SCH + SCH))
                dve.tensor_tensor(small[:, 0], col[1], col[4], ALU.add)
                dve.tensor_tensor(small[:, 1], col[1], col[4], ALU.subtract)
                dve.tensor_tensor(small[:, 2], col[2], col[5], ALU.add).then_inc(c["ln_small"].sem, 1)
                dve.wait_ge(c["ln_small"].sem, c["ln_small"](batch * 2 + 1))
                if gate_first:
                    dve.wait_ge(c["centered"].sem, c["centered"](batch * SCH - SCH))
                    dve.tensor_scalar(mu[:, b % 2].rearrange("p b t -> p (b t)"), small[:, 0], 0.5, None, ALU.mult)
                dve.scalar_tensor_tensor(small[:, 3], small[:, 1], 0.25, small[:, 1], ALU.mult, ALU.mult).then_inc(c["ln_small"].sem, 1)
                dve.wait_ge(c["ln_small"].sem, c["ln_small"](batch * 2 + 2))
                dve.scalar_tensor_tensor(var[:, b % 2], small[:, 2], 1.0 / H, small[:, 3], ALU.mult, ALU.add).then_inc(c["ln_var"].sem, 1)

            def invert(i, b):
                batch = i * (BODY // SCH) + b
                dve.wait_ge(c["ln_root"].sem, c["ln_root"](batch + 1))
                dve.wait_ge(c["scaled"].sem, c["scaled"](batch * SCH - SCH))
                dve.reciprocal(rs[:, b % 2].rearrange("p b t -> p (b t)"), std[:, b % 2]).then_inc(c["ln_scale"].sem, 1)
                dve.wait_ge(c["ln_scale"].sem, c["ln_scale"](batch + 1))

            def scale(i, q):
                m = i * BODY + q
                dve.wait_ge(c["centered"].sem, c["centered"](m + 1))
                dve.wait_ge(c["wt_done"].sem, c["wt_done"](m - 3))
                dve.tensor_tensor(scaled[:, q % RING], centered[:, q % RING], per_token(rs, q),
                                  ALU.mult).then_inc(c["scaled"].sem, 1)

            def gate_output(i, q):
                m = i * BODY + q
                dve.wait_ge(c["out_mm_done"].sem, c["out_mm_done"](m + 1))
                load = c[f"gc_in{q % RING}"]
                dve.wait_ge(load.sem, load(i * 64 + (q // RING + 1) * 16))
                dve.wait_ge(c["x_new"].sem, c["x_new"](m - 3))
                dve.scalar_tensor_tensor(og[:, q % RING], OUT[q % 4], k["out_bias"][:], gs[:, q % RING, :],
                                         ALU.add, ALU.mult).then_inc(c["out_gated"].sem, 1)

            def count(i, q):
                m = i * BODY + q
                dve.wait_ge(c["x_new"].sem, c["x_new"](m + 1))
                dve.bn_stats(k["gn_stats"][:, bass.ds(m, 1), :].rearrange("p a b -> p (a b)"), xo[:, q % RING, :]).then_inc(c["counted"].sem, 1)

            def step(i, q, more):
                if more(STAT):
                    statistics(i, q + STAT)
                    if (q + STAT) % SCH == SCH - 1:
                        moments(i, (q + STAT) // SCH)
                if more(CENTER) and (q + CENTER) % SCH == 0:
                    invert(i, (q + CENTER) // SCH)
                if gate_first and more(SCALE):
                    scale(i, q + SCALE)
                if not gate_first and more(OUTGATED):
                    gate_output(i, q + OUTGATED)
                if counted:
                    count(i, q)

            if HH < P:
                dve.memset(u[:], 0.0).then_inc(c["u_cleared"].sem, 1)
            for q in range(SCH):
                statistics(0, q)
            moments(0, 0)
            for q in range(STAT - SCH):
                statistics(0, q + SCH)
                if q == 0:
                    invert(0, 0)
                if gate_first and q < SCALE:
                    scale(0, q)
            if not gate_first:
                for q in range(OUTGATED):
                    gate_output(0, q)
            bodies_of(dve, step)

        @block.gpsimd
        def _(pool):
            def center(i, q):
                m = i * BODY + q
                if q % SCH == 0:
                    batch = i * (BODY // SCH) + q // SCH
                    pool.wait_ge(c["ln_var"].sem, c["ln_var"](batch + 1))
                pool.wait_ge(c["scaled"].sem, c["scaled"](m - 3))
                pool.tensor_tensor(centered[:, q % RING], rows[:, :, bass.ds(m * 2 * ROWS, 2 * ROWS), :], per_token(mu, q),
                                   ALU.subtract).then_inc(c["centered"].sem, 1)

            def scale(i, q):
                m = i * BODY + q
                if q % SCH == 0:
                    batch = i * (BODY // SCH) + q // SCH
                    pool.wait_ge(c["ln_scale"].sem, c["ln_scale"](batch + 1))
                pool.wait_ge(c["wt_done"].sem, c["wt_done"](m - 3))
                pool.tensor_tensor(scaled[:, q % RING], rows[:, :, bass.ds(m * 2 * ROWS, 2 * ROWS), :], per_token(rs, q),
                                   ALU.mult).then_inc(c["scaled"].sem, 1)

            def gate_input(i, q):
                m = i * BODY + q
                pool.wait_ge(c["wt_copied"].sem, c["wt_copied"](m + 1))
                load = c[f"gc_in{q % RING}"]
                pool.wait_ge(load.sem, load(i * 64 + (q // RING + 1) * 16))
                pool.wait_ge(c["out_mm_done"].sem, c["out_mm_done"](m - 3))
                pool.tensor_tensor(u[:, q % RING], wt[:, q % RING], gs[:, q % RING, :], ALU.mult).then_inc(c["gated"].sem, 1)

            def add_residual(i, q):
                m = i * BODY + q
                pool.wait_ge(c["out_gated"].sem, c["out_gated"](m + 1))
                load, stored = c[f"xc_in{q % RING}"], c[f"x_out{q % RING}"]
                pool.wait_ge(load.sem, load(i * 64 + (q // RING + 1) * 16))
                pool.wait_ge(stored.sem, stored(i * 64 + q // RING * 16))
                if counted:
                    pool.wait_ge(c["counted"].sem, c["counted"](m - 3))
                pool.tensor_tensor(xo[:, q % RING, :], og[:, q % RING], xs[:, q % RING, :], ALU.add).then_inc(c["x_new"].sem, 1)

            def step(i, q, more):
                if gate_first and more(CENTER):
                    center(i, q + CENTER)
                if not gate_first and more(SCALE):
                    scale(i, q + SCALE)
                if gate_first:
                    if more(GATED):
                        gate_input(i, q + GATED)
                else:
                    add_residual(i, q)

            for q in range(CENTER if gate_first else SCALE):
                (center if gate_first else scale)(0, q)
            if gate_first:
                for q in range(GATED):
                    gate_input(0, q)
            bodies_of(pool, step)

        @block.tensor
        def _(pe):
            def turn(i, q):
                m = i * BODY + q
                pe.wait_ge(c["scaled"].sem, c["scaled"](m + 1))
                pe.wait_ge(c["wt_copied"].sem, c["wt_copied"](m - 3))
                for row in range(ROWS):
                    for jb in range(2):
                        at = row * S + jb * P
                        last = pe.transpose(TURNED[q % 4][:, at:at + P],
                                            scaled[:, q % RING, jb, 2 * row:2 * row + 2, :].rearrange("p g h -> p (g h)"), k["ident"][:])
                last.then_inc(c["wt_done"].sem, 1)

            def multiply(i, q):
                m = i * BODY + q
                ready = c["gated"] if gate_first else c["wt_copied"]
                pe.wait_ge(ready.sem, ready(m + 1))
                bank_free = c["x_new"] if gate_first else c["out_gated"]
                pe.wait_ge(bank_free.sem, bank_free(m - 3))
                if gate_first:
                    pe.matmul(OUT[q % 4], k["w_out"][:], u[:, q % RING], start=True, stop=False)
                    load = c[f"xc_in{q % RING}"]
                    pe.wait_ge(load.sem, load(i * 64 + (q // RING + 1) * 16))
                    mm = pe.matmul(OUT[q % 4], k["ident"][:], xs[:, q % RING, :], start=False, stop=True)
                else:
                    mm = pe.matmul(OUT[q % 4], k["w_out"][:], u[:, q % RING], start=True, stop=True)
                mm.then_inc(c["out_mm_done"].sem, 1)

            def step(i, q, more):
                if more(TURN):
                    turn(i, q + TURN)
                if more(OUTMM):
                    multiply(i, q + OUTMM)

            for q in range(TURN):
                turn(0, q)
            for q in range(OUTMM):
                multiply(0, q)
            bodies_of(pe, step)

        @block.scalar
        def _(act):
            def copy(i, q):
                m = i * BODY + q
                act.wait_ge(c["wt_done"].sem, c["wt_done"](m + 1))
                free = c["gated"] if gate_first else c["out_mm_done"]
                act.wait_ge(free.sem, free(m - 3))
                if gate_first:
                    ins = act.activation(wt[:, q % RING], TURNED[q % 4], ACT.Identity, scale=k["vec"][:, V_ON_G:V_ON_G + 1],
                                         bias=k["vec"][:, V_ON_B:V_ON_B + 1])
                else:
                    ins = act.activation(u[0:HH, q % RING], TURNED[q % 4], ACT.Copy)
                ins.then_inc(c["wt_copied"].sem, 1)

            def root(i, b):
                batch = i * (BODY // SCH) + b
                act.wait_ge(c["ln_var"].sem, c["ln_var"](batch + 1))
                act.wait_ge(c["ln_scale"].sem, c["ln_scale"](batch - 1))
                act.activation(std[:, b % 2], var[:, b % 2], ACT.Sqrt, bias=k["unit"][:, 2:3]).then_inc(c["ln_root"].sem, 1)

            def step(i, q, more):
                if more(TURN):
                    copy(i, q + TURN)
                if gate_first:
                    m = i * BODY + q
                    act.wait_ge(c["out_mm_done"].sem, c["out_mm_done"](m + 1))
                    stored = c[f"x_out{q % RING}"]
                    act.wait_ge(stored.sem, stored(i * 64 + q // RING * 16))
                    act.wait_ge(c["counted"].sem, c["counted"](m - 3))
                    act.activation(xo[:, q % RING, :], OUT[q % 4], ACT.Copy).then_inc(c["x_new"].sem, 1)
                if more(STAT) and (q + STAT) % SCH == SCH - 1:
                    root(i, (q + STAT) // SCH)

            root(0, 0)
            if HH < P:
                act.wait_ge(c["u_cleared"].sem, c["u_cleared"](1))
            for q in range(TURN):
                copy(0, q)
            bodies_of(act, step)

    for s in range(RING):
        for name in ("xc_in", "gc_in", "x_out"):
            c[f"{name}{s}"].advance(16 * NCH // RING)
    if HH < P:
        c["u_cleared"].advance(1)
    batches = NCH // SCH
    for name in ("ln_var", "ln_root", "ln_scale"):
        c[name].advance(batches)
    c["ln_small"].advance(2 * batches)
    for name in ("ln_stat", "scaled", "wt_done", "wt_copied", "out_mm_done", "x_new",
                 *(("centered", "gated") if gate_first else ("out_gated",))) + (("counted",) if counted else ()):
        c[name].advance(NCH)


def constants():
    basis = np.zeros((C, C), np.float32)
    for m in range(C - 1):
        basis[:m + 1, m] = 1 / np.sqrt((m + 1) * (m + 2))
        basis[m + 1, m] = -(m + 1) / np.sqrt((m + 1) * (m + 2))
    live = (np.arange(P) % C != C - 1)
    group = np.arange(P) % C // 2
    var_w = np.zeros((P, 4 * BATCH - 2), np.float32)
    spread = np.zeros((P, BATCH, P), np.float32)
    for g in range(2):
        half = slice(g * C, g * C + C)
        var_w[half, 2 * BATCH - 2 + g] = live[half] / C
        for q in range(BATCH):
            for part in range(3):
                spread[R_PART * part + 2 * q + g, q, half] = live[half]
    spread[R_ONE] = ~live
    unit = np.zeros((P, 3), np.float32)
    unit[:, 0] = ~live
    unit[:, 1] = np.where(live, EPS, 1)
    unit[:, 2] = EPS
    h_center = {}
    for n, H in ((2, 16), (3, C)):
        h_center[f"h_center{n}"] = np.zeros((P, P), np.float32)
        h_center[f"h_center{n}"][:2 * H, :2 * H] = np.kron(np.eye(2), np.eye(H) - 1 / H)
    last_row = np.zeros((2, P), np.float32)
    last_row[0, C - 1] = last_row[1, P - 1] = 1
    return {
        **h_center, "basis": np.kron(np.eye(2), basis), "var_w": var_w, "spread": spread.reshape(P, BATCH * P), "ident": np.eye(P),
        "pool_w": (group[:, None] == group[None, :]) / 4, "last_row": last_row, "unit": unit, "one": np.ones((1, P)),
    }


def twice(w):
    out = np.zeros((2, w.shape[0], 2, w.shape[1]), np.float32)
    for g in range(2):
        out[g, :, g, :] = w
    return out.reshape(2 * w.shape[0], 2 * w.shape[1])


def layouts(inputs):
    v = {name: np.asarray(value) for name, value in inputs.items()}
    x = v["x"].reshape(2, HALF * S, C).transpose(0, 2, 1).reshape(P, HALF * S)
    arrays = {"x": x}
    arrays.update(constants())

    columns = {"LN_G": V_LN_G, "LN_B": V_LN_B, "ON_G": V_ON_G, "ON_B": V_ON_B, "GATE_B": V_GATE_B, "OUT_B": V_OUT_B}

    def vectors(**by_column):
        out = np.zeros((P, NVEC), np.float32)
        for name, w in by_column.items():
            w = np.concatenate([w, w])
            out[:len(w), columns[name]] = w
        return out

    def add(n, gates, projections, out_gate, w_out, vec, gate_bias=None, proj_bias=None, out_gate_bias=None):
        w = [twice(np.concatenate(part, axis=1)) for part in (gates, projections)] + [twice(out_gate)]
        arrays[f"w_proj{n}"] = np.concatenate(w, axis=1)
        rows = np.zeros((2, 640), np.float32)
        if gate_bias is not None:
            for at, bias in ((0, np.concatenate(gate_bias)), (256, np.concatenate(proj_bias)), (512, out_gate_bias)):
                for g in range(2):
                    rows[g, at + g * len(bias):at + (g + 1) * len(bias)] = bias
        arrays[f"b_rows{n}"] = rows
        arrays[f"w_out{n}"] = twice(w_out)
        arrays[f"vec{n}"] = vec

    l0 = {q: v["L0_conv_" + q] for q in ("norm_g", "norm_b", "Wl", "Wr", "Wlg", "Wrg", "Wog", "out_norm_g", "out_norm_b", "Wout")}
    add(0, (l0["Wlg"].T, l0["Wrg"].T), (l0["Wl"].T, l0["Wr"].T), l0["Wog"].T, l0["Wout"].T,
        vectors(LN_G=l0["norm_g"], LN_B=l0["norm_b"], ON_G=l0["out_norm_g"], ON_B=l0["out_norm_b"]))
    arrays["mask0"] = v["L0_conv_mask"].reshape(S, S)
    l1 = {q: v["L1_conv_" + q] for q in ("norm_w", "norm_b", "w_left", "w_right", "w_lgate", "w_rgate", "w_ogate", "onorm_w", "onorm_b", "w_out")}
    add(1, (l1["w_lgate"].T, l1["w_rgate"].T), (l1["w_left"].T, l1["w_right"].T), l1["w_ogate"].T, l1["w_out"].T,
        vectors(LN_G=l1["norm_w"], LN_B=l1["norm_b"], ON_G=l1["onorm_w"], ON_B=l1["onorm_b"]))
    arrays["mask1"] = v["L1_conv_mask"].reshape(S, S)
    l2 = {q: v["L2_conv_" + q] for q in ("Wa1", "ba1", "Wa2", "ba2", "Wb1", "bb1", "Wb2", "bb2", "ln2_g", "ln2_b", "Wg", "bg", "Wz", "bz")}
    w = np.zeros((P, 640), np.float32)
    for half, parts in enumerate((("Wa1", "Wb1"), ("Wa2", "Wb2"))):
        w[:, half * C:half * C + C] = twice(np.concatenate([l2[q] for q in parts], axis=1))
    w[:, 512:640] = twice(l2["Wg"])
    arrays["w_proj2"] = w
    rows = np.zeros((2, 640), np.float32)
    tile = np.concatenate([np.concatenate([l2[q] for q in parts] * 2) for parts in (("ba1", "bb1"), ("ba2", "bb2"))])
    rows[0, 0:512] = np.concatenate([tile] * 4)
    arrays["b_rows2"] = rows
    w_out = np.zeros((P, P), np.float32)
    w_out[:32] = twice(l2["Wz"])
    arrays["w_out2"] = w_out
    arrays["vec2"] = vectors(ON_G=l2["ln2_g"], ON_B=l2["ln2_b"], GATE_B=l2["bg"], OUT_B=l2["bz"])
    l3 = {q: v["L3_conv_" + q] for q in ("ln_in_w", "ln_in_b", "Wga", "bga", "Wla", "bla", "Wgb", "bgb", "Wlb", "blb", "ln_o_w", "ln_o_b", "Wgo", "bgo", "Wlo", "blo")}
    add(3, (l3["Wga"], l3["Wgb"]), (l3["Wla"], l3["Wlb"]), l3["Wgo"], l3["Wlo"],
        vectors(LN_G=l3["ln_in_w"], LN_B=l3["ln_in_b"], ON_G=l3["ln_o_w"], ON_B=l3["ln_o_b"], OUT_B=l3["blo"]),
        (l3["bga"], l3["bgb"]), (l3["bla"], l3["blb"]), l3["bgo"])
    return {name: np.ascontiguousarray(value, dtype=np.float32) for name, value in arrays.items()}


def scratch(nc):
    out = {}
    for name in ("x_dram0", "x_dram1", "gate"):
        out[name] = nc.dram_tensor(name, [P, HALF * S], F32, kind="Internal").ap()
    for n, (groups, per, dt) in enumerate(((8, 8, F32), (4, 16, BF16), (2, 8, F32), (8, 8, F32))):
        out[f"left_right{n}"] = nc.dram_tensor(f"left_right{n}", [2, groups, P, 2, S // SEG, SEG, per], dt, kind="Internal").ap()
    return out


def kernel(**inputs):
    import concourse.bacc as bacc
    from concourse.bass_utils import run_bass_kernel_spmd

    nc = bacc.Bacc("TRN2", target_bir_lowering=False, num_devices=1)
    arrays = layouts(inputs)
    a = {name: nc.dram_tensor(f"in_{name}", list(v.shape), F32, kind="ExternalInput").ap() for name, v in arrays.items()}
    a.update(scratch(nc))
    out = nc.dram_tensor("out", [P, HALF * S], F32, kind="ExternalOutput").ap()
    build(nc, a, out)
    r = run_bass_kernel_spmd(nc, [{f"in_{name}": v for name, v in arrays.items()}], core_ids=[0])
    y = np.asarray(r.results[0]["out"])
    return y.reshape(2, C, HALF * S).transpose(0, 2, 1).reshape(1, S, S, C)
```
